# Optimizing a Trainium2 kernel written in Bass

```python
import numpy as np
import jax
import jax.numpy as jnp

def _softmax(x, axis=-1):
    return jax.nn.softmax(x, axis=axis)

def _gelu(x):
    return jax.nn.gelu(x, approximate=True)

def _silu(x):
    return jax.nn.silu(x)

def _sigmoid(x):
    return jax.nn.sigmoid(x)

def _layernorm(x, axis=-1, eps=1e-05):
    m = jnp.mean(x, axis=axis, keepdims=True)
    v = jnp.var(x, axis=axis, keepdims=True)
    return (x - m) / jnp.sqrt(v + eps)

def _scatter_add(tgt, idx, src, axis=0):
    return tgt.at[idx].add(src)

def _segment_sum(src, seg, n):
    return jax.ops.segment_sum(src, seg, n)
kernel_name = 'mk_decoder_preln_d2_seqx_r4_464df0'

def setup_inputs(seed: int=0):
    np.random.seed(seed)
    _w = jnp.asarray

    def _rec_inputs():
        import jax
        import jax.numpy as jnp
        _rk = jax.random.key(seed)
        x = -0.0002928 + 1 * jax.random.normal(jax.random.fold_in(_rk, 1), (2, 512, 256), jnp.float32)
        _lenS = 512 - jax.random.randint(jax.random.fold_in(_rk, 7), (2,), 0, max(1, 512 // 4) + 1, jnp.int32)
        _lenS2 = 1024 - jax.random.randint(jax.random.fold_in(_rk, 8), (2,), 0, max(1, 1024 // 4) + 1, jnp.int32)
        _ctx_1024P = jax.random.normal(jax.random.fold_in(_rk, 11), (2, 16, 256), jnp.float32)
        _ctx_1024c = jax.random.dirichlet(jax.random.fold_in(_rk, 511), 0.3 * jnp.ones((16,), jnp.float32), (2, 1024))
        _ctx_1024t = jnp.einsum('bsk,bkd->bsd', _ctx_1024c, _ctx_1024P)
        _ctx_1024t = _ctx_1024t * jax.lax.rsqrt(jnp.mean(jnp.square(_ctx_1024t)) + 1e-12) * 0.953939
        ctx_1024 = -1.39393e-06 + 0.999914 * (_ctx_1024t + 0.3 * jax.random.normal(jax.random.fold_in(_rk, 611), (2, 1024, 256), jnp.float32))
        return (x, ctx_1024)
    x, ctx_1024 = _rec_inputs()

    def _L0_attn_setup():
        import jax, jax.numpy as jnp
        import numpy as np
        DIM = 256
        HEADS = 16
        HIDDEN = 512
        EPS = 1e-06

        def _rmsnorm(x, scale):
            norm = jnp.linalg.norm(x, axis=-1, keepdims=True)
            return x * (scale * (x.shape[-1] ** 0.5 + EPS) / norm)
        key = jax.random.key(seed)
        ks = jax.random.split(key, 8)
        B, N, C = (4, 1024, DIM)
        s = 0.02
        return {'x': jax.random.normal(ks[0], (B, N, C), dtype=jnp.float32), 'scale1': jnp.ones((C,), jnp.float32), 'scale2': jnp.ones((C,), jnp.float32), 'gamma': jnp.ones((C,), jnp.float32), 'qkv_w': jax.random.normal(ks[1], (3 * C, C), jnp.float32) * s, 'proj_w': jax.random.normal(ks[2], (C, C), jnp.float32) * s, 'proj_b': jnp.zeros((C,), jnp.float32), 'conv1_w': jax.random.normal(ks[3], (HIDDEN, C), jnp.float32) * s, 'conv1_b': jnp.zeros((HIDDEN,), jnp.float32), 'conv2_w': jax.random.normal(ks[4], (C, HIDDEN), jnp.float32) * s, 'conv2_b': jnp.zeros((C,), jnp.float32)}
    _L0_attn_all = _L0_attn_setup()
    _L0_attn_in = {k: v for k, v in _L0_attn_all.items() if k in ('scale1', 'scale2', 'gamma', 'qkv_w', 'proj_w', 'proj_b', 'conv1_w', 'conv1_b', 'conv2_w', 'conv2_b')}
    del _L0_attn_all

    def _L0_xattn_setup():
        import jax, jax.numpy as jnp
        import numpy as np
        B, S, D, H, K_TOP = (2, 512, 256, 16, 64)
        DH = D // H
        SCALE = DH ** (-0.5)

        def _split_heads(x):
            b, s, _ = x.shape
            return x.reshape(b, s, H, DH).transpose(0, 2, 1, 3)

        def _straight_through_topk_fwd_math(scores):
            soft = jax.nn.softmax(scores, axis=-1)
            vals, idx = jax.lax.top_k(soft, K_TOP)
            b_i = jnp.arange(scores.shape[0])[:, None, None, None]
            h_i = jnp.arange(scores.shape[1])[None, :, None, None]
            q_i = jnp.arange(scores.shape[2])[None, None, :, None]
            hard = jnp.zeros_like(soft).at[b_i, h_i, q_i, idx].set(vals)
            return hard / (hard.sum(axis=-1, keepdims=True) + 1e-09)
        key = jax.random.key(seed)
        kq, kk, kv, kwq, kwk = jax.random.split(key, 5)
        return {'query': jax.random.normal(kq, (B, S, D), dtype=jnp.float32), 'key': jax.random.normal(kk, (B, S, D), dtype=jnp.float32), 'value': jax.random.normal(kv, (B, S, D), dtype=jnp.float32), 'Wq': jax.random.normal(kwq, (D, D), dtype=jnp.float32) * 0.02, 'Wk': jax.random.normal(kwk, (D, D), dtype=jnp.float32) * 0.02}
    _L0_xattn_all = _L0_xattn_setup()
    _L0_xattn_in = {k: v for k, v in _L0_xattn_all.items() if k in ('Wq', 'Wk')}
    del _L0_xattn_all

    def _L0_ffn_setup():
        import jax, jax.numpy as jnp
        import numpy as np
        HIDDEN = 256
        INNER = 1024

        def _weight_quant(w):
            scale = 1.0 / jnp.clip(jnp.mean(jnp.abs(w)), 1e-05)
            wq = jnp.clip(jnp.round(w * scale), -1.0, 1.0) / scale
            return w + jax.lax.stop_gradient(wq - w)

        def _act_quant(x):
            scale = 127.0 / jnp.clip(jnp.max(jnp.abs(x), axis=-1, keepdims=True), 1e-05)
            xq = jnp.clip(jnp.round(x * scale), -128.0, 127.0) / scale
            return x + jax.lax.stop_gradient(xq - x)

        def _bitlinear(x, w):
            return jnp.einsum('bsi,oi->bso', _act_quant(x), _weight_quant(w))
        key = jax.random.key(seed)
        k0, k1, k2, k3 = jax.random.split(key, 4)
        x = jax.random.normal(k0, (4, 512, HIDDEN), dtype=jnp.float32)
        w_gate = jax.random.normal(k1, (INNER, HIDDEN), dtype=jnp.float32) / np.sqrt(HIDDEN)
        w_up = jax.random.normal(k2, (INNER, HIDDEN), dtype=jnp.float32) / np.sqrt(HIDDEN)
        w_down = jax.random.normal(k3, (HIDDEN, INNER), dtype=jnp.float32) / np.sqrt(INNER)
        return {'x': x, 'w_gate': w_gate, 'w_up': w_up, 'w_down': w_down}
    _L0_ffn_all = _L0_ffn_setup()
    _L0_ffn_in = {k: v for k, v in _L0_ffn_all.items() if k in ('w_gate', 'w_up', 'w_down')}
    del _L0_ffn_all

    def _L1_attn_setup():
        import jax, jax.numpy as jnp
        import numpy as np
        import math
        D_MODEL = 256
        N_HEADS = 16
        HEAD_DIM = D_MODEL // N_HEADS

        def get_slopes(n_heads: int) -> jnp.ndarray:

            def pow2_slopes(n):
                start = 2.0 ** (-8.0 / n)
                return np.array([start * start ** i for i in range(n)], dtype=np.float32)
            if math.log2(n_heads).is_integer():
                return jnp.asarray(pow2_slopes(n_heads))
            closest = 2 ** math.floor(math.log2(n_heads))
            base = pow2_slopes(closest)
            extra = pow2_slopes(2 * closest)[::2][:n_heads - closest]
            return jnp.asarray(np.concatenate([base, extra]))
        key = jax.random.key(seed)
        ks = jax.random.split(key, 9)
        s = 1.0 / math.sqrt(D_MODEL)
        x = jax.random.normal(ks[0], (2, 512, D_MODEL), dtype=jnp.float32)
        q_w = jax.random.uniform(ks[1], (D_MODEL, D_MODEL), jnp.float32, -s, s)
        q_b = jax.random.uniform(ks[2], (D_MODEL,), jnp.float32, -s, s)
        k_w = jax.random.uniform(ks[3], (D_MODEL, D_MODEL), jnp.float32, -s, s)
        k_b = jax.random.uniform(ks[4], (D_MODEL,), jnp.float32, -s, s)
        v_w = jax.random.uniform(ks[5], (D_MODEL, D_MODEL), jnp.float32, -s, s)
        v_b = jax.random.uniform(ks[6], (D_MODEL,), jnp.float32, -s, s)
        o_w = jax.random.uniform(ks[7], (D_MODEL, D_MODEL), jnp.float32, -s, s)
        o_b = jax.random.uniform(ks[8], (D_MODEL,), jnp.float32, -s, s)
        return {'x': x, 'q_w': q_w, 'q_b': q_b, 'k_w': k_w, 'k_b': k_b, 'v_w': v_w, 'v_b': v_b, 'o_w': o_w, 'o_b': o_b}
    _L1_attn_all = _L1_attn_setup()
    _L1_attn_in = {k: v for k, v in _L1_attn_all.items() if k in ('q_w', 'q_b', 'k_w', 'k_b', 'v_w', 'v_b', 'o_w', 'o_b')}
    del _L1_attn_all

    def _L1_xattn_setup():
        import jax, jax.numpy as jnp
        import numpy as np
        HEAD = 16
        EMB = 256
        B, S = (8, 1024)

        def _proj_heads(x, W, b, H, d):
            Bx, Sx, _ = x.shape
            y = x @ W.T + b
            return y.reshape(Bx, Sx, H, d).transpose(0, 2, 1, 3)
        key = jax.random.key(seed)
        ks = jax.random.split(key, 11)
        scale = 1.0 / np.sqrt(EMB).astype(np.float32)
        inp = {'query': jax.random.normal(ks[0], (B, S, EMB), jnp.float32), 'key': jax.random.normal(ks[1], (B, S, EMB), jnp.float32), 'value': jax.random.normal(ks[2], (B, S, EMB), jnp.float32), 'Wq': jax.random.normal(ks[3], (EMB, EMB), jnp.float32) * scale, 'bq': jnp.zeros((EMB,), jnp.float32), 'Wk': jax.random.normal(ks[4], (EMB, EMB), jnp.float32) * scale, 'bk': jnp.zeros((EMB,), jnp.float32), 'Wv': jax.random.normal(ks[5], (EMB, EMB), jnp.float32) * scale, 'bv': jnp.zeros((EMB,), jnp.float32), 'Wo': jax.random.normal(ks[6], (EMB, EMB), jnp.float32) * scale, 'bo': jnp.zeros((EMB,), jnp.float32)}
        return inp
    _L1_xattn_all = _L1_xattn_setup()
    _L1_xattn_in = {k: v for k, v in _L1_xattn_all.items() if k in ('Wq', 'bq', 'Wk', 'bk', 'Wv', 'bv', 'Wo', 'bo')}
    del _L1_xattn_all

    def _L1_ffn_setup():
        import jax, jax.numpy as jnp
        import numpy as np
        B, T, D, R, E = (32, 256, 256, 64, 8)
        key = jax.random.key(seed)
        ks = jax.random.split(key, 12)
        inp = {}
        inp['x'] = jax.random.normal(ks[0], (B, T, D), dtype=jnp.float32)
        inp['base_W'] = jax.random.normal(ks[1], (D, D), dtype=jnp.float32) * (1.0 / np.sqrt(D))
        inp['base_b'] = jax.random.normal(ks[2], (D,), dtype=jnp.float32) * 0.01
        inp['disc_mu'] = jax.random.normal(ks[3], (E, D), dtype=jnp.float32) * 0.5
        inp['disc_sigma'] = jax.random.uniform(ks[4], (E, D), dtype=jnp.float32, minval=0.5, maxval=1.5)
        inp['down_W'] = jax.random.normal(ks[5], (E, D, R), dtype=jnp.float32) * (1.0 / np.sqrt(D))
        inp['down_b'] = jax.random.normal(ks[6], (E, R), dtype=jnp.float32) * 0.01
        inp['up_W'] = jax.random.normal(ks[7], (E, R, D), dtype=jnp.float32) * (1.0 / np.sqrt(R))
        inp['up_b'] = jax.random.normal(ks[8], (E, D), dtype=jnp.float32) * 0.01
        inp['conv_W'] = jax.random.normal(ks[9], (E, D, D), dtype=jnp.float32) * 0.02
        inp['conv_b'] = jax.random.normal(ks[10], (E, D), dtype=jnp.float32) * 0.01
        return inp
    _L1_ffn_all = _L1_ffn_setup()
    _L1_ffn_in = {k: v for k, v in _L1_ffn_all.items() if k in ('base_W', 'base_b', 'disc_mu', 'disc_sigma', 'down_W', 'down_b', 'up_W', 'up_b', 'conv_W', 'conv_b')}
    del _L1_ffn_all
    return {'x': x, 'ctx_1024': ctx_1024, 'L0_attn_scale1': _L0_attn_in['scale1'], 'L0_attn_scale2': _L0_attn_in['scale2'], 'L0_attn_gamma': _L0_attn_in['gamma'], 'L0_attn_qkv_w': _L0_attn_in['qkv_w'], 'L0_attn_proj_w': _L0_attn_in['proj_w'], 'L0_attn_proj_b': _L0_attn_in['proj_b'], 'L0_attn_conv1_w': _L0_attn_in['conv1_w'], 'L0_attn_conv1_b': _L0_attn_in['conv1_b'], 'L0_attn_conv2_w': _L0_attn_in['conv2_w'], 'L0_attn_conv2_b': _L0_attn_in['conv2_b'], 'L0_xattn_Wq': _L0_xattn_in['Wq'], 'L0_xattn_Wk': _L0_xattn_in['Wk'], 'L0_ffn_w_gate': _L0_ffn_in['w_gate'], 'L0_ffn_w_up': _L0_ffn_in['w_up'], 'L0_ffn_w_down': _L0_ffn_in['w_down'], 'L1_attn_q_w': _L1_attn_in['q_w'], 'L1_attn_q_b': _L1_attn_in['q_b'], 'L1_attn_k_w': _L1_attn_in['k_w'], 'L1_attn_k_b': _L1_attn_in['k_b'], 'L1_attn_v_w': _L1_attn_in['v_w'], 'L1_attn_v_b': _L1_attn_in['v_b'], 'L1_attn_o_w': _L1_attn_in['o_w'], 'L1_attn_o_b': _L1_attn_in['o_b'], 'L1_xattn_Wq': _L1_xattn_in['Wq'], 'L1_xattn_bq': _L1_xattn_in['bq'], 'L1_xattn_Wk': _L1_xattn_in['Wk'], 'L1_xattn_bk': _L1_xattn_in['bk'], 'L1_xattn_Wv': _L1_xattn_in['Wv'], 'L1_xattn_bv': _L1_xattn_in['bv'], 'L1_xattn_Wo': _L1_xattn_in['Wo'], 'L1_xattn_bo': _L1_xattn_in['bo'], 'L1_ffn_base_W': _L1_ffn_in['base_W'], 'L1_ffn_base_b': _L1_ffn_in['base_b'], 'L1_ffn_disc_mu': _L1_ffn_in['disc_mu'], 'L1_ffn_disc_sigma': _L1_ffn_in['disc_sigma'], 'L1_ffn_down_W': _L1_ffn_in['down_W'], 'L1_ffn_down_b': _L1_ffn_in['down_b'], 'L1_ffn_up_W': _L1_ffn_in['up_W'], 'L1_ffn_up_b': _L1_ffn_in['up_b'], 'L1_ffn_conv_W': _L1_ffn_in['conv_W'], 'L1_ffn_conv_b': _L1_ffn_in['conv_b']}

def reference(x, ctx_1024, L0_attn_scale1, L0_attn_scale2, L0_attn_gamma, L0_attn_qkv_w, L0_attn_proj_w, L0_attn_proj_b, L0_attn_conv1_w, L0_attn_conv1_b, L0_attn_conv2_w, L0_attn_conv2_b, L0_xattn_Wq, L0_xattn_Wk, L0_ffn_w_gate, L0_ffn_w_up, L0_ffn_w_down, L1_attn_q_w, L1_attn_q_b, L1_attn_k_w, L1_attn_k_b, L1_attn_v_w, L1_attn_v_b, L1_attn_o_w, L1_attn_o_b, L1_xattn_Wq, L1_xattn_bq, L1_xattn_Wk, L1_xattn_bk, L1_xattn_Wv, L1_xattn_bv, L1_xattn_Wo, L1_xattn_bo, L1_ffn_base_W, L1_ffn_base_b, L1_ffn_disc_mu, L1_ffn_disc_sigma, L1_ffn_down_W, L1_ffn_down_b, L1_ffn_up_W, L1_ffn_up_b, L1_ffn_conv_W, L1_ffn_conv_b):
    import jax
    import jax.numpy as jnp

    def _L0_attn_ref(x, scale1, scale2, gamma, qkv_w, proj_w, proj_b, conv1_w, conv1_b, conv2_w, conv2_b):
        import jax, jax.numpy as jnp
        import numpy as np
        DIM = 256
        HEADS = 16
        HIDDEN = 512
        EPS = 1e-06

        def _rmsnorm(x, scale):
            norm = jnp.linalg.norm(x, axis=-1, keepdims=True)
            return x * (scale * (x.shape[-1] ** 0.5 + EPS) / norm)
        B, N, C = x.shape
        h, d = (HEADS, C // HEADS)
        xn = _rmsnorm(x, scale1)
        qkv = jnp.einsum('bnc,fc->bnf', xn, qkv_w)
        qkv = qkv.reshape(B, N, 3, h, d).transpose(2, 0, 3, 1, 4)
        q, k, v = (qkv[0], qkv[1], qkv[2])
        phi = lambda t: jnp.exp(-0.5 * t * t)
        q, k = (phi(q), phi(k))
        kv = jnp.einsum('bhnd,bhne->bhde', k, v)
        z = 1.0 / (jnp.einsum('bhnd,bhd->bhn', q, k.sum(2)) + 1e-06)
        out = jnp.einsum('bhnd,bhde,bhn->bhne', q, kv, z)
        out = out.transpose(0, 2, 1, 3).reshape(B, N, C)
        attn = jnp.einsum('bnc,oc->bno', out, proj_w) + proj_b
        x = x + gamma * attn
        xn2 = _rmsnorm(x, scale2)
        hdd = jax.nn.gelu(jnp.einsum('bnc,hc->bnh', xn2, conv1_w) + conv1_b, approximate=False)
        mlp = jnp.einsum('bnh,ch->bnc', hdd, conv2_w) + conv2_b
        return x + gamma * mlp

    def _L0_xattn_ref(query, key, value, Wq, Wk):
        import jax, jax.numpy as jnp
        import numpy as np
        B, S, D, H, K_TOP = (2, 512, 256, 16, 64)
        DH = D // H
        SCALE = DH ** (-0.5)

        def _split_heads(x):
            b, s, _ = x.shape
            return x.reshape(b, s, H, DH).transpose(0, 2, 1, 3)

        def _straight_through_topk_fwd_math(scores):
            soft = jax.nn.softmax(scores, axis=-1)
            vals, idx = jax.lax.top_k(soft, K_TOP)
            b_i = jnp.arange(scores.shape[0])[:, None, None, None]
            h_i = jnp.arange(scores.shape[1])[None, :, None, None]
            q_i = jnp.arange(scores.shape[2])[None, None, :, None]
            hard = jnp.zeros_like(soft).at[b_i, h_i, q_i, idx].set(vals)
            return hard / (hard.sum(axis=-1, keepdims=True) + 1e-09)
        q = _split_heads(jnp.einsum('bsd,ed->bse', query, Wq))
        k = _split_heads(jnp.einsum('bsd,ed->bse', key, Wk))
        v = _split_heads(value)
        scores = jnp.einsum('bhqa,bhka->bhqk', q, k) * SCALE
        w = _straight_through_topk_fwd_math(scores)
        e = jnp.einsum('bhqv,bhva->bhqa', w, v)
        e = e.transpose(0, 2, 1, 3).reshape(query.shape)
        return e

    def _L0_ffn_ref(x, w_gate, w_up, w_down):
        import jax, jax.numpy as jnp
        import numpy as np
        HIDDEN = 256
        INNER = 1024

        def _weight_quant(w):
            scale = 1.0 / jnp.clip(jnp.mean(jnp.abs(w)), 1e-05)
            wq = jnp.clip(jnp.round(w * scale), -1.0, 1.0) / scale
            return w + jax.lax.stop_gradient(wq - w)

        def _act_quant(x):
            scale = 127.0 / jnp.clip(jnp.max(jnp.abs(x), axis=-1, keepdims=True), 1e-05)
            xq = jnp.clip(jnp.round(x * scale), -128.0, 127.0) / scale
            return x + jax.lax.stop_gradient(xq - x)

        def _bitlinear(x, w):
            return jnp.einsum('bsi,oi->bso', _act_quant(x), _weight_quant(w))
        gate = jax.nn.silu(_bitlinear(x, w_gate))
        up = _bitlinear(x, w_up)
        return _bitlinear(gate * up, w_down)

    def _L1_attn_ref(x, q_w, q_b, k_w, k_b, v_w, v_b, o_w, o_b):
        import jax, jax.numpy as jnp
        import numpy as np
        import math
        D_MODEL = 256
        N_HEADS = 16
        HEAD_DIM = D_MODEL // N_HEADS

        def get_slopes(n_heads: int) -> jnp.ndarray:

            def pow2_slopes(n):
                start = 2.0 ** (-8.0 / n)
                return np.array([start * start ** i for i in range(n)], dtype=np.float32)
            if math.log2(n_heads).is_integer():
                return jnp.asarray(pow2_slopes(n_heads))
            closest = 2 ** math.floor(math.log2(n_heads))
            base = pow2_slopes(closest)
            extra = pow2_slopes(2 * closest)[::2][:n_heads - closest]
            return jnp.asarray(np.concatenate([base, extra]))
        B, S, D = x.shape
        H, hd = (N_HEADS, HEAD_DIM)
        Q = (x @ q_w.T + q_b).reshape(B, S, H, hd).transpose(0, 2, 1, 3)
        K = (x @ k_w.T + k_b).reshape(B, S, H, hd).transpose(0, 2, 1, 3)
        V = (x @ v_w.T + v_b).reshape(B, S, H, hd).transpose(0, 2, 1, 3)
        scores = jnp.einsum('bhqd,bhkd->bhqk', Q, K) / math.sqrt(hd)
        pos = jnp.arange(S)
        rel = (pos[None, :] - pos[:, None]).astype(scores.dtype)
        slopes = get_slopes(H)
        scores = scores + slopes[None, :, None, None] * rel[None, None, :, :]
        causal = pos[None, :] <= pos[:, None]
        scores = jnp.where(causal[None, None], scores, -jnp.inf)
        attn = jax.nn.softmax(scores, axis=-1)
        out = jnp.einsum('bhqk,bhkd->bhqd', attn, V)
        out = out.transpose(0, 2, 1, 3).reshape(B, S, D)
        return out @ o_w.T + o_b

    def _L1_xattn_ref(query, key, value, Wq, bq, Wk, bk, Wv, bv, Wo, bo):
        import jax, jax.numpy as jnp
        import numpy as np
        HEAD = 16
        EMB = 256
        B, S = (8, 1024)

        def _proj_heads(x, W, b, H, d):
            Bx, Sx, _ = x.shape
            y = x @ W.T + b
            return y.reshape(Bx, Sx, H, d).transpose(0, 2, 1, 3)
        Bx, Sx, E = query.shape
        H = HEAD
        d = E // H
        q = jax.nn.elu(_proj_heads(query, Wq, bq, H, d))
        k = jax.nn.elu(_proj_heads(key, Wk, bk, H, d))
        v = _proj_heads(value, Wv, bv, H, d)
        sqrt_S = jnp.asarray(np.sqrt(Sx), jnp.float32)
        k = k / (jnp.linalg.norm(k, axis=2, keepdims=True) * sqrt_S)
        sqrt_d = jnp.asarray(np.sqrt(d), jnp.float32)
        q = q / (jnp.linalg.norm(q, axis=3, keepdims=True) * sqrt_d)
        scores = jnp.einsum('bhsd,bhse->bhde', k, v)
        x = jnp.einsum('bhsd,bhde->bhse', q, scores)
        x = x.transpose(0, 2, 1, 3).reshape(Bx, Sx, E)
        return x @ Wo.T + bo

    def _L1_ffn_ref(x, base_W, base_b, disc_mu, disc_sigma, down_W, down_b, up_W, up_b, conv_W, conv_b):
        import jax, jax.numpy as jnp
        import numpy as np
        B, T, D, R, E = (32, 256, 256, 64, 8)
        base = jnp.einsum('btd,od->bto', x, base_W) + base_b
        m1 = x.mean(axis=1)
        m2 = (x * x).mean(axis=1)
        inv_var = 1.0 / (disc_sigma * disc_sigma)
        losses = (jnp.einsum('bd,ed->eb', m2, inv_var) - 2.0 * jnp.einsum('bd,ed->eb', m1, disc_mu * inv_var) + jnp.sum(disc_mu * disc_mu * inv_var, axis=1)[:, None]) / D
        idx = jnp.argmin(losses, axis=0)
        Wd, bd = (down_W[idx], down_b[idx])
        Wu, bu = (up_W[idx], up_b[idx])
        Wc, bc = (conv_W[idx], conv_b[idx])
        h = jax.nn.relu(jnp.einsum('btd,bdr->btr', x, Wd) + bd[:, None, :])
        a = jnp.einsum('btr,brd->btd', h, Wu) + bu[:, None, :]
        y = jnp.einsum('btd,bod->bto', a, Wc) + bc[:, None, :]
        return base + y
    x = x + _L0_attn_ref(_layernorm(x, axis=-1), L0_attn_scale1, L0_attn_scale2, L0_attn_gamma, L0_attn_qkv_w, L0_attn_proj_w, L0_attn_proj_b, L0_attn_conv1_w, L0_attn_conv1_b, L0_attn_conv2_w, L0_attn_conv2_b)
    x = x + _L0_xattn_ref(_layernorm(x, axis=-1), ctx_1024, ctx_1024, L0_xattn_Wq, L0_xattn_Wk)
    x = x + _L0_ffn_ref(_layernorm(x, axis=-1), L0_ffn_w_gate, L0_ffn_w_up, L0_ffn_w_down)
    x = x + _L1_attn_ref(_layernorm(x, axis=-1), L1_attn_q_w, L1_attn_q_b, L1_attn_k_w, L1_attn_k_b, L1_attn_v_w, L1_attn_v_b, L1_attn_o_w, L1_attn_o_b)
    x = x + _L1_xattn_ref(_layernorm(x, axis=-1), ctx_1024, ctx_1024, L1_xattn_Wq, L1_xattn_bq, L1_xattn_Wk, L1_xattn_bk, L1_xattn_Wv, L1_xattn_bv, L1_xattn_Wo, L1_xattn_bo)
    x = x + _L1_ffn_ref(_layernorm(x, axis=-1), L1_ffn_base_W, L1_ffn_base_b, L1_ffn_disc_mu, L1_ffn_disc_sigma, L1_ffn_down_W, L1_ffn_down_b, L1_ffn_up_W, L1_ffn_up_b, L1_ffn_conv_W, L1_ffn_conv_b)
    return x

_drawn_inputs = setup_inputs


def setup_inputs(seed=0):
    import zlib

    import numpy as np

    out = dict(_drawn_inputs(seed))
    spreads = {'L0_attn_scale1': (1.0, 0.6),
     'L0_attn_scale2': (1.0, 0.6),
     'L0_attn_gamma': (1.0, 0.6),
     'L0_attn_proj_b': (0.0, 0.1),
     'L0_attn_conv1_b': (0.0, 0.565),
     'L0_attn_conv2_b': (0.0, 0.1),
     'L1_xattn_bq': (0.0, 0.8),
     'L1_xattn_bk': (0.0, 0.8),
     'L1_xattn_bv': (0.0, 0.8),
     'L1_xattn_bo': (0.0, 0.1)}
    factors = {'L0_attn_qkv_w': 8.0,
     'L0_attn_proj_w': 8.0,
     'L1_attn_q_w': 4.724,
     'L1_attn_q_b': 8.0,
     'L1_attn_k_w': 4.431,
     'L1_attn_k_b': 64.0,
     'L1_attn_v_b': 6.216,
     'L1_attn_o_b': 3.599,
     'L1_ffn_base_b': 8.0,
     'L1_ffn_down_b': 64.0,
     'L1_ffn_up_b': 49.19,
     'L1_ffn_conv_b': 8.0}
    for name, (base, spread) in spreads.items():
        noise = np.random.default_rng([zlib.crc32(name.encode()), seed]).standard_normal(out[name].shape)
        drawn = base * np.exp(spread * noise) if base else spread * noise
        out[name] = jnp.asarray(drawn.astype(out[name].dtype))
    for name, factor in factors.items():
        out[name] = (out[name] * factor).astype(out[name].dtype)
    return out
```

```python
from contextlib import ExitStack

import numpy as np

import concourse.bass as bass
from concourse import mybir

P = 128
B, S, D = 2, 512, 256
SC = 1024
H, DH = 16, 16
T = B * S // P
TB = S // P
CT = B * SC // P
CTB = SC // P
C = D // P
HC = P // DH
HID = 512
MC = HID // P
INNER = 1024
KC = INNER // P
E, R = 8, 64
K_TOP = 64
NTOP = K_TOP // 8
KV = P + HC
AUG = DH + 2

F32 = mybir.dt.float32
BF16 = mybir.dt.bfloat16
U32 = mybir.dt.uint32
ALU = mybir.AluOpType
ACT = mybir.ActivationFunctionType
AX = mybir.AxisListType

LN_EPS = 1e-5
RMS_GAIN = 16.0 + 1e-6
ROUND = 12582912.0
MARK = -3.0e38
MASKED = -1.0e30


def decoder(nc, t):
    with ExitStack() as ctx:
        def sb(name, shape, dt=F32):
            return ctx.enter_context(nc.sbuf_tensor(name, shape, dt))

        sems = {}

        def sem(name):
            if name not in sems:
                sems[name] = ctx.enter_context(nc.semaphore(name))
            return sems[name]

        bank = [ctx.enter_context(nc.psum_tensor(f"bank{i}", [P, 512], F32)) for i in range(2)]
        wide = [ctx.enter_context(nc.psum_tensor(f"wide{i}", [P, 1024], F32)) for i in range(3)]
        def half(i, j):
            return wide[i][:, 512 * j:512 * j + 512]

        ident = sb("ident", [P, P])
        ident_bf = sb("ident_bf", [P, P], BF16)
        ones = sb("ones", [P, P])
        blockmask = sb("blockmask", [P, P])
        headmask = sb("headmask", [P, HC])
        causal = sb("causal", [P, S])
        x = sb("x", [P, T, D])
        y = sb("y", [P, T, D])
        yT = sb("yT", [P, C, T * P])
        xin = sb("xin", [P, T, D])
        ctxT = sb("ctxT", [P, C, B * SC])
        bn = sb("bn", [P, T, 6])
        mv = sb("mv", [P, T, 2])
        var = sb("var", [P, T])
        sd = sb("sd", [P, T])
        rstd = sb("rstd", [P, T])
        sq = sb("sq", [P, 2, 512])
        names = {"qkvT": 3 * D, "projT": D, "conv1T": HID, "xqT": D, "xkT": D,
                 "aqT": D, "akT": D, "avT": D, "aoT": D, "lqT": D, "lkvT": 2 * D, "loT": D, "baseT": D}
        w = {n: sb("w_" + n, [P, C, k]) for n, k in names.items()}
        conv2T = sb("w_conv2T", [P, MC, D])
        wq_gate = sb("wq_gate", [P, C, INNER], BF16)
        wq_up = sb("wq_up", [P, C, INNER], BF16)
        wq_down = sb("wq_down", [P, KC, D], BF16)
        cols = {n: sb("c_" + n, [P, k]) for n, k in
                {"scale1": C, "scale2": C, "conv1_b": MC, "aq_b": C, "ak_b": C, "lq_b": C}.items()}
        rows = {n: sb("r_" + n, [1, k]) for n, k in
                {"proj_b": D, "conv2_b": D, "av_b": D, "ao_b": D, "lkv_b": 2 * D, "lo_b": D,
                 "base_b": D}.items()}
        gamma = sb("gamma", [P, D])
        vB = sb("vB", [P, B * H * CTB * DH])
        w_mean = sb("w_mean", [P, 3])
        w_scale = sb("w_scale", [P, 3])
        w_abs = sb("w_abs", [P, 3])
        gate_out = sb("gate_out", [P, 1])
        bq_dram = nc.dram_tensor("bq_dram", [B * H * DH, S], F32, kind="Internal").ap()
        bk_dram = nc.dram_tensor("bk_dram", [B * H * DH, SC], F32, kind="Internal").ap()
        dq_dram = nc.dram_tensor("dq_dram", [B * H * DH, S], F32, kind="Internal").ap()
        dk_dram = nc.dram_tensor("dk_dram", [B * H * DH, S], F32, kind="Internal").ap()

        WORK = 19552
        work = sb("work", [P, WORK])

        class Area:
            def __init__(self):
                self.at = 0

            def take(self, *shape, dt=F32):
                n = int(np.prod(shape))
                words = n if dt != BF16 else (n + 1) // 2
                ap = work[:, self.at:self.at + words]
                self.at += words
                assert self.at <= WORK, self.at
                if dt != F32:
                    ap = ap.bitcast(dt)
                if len(shape) > 1:
                    lab = "abcd"[:len(shape)]
                    ap = ap.rearrange(f"p ({' '.join(lab)}) -> p {' '.join(lab)}",
                                      **{k: v for k, v in zip(lab, shape)})
                return ap

        a = Area()
        a_qT = a.take(C, T * P)
        a_k = a.take(T, D)
        a_v = a.take(T, C, P + 1)
        a_kv = a.take(B, C, KV)
        a_den = a.take(2, C, HC)
        a_z = a.take(C, HC)
        a_x1 = a.take(T, D)
        a_tmp = a.take(2, D)
        a_hT = a.take(MC, T * P)
        w_raw = [a.take(C * INNER) for _ in range(3)]
        b = Area()
        b_q = b.take(2, S)
        b_k = b.take(2, SC)
        b_s = b.take(2, SC)
        b_z = b.take(2, SC)
        b_e = b.take(2, SC)
        b_p = b.take(2, SC)
        b_pT = b.take(2, SC)
        b_o = b.take(B * H * TB * DH)
        b_proj = b.take(2, 512)
        b_max = b.take(2, NTOP, 8)
        b_neg = b.take(2, 1)
        b_all = b.take(2, 1)
        b_top = b.take(2, 1)
        b_den = b.take(2, 1)
        b_r = b.take(2, 1)
        c = Area()
        c_am = c.take(T)
        c_am1 = c.take(T)
        c_s = c.take(T)
        c_si = c.take(T)
        c_ag = c.take(T)
        c_au = c.take(T)
        c_q = c.take(2, D)
        c_qb = c.take(2, D, dt=BF16)
        c_qT = c.take(C, T * P, dt=BF16)
        c_g = c.take(2, INNER)
        c_h = c.take(2, INNER)
        c_hr = c.take(INNER)
        c_hb = c.take(2, INNER, dt=BF16)
        c_hT = c.take(2, KC, P, dt=BF16)
        c_hm = c.take(T)
        c_hm1 = c.take(T)
        c_hs = c.take(T)
        c_hi = c.take(T)
        c_ad = c.take(T)
        d = Area()
        d_q = d.take(2, S)
        d_k = d.take(2, S)
        d_s = d.take(2, S)
        d_p = d.take(2, S)
        d_pT = d.take(2, S)
        d_v = d.take(B * H * TB * DH)
        d_o = d.take(B * H * TB * DH)
        d_proj = d.take(2, 512)
        d_max = d.take(2, 1)
        d_neg = d.take(2, 1)
        d_sum = d.take(2, 1)
        d_r = d.take(2, 1)
        e = Area()
        e_k = e.take(CT, D)
        e_v = e.take(CT, D)
        e_t = e.take(2, 2 * D)
        e_kk = e.take(2, D)
        e_qT = e.take(C, T * P)
        e_qq = e.take(C, T * P)
        e_kv = e.take(B, C, P)
        e_kn = e.take(B * C)
        e_kr = e.take(B * C)
        e_qn = e.take(2, C, HC)
        e_qr = e.take(2, C, HC)
        f = Area()
        f_mu = f.take(C, E)
        f_sig = f.take(C, E)
        f_s2 = f.take(C, E)
        f_iv = f.take(C, E)
        f_mi = f.take(C, E)
        f_mm = f.take(C, E)
        f_m2i = f.take(C, E)
        f_bn = f.take(C, B, 6)
        f_mv = f.take(C, B, 2)
        f_m1s = f.take(C, B)
        f_m2 = f.take(C, B)
        f_sq = f.take(C, B)
        f_nl = f.take(E)
        f_best = f.take(8)
        f_idx = f.take(8, dt=U32)
        f_down = f.take(B, C, R)
        f_up = f.take(B, D)
        f_conv = f.take(B, C, D)
        f_db = f.take(B)
        f_ub = f.take(B, C)
        f_cb = f.take(B, D)
        f_hT = f.take(T * P)
        f_aT = f.take(C, T * P)

        block = ctx.enter_context(nc.Block())

        LNS = ["A", "B", "C", "D", "E", "F"]

        @block.sync
        def _(sp):
            sp.dma_start(x[:], t["x"]).then_inc(sem("x_loaded"), 16)
            for n, ap in (("ident", ident), ("blockmask", blockmask), ("headmask", headmask),
                          ("causal", causal)):
                sp.dma_start(ap[:], t[n]).then_inc(sem("const_loaded"), 16)
            for n in ("scale1", "scale2", "conv1_b", "aq_b", "ak_b", "lq_b"):
                sp.dma_start(cols[n][:], t[n]).then_inc(sem("const_loaded"), 16)
            for n in ("proj_b", "conv2_b", "av_b", "ao_b", "lkv_b", "lo_b", "base_b"):
                sp.dma_start(rows[n][:], t[n]).then_inc(sem("const_loaded"), 16)
            sp.dma_start(gamma[:], t["gamma"].broadcast_to([P, D])).then_inc(sem("const_loaded"), 16)
            sp.dma_start(w["qkvT"][:], t["qkvT"]).then_inc(sem("w_A"), 16)
            sp.dma_start(w["projT"][:], t["projT"]).then_inc(sem("w_A"), 16)
            sp.dma_start(w["conv1T"][:], t["conv1T"]).then_inc(sem("w_A"), 16)
            sp.dma_start(conv2T[:], t["conv2T"]).then_inc(sem("w_A"), 16)
            for n, name in enumerate(("gateT", "upT", "downT")):
                sp.dma_start(w_raw[n], t[name]).then_inc(sem("w_raw_loaded"), 16)
            sp.dma_start(ctxT[:], t["ctxT"]).then_inc(sem("w_B"), 16)
            sp.dma_start(w["xkT"][:], t["xkT"]).then_inc(sem("w_B"), 16)
            sp.dma_start(w["xqT"][:], t["xqT"]).then_inc(sem("w_B"), 16)
            sp.dma_start(vB[:], t["ctxV"]).then_inc(sem("w_B"), 16)
            for n in ("aqT", "akT", "avT", "aoT", "lqT", "lkvT", "loT", "baseT"):
                sp.dma_start(w[n][:], t[n]).then_inc(sem("w_DEF"), 16)

            for g in range(C * B):
                cc, bb = g // B, g % B
                sp.wait_ge(sem("b_q_proj"), g + 1)
                sp.dma_start(bq_dram[(bb * C + cc) * P:(bb * C + cc + 1) * P, :],
                             b_proj[:, g % 2, :]).then_inc(sem(f"b_q_stored{g % 2}"), 16)
            for g in range(C * B * 2):
                cc, bb, hh = g // (2 * B), g // 2 % B, g % 2
                sp.wait_ge(sem("b_k_proj"), g + 1)
                sp.dma_start(bk_dram[(bb * C + cc) * P:(bb * C + cc + 1) * P, 512 * hh:512 * hh + 512],
                             b_proj[:, g % 2, :]).then_inc(sem(f"b_k_stored{g % 2}"), 16)
            for g in range(2):
                sp.wait_ge(sem(f"b_q_stored{g}"), 16 * C * B // 2)
                sp.wait_ge(sem(f"b_k_stored{g}"), 16 * C * B)
            for u in range(2):
                sp.dma_start(b_q[0:DH, u, :], bq_dram[u * DH:(u + 1) * DH, :]).then_inc(sem(f"b_head{u}_loaded"), 16)
                sp.dma_start(b_k[0:DH, u, :], bk_dram[u * DH:(u + 1) * DH, :]).then_inc(sem(f"b_head{u}_loaded"), 16)
            with sp.Fori(0, B * H // 2 - 1) as i:
                for u in range(2):
                    sp.wait_ge(sem("b_scores"), i * (2 * TB) + (u + 1) * TB)
                    at = (i * 2 + (2 + u)) * DH
                    sp.dma_start(b_q[0:DH, u, :], bq_dram[bass.ds(at, DH), :]).then_inc(sem(f"b_head{u}_loaded"), 16)
                    sp.dma_start(b_k[0:DH, u, :], bk_dram[bass.ds(at, DH), :]).then_inc(sem(f"b_head{u}_loaded"), 16)

            sp.wait_ge(sem("c_added"), T)
            for u in range(2):
                sp.dma_start(d_q[DH:AUG, u, :], t["alibi_q"]).then_inc(sem(f"d_head{u}_loaded"), 16)
            for g in range(C * B):
                cc, bb = g // B, g % B
                for n, dst, s_in, s_out in ((0, dq_dram, "d_q_proj", "d_q_stored"), (1, dk_dram, "d_k_proj", "d_k_stored")):
                    sp.wait_ge(sem(s_in), g + 1)
                    sp.dma_start(dst[(bb * C + cc) * P:(bb * C + cc + 1) * P, :],
                                 d_proj[:, n, :]).then_inc(sem(s_out), 16)
            sp.wait_ge(sem("d_q_stored"), 16 * C * B)
            sp.wait_ge(sem("d_k_stored"), 16 * C * B)

            def load_d(u, at, ah):
                sp.dma_start(d_q[0:DH, u, :], dq_dram[bass.ds(at, DH), :]).then_inc(sem(f"d_head{u}_loaded"), 16)
                sp.dma_start(d_k[0:DH, u, :], dk_dram[bass.ds(at, DH), :]).then_inc(sem(f"d_head{u}_loaded"), 16)
                sp.dma_start(d_k[DH:AUG, u, :], t["alibi_k"][bass.ds(ah, 2), :]).then_inc(sem(f"d_head{u}_loaded"), 16)

            for u in range(2):
                load_d(u, u * DH, u * 2)
            with sp.Fori(0, B * H // 2 - 1) as i:
                for u in range(2):
                    sp.wait_ge(sem("d_scores"), i * (2 * TB) + (u + 1) * TB)
                    load_d(u, (i * 2 + (2 + u)) * DH, (i * 2 + (2 + u)) * 2)

            sp.wait_ge(sem("e_added"), T)
            sp.dma_start(f_mu, t["muT"]).then_inc(sem("f_table_loaded"), 16)
            sp.dma_start(f_sig, t["sigmaT"]).then_inc(sem("f_table_loaded"), 16)
            sp.wait_ge(sem("f_chosen"), 1)
            for bb in range(B):
                k = sp.value_load(f_idx[bb:bb + 1, 0:1], min_val=0, max_val=E - 1)
                sp.dma_start(f_down[:, bb], t["down"][bass.ds(k, 1)].rearrange("a p c r -> p (a c) r")).then_inc(sem("f_expert_loaded"), 16)
                sp.dma_start(f_up[0:R, bb], t["up"][bass.ds(k, 1)].rearrange("a r d -> (a r) d")).then_inc(sem("f_expert_loaded"), 16)
                sp.dma_start(f_conv[:, bb], t["convT"][bass.ds(k, 1)].rearrange("a p c d -> p (a c) d")).then_inc(sem("f_expert_loaded"), 16)
                sp.dma_start(f_db[0:R, bb:bb + 1], t["down_b"][bass.ds(k, 1)].rearrange("a r o -> (a r) o")).then_inc(sem("f_expert_loaded"), 16)
                sp.dma_start(f_ub[:, bb], t["up_b"][bass.ds(k, 1)].rearrange("a p c -> p (a c)")).then_inc(sem("f_expert_loaded"), 16)
                sp.dma_start(f_cb[0:1, bb], t["conv_b"][bass.ds(k, 1)]).then_inc(sem("f_expert_loaded"), 16)
            for tt in range(T):
                sp.wait_ge(sem("f_added"), tt + 1)
                sp.dma_start(t["out"][:, tt, :], x[:, tt, :]).then_inc(sem("out_stored"), 16)
            sp.wait_ge(sem("out_stored"), 16 * T)

        @block.tensor
        def _(pe):
            def transposes(src, ready, done, free, dst_banks=bank):
                for tt in range(T):
                    pe.wait_ge(sem(ready), tt + 1)
                    if tt >= 2:
                        pe.wait_ge(sem(free), tt - 1)
                    for cc in range(C):
                        last = nc.tensor.transpose(dst_banks[tt % 2][:, cc * P:(cc + 1) * P],
                                                   src(tt, cc), ident[:])
                    last.then_inc(sem(done), 1)

            def tile_of(buf):
                return lambda tt, cc: buf[:, tt, cc * P:(cc + 1) * P]

            def channels_out(dst, wT, col, srcT, tok, n, k=C):
                for ic in range(k):
                    last = nc.tensor.matmul(dst, wT[:, ic, col:col + P], srcT[:, ic, tok:tok + n],
                                            start=(ic == 0), stop=(ic == k - 1))
                return last

            def tokens_out(dst, srcT, tt, wT, lo, n, bias=None, k=C):
                for ic in range(k):
                    last = nc.tensor.matmul(dst, srcT[:, ic, tt * P:(tt + 1) * P], wT[:, ic, lo:lo + n],
                                            start=(ic == 0), stop=(ic == k - 1 and bias is None))
                if bias is not None:
                    last = nc.tensor.matmul(dst, ones[0:1, 0:P], bias, start=False, stop=True)
                return last

            pe.wait_ge(sem("const_loaded"), 16 * 18)
            pe.wait_ge(sem("ones_set"), 1)
            transposes(tile_of(y), "a_y", "a_tr", "a_yT")
            pe.wait_ge(sem("w_A"), 64)
            pe.wait_ge(sem("a_yT"), T)
            for g in range(C * B):
                cc, bb = g // B, g % B
                if g >= 2:
                    pe.wait_ge(sem("a_qT"), g - 1)
                channels_out(half(0, g % 2), w["qkvT"], cc * P, yT, bb * S, S).then_inc(sem("a_q_ps"), 1)
            for tt in range(T):
                if tt >= 2:
                    pe.wait_ge(sem("a_kv"), tt - 1)
                tokens_out(half(1, tt % 2), yT, tt, w["qkvT"], D, 2 * D).then_inc(sem("a_kv_ps"), 1)
            pe.wait_ge(sem("a_vones"), 1)
            pe.wait_ge(sem("a_kv"), T)
            for bb in range(B):
                for cc in range(C):
                    for j in range(TB):
                        tt = bb * TB + j
                        last = nc.tensor.matmul(half(2, bb)[:, cc * KV:cc * KV + P + 1],
                                                a_k[:, tt, cc * P:(cc + 1) * P], a_v[:, tt, cc, :],
                                                start=(j == 0), stop=(j == TB - 1))
                last.then_inc(sem("a_kvsum_ps"), 1)
            pe.wait_ge(sem("w_abs"), 1)
            nc.tensor.matmul(half(0, 0)[:, 0:3], ones[:], w_abs[:], start=True, stop=True).then_inc(sem("w_abs_ps"), 1)
            for tt in range(T):
                pe.wait_ge(sem("a_kvsum"), tt // TB + 1)
                if tt >= 2:
                    pe.wait_ge(sem("a_at"), tt - 1)
                for cc in range(C):
                    last = nc.tensor.matmul(bank[tt % 2][:, cc * KV:(cc + 1) * KV],
                                            a_qT[:, cc, tt * P:(tt + 1) * P], a_kv[:, tt // TB, cc, :],
                                            start=True, stop=True)
                last.then_inc(sem("a_at_ps"), 1)
            pe.wait_ge(sem("a_at"), T)
            transposes(tile_of(y), "a_at", "a_tr2", "a_atT")
            for tt in range(T):
                pe.wait_ge(sem("a_atT"), tt + 1)
                if tt < 2:
                    pe.wait_ge(sem("w_mean"), 1)
                else:
                    pe.wait_ge(sem("a_x1"), tt - 1)
                tokens_out(half(0, tt % 2)[:, 0:D], yT, tt, w["projT"], 0, D, rows["proj_b"][:]).then_inc(sem("a_proj_ps"), 1)
            transposes(tile_of(y), "a_y2", "a_tr3", "a_y2T")
            pe.wait_ge(sem("a_y2T"), T)
            for g in range(MC * B):
                m, bb = g // B, g % B
                if g >= 2:
                    pe.wait_ge(sem("a_hT"), g - 1)
                channels_out(half(1, g % 2), w["conv1T"], m * P, yT, bb * S, S).then_inc(sem("a_h_ps"), 1)
            pe.wait_ge(sem("a_hT"), MC * B)
            for tt in range(T):
                if tt >= 2:
                    pe.wait_ge(sem("a_added"), tt - 1)
                tokens_out(half(2, tt % 2)[:, 0:D], a_hT, tt, conv2T, 0, D, rows["conv2_b"][:], k=MC).then_inc(sem("a_mlp_ps"), 1)

            transposes(tile_of(y), "b_y", "b_tr", "b_yT")
            pe.wait_ge(sem("w_B"), 64)
            pe.wait_ge(sem("b_yT"), T)
            for g in range(C * B):
                cc, bb = g // B, g % B
                if g >= 2:
                    pe.wait_ge(sem("b_q_proj"), g - 1)
                channels_out(half(0, g % 2), w["xqT"], cc * P, yT, bb * S, S).then_inc(sem("b_q_ps"), 1)
            for g in range(C * B * 2):
                cc, bb, hh = g // (2 * B), g // 2 % B, g % 2
                if g >= 2:
                    pe.wait_ge(sem("b_k_proj"), g - 1)
                channels_out(half(1, g % 2), w["xkT"], cc * P, ctxT, bb * SC + 512 * hh, 512).then_inc(sem("b_k_ps"), 1)
            pe.wait_ge(sem("b_k_proj"), C * B * 2)

            with pe.Fori(0, B * H // 2) as i:
                def scores(j):
                    u, qt = j // TB, j % TB
                    if qt == 0:
                        pe.wait_ge(sem(f"b_head{u}_loaded"), i * 32 + 32)
                    if j >= 2:
                        pe.wait_ge(sem("b_s_copied"), i * 8 + (j - 1))
                    for hh in range(2):
                        last = nc.tensor.matmul(wide[j % 2][:, 512 * hh:512 * hh + 512],
                                                b_q[0:DH, u, qt * P:(qt + 1) * P],
                                                b_k[0:DH, u, 512 * hh:512 * hh + 512], start=True, stop=True)
                    last.then_inc(sem("b_scores"), 1)

                def weights_out(j):
                    u = j // TB
                    pe.wait_ge(sem("b_probs"), i * 8 + (j + 1))
                    if j >= 1:
                        pe.wait_ge(sem("b_pT"), i * 8 + j)
                    for kt in range(CTB):
                        last = nc.tensor.transpose(wide[2][:, kt * P:(kt + 1) * P],
                                                   b_p[:, j % 2, kt * P:(kt + 1) * P], ident[:])
                    last.then_inc(sem("b_p_tr"), 1)
                    pe.wait_ge(sem("b_pT"), i * 8 + (j + 1))
                    if j >= 1:
                        pe.wait_ge(sem("b_o"), i * 8 + j)
                    for kt in range(CTB):
                        last = nc.tensor.matmul(bank[0][:, 0:DH], b_pT[:, j % 2, kt * P:(kt + 1) * P],
                                                vB[:, bass.ds((i * 2 + u) * (CTB * DH) + kt * DH, DH)],
                                                start=(kt == 0), stop=(kt == CTB - 1))
                    last.then_inc(sem("b_o_ps"), 1)

                for j in range(2 * TB):
                    scores(j)
                    if j >= 1:
                        weights_out(j - 1)
                weights_out(2 * TB - 1)
                pe.wait_ge(sem("b_o"), i * 8 + 8)

            for tt in range(T):
                pe.wait_ge(sem("c_xq"), tt + 1)
                if tt >= 2:
                    pe.wait_ge(sem("c_xqT"), tt - 1)
                for cc in range(C):
                    last = nc.tensor.transpose(bank[tt % 2][:, 0:P].bitcast(BF16)[:, cc * P:(cc + 1) * P],
                                               c_qb[:, tt % 2, cc * P:(cc + 1) * P], ident_bf[:])
                last.then_inc(sem("c_xq_tr"), 1)
            pe.wait_ge(sem("w_rounded"), 3)
            pe.wait_ge(sem("c_xqT"), T)
            for tt in range(T):
                for n, (dst, wq) in enumerate(((wide[0], wq_gate), (wide[1], wq_up))):
                    if tt >= 1:
                        pe.wait_ge(sem(("c_g", "c_h")[n]), tt)
                    for hh in range(2):
                        for ic in range(C):
                            last = nc.tensor.matmul(dst[:, 512 * hh:512 * hh + 512], c_qT[:, ic, tt * P:(tt + 1) * P],
                                                    wq[:, ic, 512 * hh:512 * hh + 512],
                                                    start=(ic == 0), stop=(ic == C - 1))
                    last.then_inc(sem(("c_g_ps", "c_u_ps")[n]), 1)
                pe.wait_ge(sem("c_hq"), tt + 1)
                if tt >= 2:
                    pe.wait_ge(sem("c_hT"), tt - 1)
                for kt in range(KC):
                    last = nc.tensor.transpose(half(2, tt % 2).bitcast(BF16)[:, kt * P:(kt + 1) * P],
                                               c_hb[:, tt % 2, kt * P:(kt + 1) * P], ident_bf[:])
                last.then_inc(sem("c_h_tr"), 1)
                pe.wait_ge(sem("c_hT"), tt + 1)
                if tt >= 2:
                    pe.wait_ge(sem("c_added"), tt - 1)
                for kt in range(KC):
                    last = nc.tensor.matmul(bank[tt % 2][:, 0:D], c_hT[:, tt % 2, kt], wq_down[:, kt, :],
                                            start=(kt == 0), stop=(kt == KC - 1))
                last.then_inc(sem("c_d_ps"), 1)

            transposes(tile_of(y), "d_y", "d_tr", "d_yT")
            pe.wait_ge(sem("w_DEF"), 16 * 8)
            pe.wait_ge(sem("d_yT"), T)
            for g in range(C * B):
                cc, bb = g // B, g % B
                for n, wn in enumerate(("aqT", "akT")):
                    if g >= 1:
                        pe.wait_ge(sem(("d_q_proj", "d_k_proj")[n]), g)
                    channels_out(half(0, n), w[wn], cc * P, yT, bb * S, S).then_inc(sem(("d_q_ps", "d_k_ps")[n]), 1)
            for tt in range(T):
                if tt >= 2:
                    pe.wait_ge(sem("d_v"), tt - 1)
                tokens_out(half(1, tt % 2)[:, 0:D], yT, tt, w["avT"], 0, D, rows["av_b"][:]).then_inc(sem("d_v_ps"), 1)
            pe.wait_ge(sem("d_v"), T)
            with pe.Fori(0, B * H // 2) as i:
                def scores(j):
                    u, qt = j // TB, j % TB
                    if qt == 0:
                        pe.wait_ge(sem(f"d_head{u}_loaded"), i * 48 + (16 + 48))
                    if j >= 2:
                        pe.wait_ge(sem("d_s"), i * 8 + (j - 1))
                    n = (qt + 1) * P
                    nc.tensor.matmul(half(0, j % 2)[:, 0:n], d_q[0:AUG, u, qt * P:(qt + 1) * P],
                                     d_k[0:AUG, u, 0:n], start=True, stop=True).then_inc(sem("d_scores"), 1)

                def weights_out(j):
                    u, qt = j // TB, j % TB
                    pe.wait_ge(sem("d_p"), i * 8 + (j + 1))
                    if j >= 2:
                        pe.wait_ge(sem("d_pT"), i * 8 + (j - 1))
                    for kt in range(qt + 1):
                        last = nc.tensor.transpose(half(1, j % 2)[:, kt * P:(kt + 1) * P],
                                                   d_p[:, j % 2, kt * P:(kt + 1) * P], ident[:])
                    last.then_inc(sem("d_p_tr"), 1)
                    pe.wait_ge(sem("d_pT"), i * 8 + (j + 1))
                    if j >= 2:
                        pe.wait_ge(sem("d_o"), i * 8 + (j - 1))
                    for kt in range(qt + 1):
                        last = nc.tensor.matmul(bank[j % 2][:, 0:DH], d_pT[:, j % 2, kt * P:(kt + 1) * P],
                                                d_v[:, bass.ds((i * 2 + u) * (TB * DH) + kt * DH, DH)],
                                                start=(kt == 0), stop=(kt == qt))
                    last.then_inc(sem("d_o_ps"), 1)

                for j in range(2 * TB):
                    scores(j)
                    if j >= 1:
                        weights_out(j - 1)
                weights_out(2 * TB - 1)
                pe.wait_ge(sem("d_o"), i * 8 + 8)
            transposes(tile_of(y), "d_ao", "d_ao_tr", "d_aoT")
            for tt in range(T):
                pe.wait_ge(sem("d_aoT"), tt + 1)
                if tt >= 2:
                    pe.wait_ge(sem("d_added"), tt - 1)
                tokens_out(half(2, tt % 2)[:, 0:D], yT, tt, w["aoT"], 0, D, rows["ao_b"][:]).then_inc(sem("d_out_ps"), 1)

            pe.wait_ge(sem("d_added"), T)
            for tt in range(CT):
                if tt >= 2:
                    pe.wait_ge(sem("e_kv"), tt - 1)
                tokens_out(half(0, tt % 2), ctxT, tt, w["lkvT"], 0, 2 * D, rows["lkv_b"][:]).then_inc(sem("e_kv_ps"), 1)
            pe.wait_ge(sem("e_kv"), CT)
            for bb in range(B):
                for cc in range(C):
                    for j in range(CTB):
                        tt = bb * CTB + j
                        last = nc.tensor.matmul(half(1, bb)[:, cc * P:(cc + 1) * P],
                                                e_k[:, tt, cc * P:(cc + 1) * P], e_v[:, tt, cc * P:(cc + 1) * P],
                                                start=(j == 0), stop=(j == CTB - 1))
                last.then_inc(sem("e_sum_ps"), 1)
            for tt in range(CT):
                pe.wait_ge(sem("e_kk"), tt + 1)
                for cc in range(C):
                    bb = tt // CTB
                    last = nc.tensor.matmul(half(2, cc)[:, bb:bb + 1],
                                            e_kk[:, tt % 2, cc * P:(cc + 1) * P], ones[:, 0:1],
                                            start=(tt % CTB == 0), stop=(tt % CTB == CTB - 1))
                last.then_inc(sem("e_kk_summed"), 1)
            transposes(tile_of(y), "e_y", "e_tr", "e_yT")
            pe.wait_ge(sem("e_yT"), T)
            for g in range(C * B):
                cc, bb = g // B, g % B
                if g >= 2:
                    pe.wait_ge(sem("e_qelu"), g - 1)
                channels_out(half(0, g % 2), w["lqT"], cc * P, yT, bb * S, S).then_inc(sem("e_q_ps"), 1)
            pe.wait_ge(sem("e_qT"), C * B)
            pe.wait_ge(sem("e_sum"), B)
            for tt in range(T):
                if tt >= 2:
                    pe.wait_ge(sem("e_at"), tt - 1)
                for cc in range(C):
                    nc.tensor.matmul(half(1, tt % 2)[:, cc * P:(cc + 1) * P], e_qT[:, cc, tt * P:(tt + 1) * P],
                                     e_kv[:, tt // TB, cc, :], start=True, stop=True)
                for cc in range(C):
                    last = nc.tensor.matmul(half(1, tt % 2)[:, D + cc * HC:D + (cc + 1) * HC],
                                            e_qq[:, cc, tt * P:(tt + 1) * P], headmask[:], start=True, stop=True)
                last.then_inc(sem("e_at_ps"), 1)
            transposes(tile_of(y), "e_at", "e_tr2", "e_atT")
            for tt in range(T):
                pe.wait_ge(sem("e_atT"), tt + 1)
                if tt >= 2:
                    pe.wait_ge(sem("e_added"), tt - 1)
                tokens_out(half(2, tt % 2)[:, 0:D], yT, tt, w["loT"], 0, D, rows["lo_b"][:]).then_inc(sem("e_out_ps"), 1)

            transposes(tile_of(y), "f_y", "f_tr", "f_yT")
            pe.wait_ge(sem("f_moments"), 1)
            n_terms = [(f_m2, f_iv), (f_m1s, f_mi)]
            for k_, (m, tab) in enumerate(n_terms):
                for cc in range(C):
                    nc.tensor.matmul(half(0, 0)[0:B, 0:E], m[:, cc, :], tab[:, cc, :],
                                     start=(k_ == 0 and cc == 0), stop=False)
            for cc in range(C):
                last = nc.tensor.matmul(half(0, 0)[0:B, 0:E], ones[:, 0:B], f_m2i[:, cc, :],
                                        start=False, stop=(cc == C - 1))
            last.then_inc(sem("f_loss_ps"), 1)
            pe.wait_ge(sem("f_expert_loaded"), 16 * 6 * B)
            for bb in range(B):
                for ic in range(C):
                    last = nc.tensor.matmul(half(1, bb)[0:R, :], f_down[:, bb, ic, :], yT[:, ic, bb * S:(bb + 1) * S],
                                            start=(ic == 0), stop=(ic == C - 1))
                last.then_inc(sem("f_h_ps"), 1)
            for bb in range(B):
                pe.wait_ge(sem("f_hT"), bb + 1)
                for cc in range(C):
                    g = bb * C + cc
                    if g >= 2:
                        pe.wait_ge(sem("f_aT"), g - 1)
                    nc.tensor.matmul(half(2, g % 2), f_up[0:R, bb, cc * P:(cc + 1) * P], f_hT[0:R, bb * S:(bb + 1) * S],
                                     start=True, stop=True).then_inc(sem("f_a_ps"), 1)
            for tt in range(T):
                bb = tt // TB
                pe.wait_ge(sem("f_aT"), C * (bb + 1))
                if tt >= 2:
                    pe.wait_ge(sem("f_added"), tt - 1)
                dst = bank[tt % 2][:, 0:D]
                for ic in range(C):
                    nc.tensor.matmul(dst, yT[:, ic, tt * P:(tt + 1) * P], w["baseT"][:, ic, :], start=(ic == 0), stop=False)
                for ic in range(C):
                    nc.tensor.matmul(dst, f_aT[:, ic, tt * P:(tt + 1) * P], f_conv[:, bb, ic, :], start=False, stop=False)
                nc.tensor.matmul(dst, ones[0:1, 0:P], rows["base_b"][:], start=False, stop=False)
                nc.tensor.matmul(dst, ones[0:1, 0:P], f_cb[0:1, bb, :], start=False, stop=True).then_inc(sem("f_out_ps"), 1)

        @block.scalar
        def _(act):
            def roots(ready, done, src=var, dst=sd):
                act.wait_ge(sem(ready), 1)
                nc.scalar.activation(dst[:], src[:], ACT.Sqrt).then_inc(sem(done), 1)

            def copy_T(tr, done, scales=None):
                for tt in range(T):
                    act.wait_ge(sem(tr), tt + 1)
                    if scales is None:
                        nc.scalar.activation(yT[:, :, tt * P:(tt + 1) * P],
                                             bank[tt % 2][:, 0:D].rearrange("p (c n) -> p c n", c=C),
                                             ACT.Copy).then_inc(sem(done), 1)
                    else:
                        nc.scalar.activation(yT[:, 0, tt * P:(tt + 1) * P], bank[tt % 2][:, 0:P], ACT.Copy,
                                             scale=cols[scales][:, 0:1])
                        nc.scalar.activation(yT[:, 1, tt * P:(tt + 1) * P], bank[tt % 2][:, P:D], ACT.Copy,
                                             scale=cols[scales][:, 1:2]).then_inc(sem(done), 1)

            act.wait_ge(sem("const_loaded"), 16 * 18)
            roots("a_var", "a_sd")
            for tt in range(T):
                act.wait_ge(sem("a_ln"), tt + 1)
                if tt >= 2:
                    act.wait_ge(sem("act_sq"), tt - 1)
                nc.scalar.activation(sq[:, tt % 2, 0:D], xin[:, tt, :], ACT.Square,
                                     accum_out=var[:, tt:tt + 1]).then_inc(sem("act_sq"), 1)
            act.wait_ge(sem("act_sq"), T)
            nc.scalar.activation(sd[:], var[:], ACT.Sqrt).then_inc(sem("a_norm"), 1)
            copy_T("a_tr", "a_yT", "scale1")
            for g in range(C * B):
                cc, bb = g // B, g % B
                act.wait_ge(sem("a_q_ps"), g + 1)
                nc.scalar.activation(sq[:, g % 2, :], half(0, g % 2), ACT.Square).then_inc(sem("act_sq"), 1)
                act.wait_ge(sem("act_sq"), T + g + 1)
                nc.scalar.activation(a_qT[:, cc, bb * S:(bb + 1) * S], sq[:, g % 2, :], ACT.Exp,
                                     scale=-0.5).then_inc(sem("a_qT"), 1)
            for tt in range(T):
                act.wait_ge(sem("a_kv_ps"), tt + 1)
                if tt < 2:
                    act.wait_ge(sem("a_qT"), C * B)
                nc.scalar.activation(sq[:, tt % 2, 0:D], half(1, tt % 2)[:, 0:D], ACT.Square).then_inc(sem("act_sq"), 1)
                nc.scalar.activation(a_v[:, tt, :, 0:P], half(1, tt % 2)[:, D:2 * D].rearrange("p (c n) -> p c n", c=C),
                                     ACT.Copy)
                act.wait_ge(sem("act_sq"), T + C * B + tt + 1)
                nc.scalar.activation(a_k[:, tt, :], sq[:, tt % 2, 0:D], ACT.Exp, scale=-0.5).then_inc(sem("a_kv"), 1)
            copy_T("a_tr2", "a_atT")
            for tt in range(T):
                act.wait_ge(sem("a_x1"), tt + 1)
                act.wait_ge(sem("a_kv"), T)
                if tt >= 2:
                    act.wait_ge(sem("act_sq"), 2 * T + C * B + tt - 1)
                nc.scalar.activation(sq[:, tt % 2, 0:D], a_x1[:, tt, :], ACT.Square,
                                     accum_out=var[:, tt:tt + 1]).then_inc(sem("act_sq"), 1)
            act.wait_ge(sem("act_sq"), 3 * T + C * B)
            nc.scalar.activation(sd[:], var[:], ACT.Sqrt).then_inc(sem("a_norm"), 1)
            copy_T("a_tr3", "a_y2T", "scale2")
            for g in range(MC * B):
                m, bb = g // B, g % B
                act.wait_ge(sem("a_h_ps"), g + 1)
                nc.scalar.activation(a_hT[:, m, bb * S:(bb + 1) * S], half(1, g % 2), ACT.Gelu,
                                     bias=cols["conv1_b"][:, m:m + 1]).then_inc(sem("a_hT"), 1)

            act.wait_ge(sem("w_rounded"), 3)
            roots("b_var", "b_sd")
            copy_T("b_tr", "b_yT")
            for g in range(C * B):
                act.wait_ge(sem("b_q_ps"), g + 1)
                if g >= 2:
                    act.wait_ge(sem(f"b_q_stored{g % 2}"), 16 * (g // 2))
                nc.scalar.activation(b_proj[:, g % 2, :], half(0, g % 2), ACT.Copy, scale=DH ** -0.5).then_inc(sem("b_q_proj"), 1)
            for g in range(2):
                act.wait_ge(sem(f"b_q_stored{g}"), 16 * C * B // 2)
            for g in range(C * B * 2):
                act.wait_ge(sem("b_k_ps"), g + 1)
                if g >= 2:
                    act.wait_ge(sem(f"b_k_stored{g % 2}"), 16 * (g // 2))
                nc.scalar.activation(b_proj[:, g % 2, :], half(1, g % 2), ACT.Copy).then_inc(sem("b_k_proj"), 1)

            with act.Fori(0, B * H // 2) as i:
                for j in range(2 * TB):
                    act.wait_ge(sem("b_scores"), i * 8 + (j + 1))
                    if j >= 2:
                        act.wait_ge(sem("b_exp"), i * 8 + (j - 1))
                        act.wait_ge(sem("b_probs"), i * 8 + (j - 1))
                    nc.scalar.activation(b_s[:, j % 2, :], wide[j % 2][:], ACT.Copy).then_inc(sem("b_s_copied"), 1)
                    act.wait_ge(sem("b_neg"), i * 8 + (j + 1))
                    nc.scalar.activation(b_e[:, j % 2, :], b_s[:, j % 2, :], ACT.Exp, bias=b_neg[:, j % 2, :],
                                         accum_out=b_all[:, j % 2, :]).then_inc(sem("b_exp"), 1)
                    if j >= 1:
                        act.wait_ge(sem("b_p_tr"), i * 8 + j)
                        if j >= 3:
                            act.wait_ge(sem("b_o_ps"), i * 8 + (j - 2))
                        nc.scalar.activation(b_pT[:, (j - 1) % 2, :], wide[2][:], ACT.Copy).then_inc(sem("b_pT"), 1)
                act.wait_ge(sem("b_p_tr"), i * 8 + 8)
                act.wait_ge(sem("b_o_ps"), i * 8 + 6)
                nc.scalar.activation(b_pT[:, 1, :], wide[2][:], ACT.Copy).then_inc(sem("b_pT"), 1)
                act.wait_ge(sem("b_o"), i * 8 + 8)

            roots("c_var", "c_sd")
            for tt in range(T):
                act.wait_ge(sem("c_g_ps"), tt + 1)
                if tt >= 2:
                    act.wait_ge(sem("c_h"), tt - 1)
                nc.scalar.activation(c_g[:, tt % 2, :], wide[0][:], ACT.Silu, scale=c_ag[:, tt:tt + 1]).then_inc(sem("c_g"), 1)

            roots("d_var", "d_sd")
            copy_T("d_tr", "d_yT")
            for g in range(C * B):
                cc = g // B
                act.wait_ge(sem("d_k_ps"), g + 1)
                if g >= 1:
                    act.wait_ge(sem("d_k_stored"), 16 * g)
                nc.scalar.activation(d_proj[:, 1, :], half(0, 1), ACT.Identity, bias=cols["ak_b"][:, cc:cc + 1]).then_inc(sem("d_k_proj"), 1)
            with act.Fori(0, B * H // 2) as i:
                for j in range(2 * TB):
                    n = (j % TB + 1) * P
                    act.wait_ge(sem("d_neg"), i * 8 + (j + 1))
                    if j >= 2:
                        act.wait_ge(sem("d_p_tr"), i * 8 + (j - 1))
                        act.wait_ge(sem("d_o"), i * 8 + (j - 1))
                    nc.scalar.activation(d_p[:, j % 2, 0:n], d_s[:, j % 2, 0:n], ACT.Exp, bias=d_neg[:, j % 2, :],
                                         accum_out=d_sum[:, j % 2, :]).then_inc(sem("d_p"), 1)
                    if j >= 1:
                        m = ((j - 1) % TB + 1) * P
                        act.wait_ge(sem("d_p_tr"), i * 8 + j)
                        if j >= 3:
                            act.wait_ge(sem("d_o_ps"), i * 8 + (j - 2))
                        nc.scalar.activation(d_pT[:, (j - 1) % 2, 0:m], half(1, (j - 1) % 2)[:, 0:m], ACT.Copy).then_inc(sem("d_pT"), 1)
                act.wait_ge(sem("d_p_tr"), i * 8 + 8)
                act.wait_ge(sem("d_o_ps"), i * 8 + 6)
                nc.scalar.activation(d_pT[:, 1, :], half(1, 1), ACT.Copy).then_inc(sem("d_pT"), 1)
                act.wait_ge(sem("d_o"), i * 8 + 8)
            copy_T("d_ao_tr", "d_aoT")

            for tt in range(CT):
                act.wait_ge(sem("e_kmin"), tt + 1)
                nc.scalar.activation(e_t[:, tt % 2, D:2 * D], e_t[:, tt % 2, 0:D], ACT.Exp).then_inc(sem("e_kexp"), 1)
            for tt in range(CT):
                act.wait_ge(sem("e_kv"), tt + 1)
                if tt >= 2:
                    act.wait_ge(sem("e_kk_summed"), tt - 1)
                nc.scalar.activation(e_kk[:, tt % 2, :], e_k[:, tt, :], ACT.Square).then_inc(sem("e_kk"), 1)
            act.wait_ge(sem("e_kk_summed"), CT)
            for cc in range(C):
                nc.scalar.activation(e_kn[:, cc * B:(cc + 1) * B], half(2, cc)[:, 0:B], ACT.Sqrt,
                                     scale=float(S)).then_inc(sem("e_kn"), 1)
            roots("e_var", "e_sd")
            copy_T("e_tr", "e_yT")
            for g in range(C * B):
                cc, bb = g // B, g % B
                act.wait_ge(sem("e_qmin"), g + 1)
                nc.scalar.activation(e_qq[:, cc, bb * S:(bb + 1) * S], sq[:, g % 2, :], ACT.Exp).then_inc(sem("e_qexp"), 1)
            for g in range(C * B):
                cc, bb = g // B, g % B
                act.wait_ge(sem("e_qelu"), g + 1)
                nc.scalar.activation(e_qq[:, cc, bb * S:(bb + 1) * S], e_qT[:, cc, bb * S:(bb + 1) * S],
                                     ACT.Square).then_inc(sem("e_qT"), 1)
            for tt in range(T):
                act.wait_ge(sem("e_at_ps"), tt + 1)
                if tt >= 2:
                    act.wait_ge(sem("e_at"), tt - 1)
                nc.scalar.activation(e_qn[:, tt % 2], half(1, tt % 2)[:, D:D + H].rearrange("p (c h) -> p c h", c=C),
                                     ACT.Sqrt, scale=float(DH)).then_inc(sem("e_qn"), 1)
            copy_T("e_tr2", "e_atT")

            roots("f_var", "f_sd")
            copy_T("f_tr", "f_yT")
            for bb in range(B):
                act.wait_ge(sem("f_h_ps"), bb + 1)
                nc.scalar.activation(f_hT[0:R, bb * S:(bb + 1) * S], half(1, bb)[0:R, :], ACT.Relu,
                                     bias=f_db[0:R, bb:bb + 1]).then_inc(sem("f_hT"), 1)
            for g in range(C * B):
                bb, cc = g // C, g % C
                act.wait_ge(sem("f_a_ps"), g + 1)
                nc.scalar.activation(f_aT[:, cc, bb * S:(bb + 1) * S], half(2, g % 2), ACT.Identity,
                                     bias=f_ub[:, bb, cc:cc + 1]).then_inc(sem("f_aT"), 1)

        @block.gpsimd
        def _(pool):
            pool.wait_ge(sem("w_mean"), 1)
            for n, wq in enumerate((wq_gate, wq_up, wq_down)):
                nc.gpsimd.tensor_scalar(w_raw[n], w_raw[n], w_scale[:, n:n + 1], 1.0, ALU.mult, ALU.mult).then_inc(sem("pool_step"), 1)
                pool.wait_ge(sem("pool_step"), 4 * n + 1)
                nc.gpsimd.tensor_scalar(w_raw[n], w_raw[n], ROUND, 1.0, ALU.add, ALU.mult).then_inc(sem("pool_step"), 1)
                pool.wait_ge(sem("pool_step"), 4 * n + 2)
                nc.gpsimd.tensor_scalar(w_raw[n], w_raw[n], -ROUND, 1.0, ALU.add, ALU.mult).then_inc(sem("pool_step"), 1)
                pool.wait_ge(sem("pool_step"), 4 * n + 3)
                nc.gpsimd.tensor_scalar(w_raw[n], w_raw[n], 1.0, -1.0, ALU.min, ALU.max).then_inc(sem("pool_step"), 1)
                pool.wait_ge(sem("pool_step"), 4 * n + 4)
                nc.gpsimd.tensor_copy(wq[:].rearrange("p a b -> p (a b)"), w_raw[n]).then_inc(sem("w_rounded"), 1)

        @block.vector
        def _(dve):
            steps = [0]

            def link(ins):
                steps[0] += 1
                ins.then_inc(sem("dve_step"), 1)
                dve.wait_ge(sem("dve_step"), steps[0])

            def gate():
                nc.vector.tensor_copy(gate_out[:], w_abs[:, 0:1])

            def layer_norm(s, dst, done):
                for tt in range(T):
                    ins = nc.vector.bn_stats(bn[:, tt, :], x[:, tt, :])
                link(ins)
                for tt in range(T):
                    ins = nc.vector.bn_aggr(mv[:, tt, :], bn[:, tt, :])
                link(ins)
                nc.vector.tensor_scalar(var[:], mv[:, :, 1], LN_EPS, None, ALU.add).then_inc(sem(s + "_var"), 1)
                dve.wait_ge(sem(s + "_sd"), 1)
                link(nc.vector.reciprocal(rstd[:], sd[:]))
                for tt in range(T):
                    nc.vector.tensor_scalar(dst[:, tt, :], x[:, tt, :], mv[:, tt, 0:1], rstd[:, tt:tt + 1],
                                            ALU.subtract, ALU.mult).then_inc(sem(done), 1)

            def rms_scale(src, n, done):
                dve.wait_ge(sem("a_norm"), n)
                link(nc.vector.reciprocal(rstd[:], sd[:]))
                link(nc.vector.tensor_scalar(rstd[:], rstd[:], RMS_GAIN, None, ALU.mult))
                for tt in range(T):
                    nc.vector.tensor_scalar(y[:, tt, :], src[:, tt, :], rstd[:, tt:tt + 1], None,
                                            ALU.mult).then_inc(sem(done), 1)

            nc.vector.memset(ones[:], 1.0).then_inc(sem("ones_set"), 1)
            nc.vector.memset(a_v[:, :, :, P:P + 1], 1.0).then_inc(sem("a_vones"), 1)
            dve.wait_ge(sem("const_loaded"), 16 * 18)
            link(nc.vector.tensor_copy(ident_bf[:], ident[:]))
            dve.wait_ge(sem("x_loaded"), 16)

            layer_norm("a", xin, "a_ln")
            rms_scale(xin, 1, "a_y")
            dve.wait_ge(sem("w_raw_loaded"), 48)
            for n in range(3):
                ins = nc.vector.tensor_reduce(w_abs[:, n:n + 1], w_raw[n], AX.X, ALU.add, apply_absolute_value=True)
            ins.then_inc(sem("w_abs"), 1)
            for bb in range(B):
                dve.wait_ge(sem("a_kvsum_ps"), bb + 1)
                for cc in range(C):
                    ps = half(2, bb)[:, cc * KV:(cc + 1) * KV]
                    nc.vector.tensor_tensor(a_kv[:, bb, cc, 0:P], ps[:, 0:P], blockmask[:], ALU.mult)
                    ins = nc.vector.tensor_scalar(a_kv[:, bb, cc, P:KV], headmask[:], ps[:, P:P + 1], None, ALU.mult)
                ins.then_inc(sem("a_kvsum"), 1)
            dve.wait_ge(sem("w_abs_ps"), 1)
            link(nc.vector.tensor_scalar(w_mean[:], half(0, 0)[:, 0:3], 1.0 / (D * INNER), 1e-5, ALU.mult, ALU.max))
            nc.vector.reciprocal(w_scale[:], w_mean[:]).then_inc(sem("w_mean"), 1)
            for tt in range(T):
                dve.wait_ge(sem("a_at_ps"), tt + 1)
                ps = bank[tt % 2][:, 0:C * KV].rearrange("p (c k) -> p c k", c=C)
                link(nc.vector.tensor_scalar(a_den[:, tt % 2], ps[:, :, P:KV], 1e-6, None, ALU.add))
                link(nc.vector.reciprocal(a_z, a_den[:, tt % 2]))
                for cc in range(C):
                    ins = nc.vector.tensor_tensor(y[:, tt, cc * P:(cc + 1) * P].rearrange("p (h e) -> p h e", h=HC),
                                            ps[:, cc, 0:P].rearrange("p (h e) -> p h e", h=HC),
                                            a_z[:, cc, :].unsqueeze(2).broadcast_to([P, HC, DH]),
                                            ALU.mult)
                ins.then_inc(sem("a_at"), 1)
            for tt in range(T):
                dve.wait_ge(sem("a_proj_ps"), tt + 1)
                link(nc.vector.tensor_tensor(a_tmp[:, tt % 2, :], half(0, tt % 2)[:, 0:D], gamma[:], ALU.mult))
                nc.vector.tensor_tensor(a_x1[:, tt, :], a_tmp[:, tt % 2, :], xin[:, tt, :], ALU.add).then_inc(sem("a_x1"), 1)
            rms_scale(a_x1, 2, "a_y2")
            for tt in range(T):
                dve.wait_ge(sem("a_mlp_ps"), tt + 1)
                link(nc.vector.tensor_tensor(a_tmp[:, tt % 2, :], half(2, tt % 2)[:, 0:D], gamma[:], ALU.mult))
                link(nc.vector.tensor_tensor(a_tmp[:, tt % 2, :], a_tmp[:, tt % 2, :], a_x1[:, tt, :], ALU.add))
                ins = nc.vector.tensor_tensor(x[:, tt, :], x[:, tt, :], a_tmp[:, tt % 2, :], ALU.add)
                ins.then_inc(sem("a_added"), 1)
            dve.wait_ge(sem("a_added"), T)

            layer_norm("b", y, "b_y")
            DS = 2 * NTOP + 2
            with dve.Fori(0, B * H // 2) as i:
                def chain(ins, k):
                    ins.then_inc(sem("b_step"), 1)
                    dve.wait_ge(sem("b_step"), k)

                def top(j):
                    s, z, m8 = b_s[:, j % 2, :], b_z[:, j % 2, :], b_max[:, j % 2]
                    dve.wait_ge(sem("b_s_copied"), i * 8 + (j + 1))
                    gate()
                    dve.sem_clear(sem("b_step"))
                    chain(nc.vector.max(m8[:, 0, :], s), 1)
                    nc.vector.tensor_scalar(b_neg[:, j % 2, :], m8[:, 0, 0:1], -1.0, None,
                                            ALU.mult).then_inc(sem("b_neg"), 1)
                    chain(nc.vector.match_replace(z, m8[:, 0, :], s, MARK), 2)
                    for r in range(1, NTOP):
                        chain(nc.vector.max(m8[:, r, :], z), 2 * r + 1)
                        ins = nc.vector.match_replace(z, m8[:, r, :], z, MARK)
                        chain(ins, 2 * r + 2)

                def probs(j):
                    dve.wait_ge(sem("b_exp"), i * 8 + (j + 1))
                    if j >= 2:
                        dve.wait_ge(sem("b_p_tr"), i * 8 + (j - 1))
                    nc.vector.scalar_tensor_tensor(out=b_p[:, j % 2, :], in0=b_z[:, j % 2, :], scalar=MARK,
                                                   in1=b_e[:, j % 2, :], op0=ALU.is_equal, op1=ALU.mult,
                                                   accum_out=b_top[:, j % 2, :]).then_inc(sem("b_probs"), 1)
                    dve.wait_ge(sem("b_probs"), i * 8 + (j + 1))
                    chain(nc.vector.scalar_tensor_tensor(out=b_den[:, j % 2, :], in0=b_all[:, j % 2, :], scalar=1e-9,
                                                         in1=b_top[:, j % 2, :], op0=ALU.mult, op1=ALU.add), DS - 1)
                    chain(nc.vector.reciprocal(b_r[:, j % 2, :], b_den[:, j % 2, :]), DS)

                def out(j):
                    dve.wait_ge(sem("b_o_ps"), i * 8 + (j + 1))
                    nc.vector.tensor_scalar(b_o[:, bass.ds((i * 8 + j) * DH, DH)], bank[0][:, 0:DH],
                                            b_r[:, j % 2, :], None, ALU.mult).then_inc(sem("b_o"), 1)

                for j in range(2 * TB):
                    top(j)
                    probs(j)
                    if j >= 1:
                        out(j - 1)
                out(2 * TB - 1)
            dve.wait_ge(sem("b_o"), B * H * TB)
            o4 = b_o.rearrange("p (b h q e) -> p b h q e", b=B, h=H, q=TB)
            for tt in range(T):
                xv = x[:, tt, :].rearrange("p (h e) -> p h e", h=H)
                nc.vector.tensor_tensor(xv, xv, o4[:, tt // TB, :, tt % TB, :], ALU.add).then_inc(sem("b_added"), 1)
            dve.wait_ge(sem("b_added"), T)

            layer_norm("c", y, "c_y")
            dve.wait_ge(sem("c_y"), T)

            def absmax(dst, src):
                return nc.vector.tensor_reduce(dst, src, AX.X, ALU.max, apply_absolute_value=True)

            link(absmax(c_am, y[:]))
            link(nc.vector.tensor_scalar(c_am1, c_am, 1e-5, None, ALU.max))
            link(nc.vector.reciprocal(c_s, c_am1))
            link(nc.vector.tensor_scalar(c_s, c_s, 127.0, None, ALU.mult))
            link(nc.vector.tensor_scalar(c_si, c_am1, 1.0 / 127.0, None, ALU.mult))
            nc.vector.tensor_scalar(c_ag, c_si, w_mean[:, 0:1], None, ALU.mult)
            link(nc.vector.tensor_scalar(c_au, c_si, w_mean[:, 1:2], None, ALU.mult))

            def xq_T(tt):
                dve.wait_ge(sem("c_xq_tr"), tt + 1)
                nc.vector.tensor_scalar(c_qT[:, :, tt * P:(tt + 1) * P],
                                        bank[tt % 2][:, 0:P].bitcast(BF16).rearrange("p (c n) -> p c n", c=C),
                                        127.0, -128.0, ALU.min, ALU.max).then_inc(sem("c_xqT"), 1)

            for tt in range(T):
                link(nc.vector.tensor_scalar(c_q[:, tt % 2, :], y[:, tt, :], c_s[:, tt:tt + 1], ROUND, ALU.mult, ALU.add))
                if tt >= 2:
                    dve.wait_ge(sem("c_xq_tr"), tt - 1)
                nc.vector.tensor_scalar(c_qb[:, tt % 2, :], c_q[:, tt % 2, :], ROUND, None, ALU.subtract).then_inc(sem("c_xq"), 1)
                if tt >= 1:
                    xq_T(tt - 1)
            xq_T(T - 1)
            for tt in range(T):
                dve.wait_ge(sem("c_g"), tt + 1)
                dve.wait_ge(sem("c_u_ps"), tt + 1)
                nc.vector.scalar_tensor_tensor(out=c_h[:, tt % 2, :], in0=wide[1][:], scalar=c_au[:, tt:tt + 1],
                                               in1=c_g[:, tt % 2, :], op0=ALU.mult, op1=ALU.mult).then_inc(sem("c_h"), 1)
                dve.wait_ge(sem("c_h"), tt + 1)
                link(absmax(c_hm[:, tt:tt + 1], c_h[:, tt % 2, :]))
                link(nc.vector.tensor_scalar(c_hm1[:, tt:tt + 1], c_hm[:, tt:tt + 1], 1e-5, None, ALU.max))
                link(nc.vector.reciprocal(c_hs[:, tt:tt + 1], c_hm1[:, tt:tt + 1]))
                link(nc.vector.tensor_scalar(c_hi[:, tt:tt + 1], c_hs[:, tt:tt + 1], 127.0, None, ALU.mult))
                link(nc.vector.tensor_scalar(c_hr, c_h[:, tt % 2, :], c_hi[:, tt:tt + 1], ROUND, ALU.mult, ALU.add))
                if tt >= 2:
                    dve.wait_ge(sem("c_h_tr"), tt - 1)
                nc.vector.tensor_scalar(c_hb[:, tt % 2, :], c_hr, ROUND, None, ALU.subtract).then_inc(sem("c_hq"), 1)
                nc.vector.tensor_scalar(c_ad[:, tt:tt + 1], c_hm1[:, tt:tt + 1], w_mean[:, 2:3], 1.0 / 127.0, ALU.mult, ALU.mult).then_inc(sem("c_ad"), 1)
                dve.wait_ge(sem("c_h_tr"), tt + 1)
                nc.vector.tensor_scalar(c_hT[:, tt % 2], half(2, tt % 2).bitcast(BF16).rearrange("p (k n) -> p k n", k=KC),
                                        127.0, -128.0, ALU.min, ALU.max).then_inc(sem("c_hT"), 1)
                dve.wait_ge(sem("c_d_ps"), tt + 1)
                dve.wait_ge(sem("c_ad"), tt + 1)
                nc.vector.scalar_tensor_tensor(out=x[:, tt, :], in0=bank[tt % 2][:, 0:D], scalar=c_ad[:, tt:tt + 1],
                                               in1=x[:, tt, :], op0=ALU.mult, op1=ALU.add).then_inc(sem("c_added"), 1)
            dve.wait_ge(sem("c_added"), T)

            layer_norm("d", y, "d_y")
            for g in range(C * B):
                cc = g // B
                dve.wait_ge(sem("d_q_ps"), g + 1)
                if g >= 1:
                    dve.wait_ge(sem("d_q_stored"), 16 * g)
                nc.vector.tensor_scalar(d_proj[:, 0, :], half(0, 0), cols["aq_b"][:, cc:cc + 1], DH ** -0.5,
                                        ALU.add, ALU.mult).then_inc(sem("d_q_proj"), 1)
            v4 = d_v.rearrange("p (b h q e) -> p b h q e", b=B, h=H, q=TB)
            for tt in range(T):
                dve.wait_ge(sem("d_v_ps"), tt + 1)
                nc.vector.tensor_copy(v4[:, tt // TB, :, tt % TB, :],
                                      half(1, tt % 2)[:, 0:D].rearrange("p (h e) -> p h e", h=H)).then_inc(sem("d_v"), 1)
            with dve.Fori(0, B * H // 2) as i:
                def row_max(j):
                    n = (j % TB + 1) * P
                    dve.wait_ge(sem("d_scores"), i * 8 + (j + 1))
                    if j >= 2:
                        dve.wait_ge(sem("d_p"), i * 8 + (j - 1))
                    gate()
                    nc.vector.tensor_tensor_reduce(out=d_s[:, j % 2, 0:n], in0=half(0, j % 2)[:, 0:n],
                                                   in1=causal[:, S - n:S], scale=1.0, scalar=MARK, op0=ALU.add,
                                                   op1=ALU.max, accum_out=d_max[:, j % 2, :]).then_inc(sem("d_s"), 1)
                    dve.wait_ge(sem("d_s"), i * 8 + (j + 1))
                    nc.vector.tensor_scalar(d_neg[:, j % 2, :], d_max[:, j % 2, :], -1.0, None,
                                            ALU.mult).then_inc(sem("d_neg"), 1)

                def out(j):
                    dve.wait_ge(sem("d_o_ps"), i * 8 + (j + 1))
                    nc.vector.reciprocal(d_r[:, j % 2, :], d_sum[:, j % 2, :]).then_inc(sem("d_r"), 1)
                    dve.wait_ge(sem("d_r"), i * 8 + (j + 1))
                    nc.vector.tensor_scalar(d_o[:, bass.ds((i * 8 + j) * DH, DH)], bank[j % 2][:, 0:DH],
                                            d_r[:, j % 2, :], None, ALU.mult).then_inc(sem("d_o"), 1)

                for j in range(2 * TB):
                    row_max(j)
                    if j >= 1:
                        out(j - 1)
                out(2 * TB - 1)
            dve.wait_ge(sem("d_o"), B * H * TB)
            o5 = d_o.rearrange("p (b h q e) -> p b h q e", b=B, h=H, q=TB)
            for tt in range(T):
                nc.vector.tensor_copy(y[:, tt, :].rearrange("p (h e) -> p h e", h=H),
                                      o5[:, tt // TB, :, tt % TB, :]).then_inc(sem("d_ao"), 1)

            def add_to_x(ready, banks, done):
                for tt in range(T):
                    dve.wait_ge(sem(ready), tt + 1)
                    nc.vector.tensor_tensor(x[:, tt, :], banks(tt % 2)[:, 0:D], x[:, tt, :], ALU.add).then_inc(sem(done), 1)
                dve.wait_ge(sem(done), T)

            add_to_x("d_out_ps", lambda k: half(2, k), "d_added")

            for tt in range(CT):
                k_ps = half(0, tt % 2)[:, 0:D]
                dve.wait_ge(sem("e_kv_ps"), tt + 1)
                nc.vector.tensor_scalar(e_t[:, tt % 2, 0:D], k_ps, 0.0, None, ALU.min).then_inc(sem("e_kmin"), 1)
                nc.vector.tensor_copy(e_v[:, tt, :], half(0, tt % 2)[:, D:2 * D])
                dve.wait_ge(sem("e_kexp"), tt + 1)
                link(nc.vector.tensor_scalar(e_t[:, tt % 2, 0:D], e_t[:, tt % 2, D:2 * D], -1.0, None, ALU.add))
                nc.vector.scalar_tensor_tensor(out=e_k[:, tt, :], in0=k_ps, scalar=0.0, in1=e_t[:, tt % 2, 0:D],
                                               op0=ALU.max, op1=ALU.add).then_inc(sem("e_kv"), 1)
            dve.wait_ge(sem("e_kn"), C)
            link(nc.vector.reciprocal(e_kr, e_kn))
            for bb in range(B):
                dve.wait_ge(sem("e_sum_ps"), bb + 1)
                for cc in range(C):
                    n = cc * B + bb
                    ins = nc.vector.scalar_tensor_tensor(out=e_kv[:, bb, cc, :], in0=half(1, bb)[:, cc * P:(cc + 1) * P],
                                                         scalar=e_kr[:, n:n + 1], in1=blockmask[:],
                                                         op0=ALU.mult, op1=ALU.mult)
                ins.then_inc(sem("e_sum"), 1)
            layer_norm("e", y, "e_y")
            for g in range(C * B):
                cc, bb = g // B, g % B
                q_ps, bias, sl = half(0, g % 2), cols["lq_b"][:, cc:cc + 1], slice(bb * S, (bb + 1) * S)
                dve.wait_ge(sem("e_q_ps"), g + 1)
                nc.vector.tensor_scalar(sq[:, g % 2, :], q_ps, bias, 0.0, ALU.add, ALU.min).then_inc(sem("e_qmin"), 1)
                nc.vector.tensor_scalar(e_qT[:, cc, sl], q_ps, bias, 0.0, ALU.add, ALU.max)
                dve.wait_ge(sem("e_qexp"), g + 1)
                link(nc.vector.tensor_scalar(e_qq[:, cc, sl], e_qq[:, cc, sl], -1.0, None, ALU.add))
                nc.vector.tensor_tensor(e_qT[:, cc, sl], e_qT[:, cc, sl], e_qq[:, cc, sl], ALU.add).then_inc(sem("e_qelu"), 1)
            for tt in range(T):
                dve.wait_ge(sem("e_qn"), tt + 1)
                link(nc.vector.reciprocal(e_qr[:, tt % 2], e_qn[:, tt % 2]))
                for cc in range(C):
                    ins = nc.vector.tensor_tensor(y[:, tt, cc * P:(cc + 1) * P].rearrange("p (h e) -> p h e", h=HC),
                                                  half(1, tt % 2)[:, cc * P:(cc + 1) * P].rearrange("p (h e) -> p h e", h=HC),
                                                  e_qr[:, tt % 2, cc, :].unsqueeze(2).broadcast_to([P, HC, DH]), ALU.mult)
                ins.then_inc(sem("e_at"), 1)
            add_to_x("e_out_ps", lambda k: half(2, k), "e_added")

            layer_norm("f", y, "f_y")
            dve.wait_ge(sem("f_table_loaded"), 32)
            link(nc.vector.tensor_tensor(f_s2, f_sig, f_sig, ALU.mult))
            link(nc.vector.reciprocal(f_iv, f_s2))
            link(nc.vector.tensor_tensor(f_mi, f_mu, f_iv, ALU.mult))
            link(nc.vector.tensor_tensor(f_m2i, f_mu, f_mi, ALU.mult))
            dve.wait_ge(sem("f_yT"), T)
            for cc in range(C):
                for bb in range(B):
                    ins = nc.vector.bn_stats(f_bn[:, cc, bb, :], yT[:, cc, bb * S:(bb + 1) * S])
            link(ins)
            for cc in range(C):
                for bb in range(B):
                    ins = nc.vector.bn_aggr(f_mv[:, cc, bb, :], f_bn[:, cc, bb, :])
            link(ins)
            nc.vector.tensor_scalar(f_m1s, f_mv[:, :, :, 0], -2.0, None, ALU.mult)
            link(nc.vector.tensor_tensor(f_sq, f_mv[:, :, :, 0], f_mv[:, :, :, 0], ALU.mult))
            nc.vector.tensor_tensor(f_m2, f_sq, f_mv[:, :, :, 1], ALU.add).then_inc(sem("f_moments"), 1)
            dve.wait_ge(sem("f_loss_ps"), 1)
            link(nc.vector.tensor_scalar(f_nl[0:B], half(0, 0)[0:B, 0:E], -1.0 / D, None, ALU.mult))
            link(nc.vector.max(f_best[0:B], f_nl[0:B]))
            nc.vector.max_index(f_idx[0:B], f_best[0:B], f_nl[0:B]).then_inc(sem("f_chosen"), 1)
            add_to_x("f_out_ps", lambda k: bank[k], "f_added")


def kernel(**inputs):
    import concourse.bacc as bacc
    from concourse.bass_utils import run_bass_kernel_spmd

    def arr(name):
        return np.asarray(inputs[name])

    def keep(a):
        return np.ascontiguousarray(a)

    def tiles(a):
        return keep(a.reshape(-1, P, a.shape[-1]).transpose(1, 0, 2))

    def wT(*names):
        return tiles(np.concatenate([arr(n) for n in names], 0).T)

    def col(name):
        return keep(arr(name).reshape(-1, P).T)

    def row(*names):
        return keep(np.concatenate([arr(n) for n in names]).reshape(1, -1))

    ctx = arr("ctx_1024").reshape(B * SC, D)
    pos = np.arange(S, dtype=np.float32)
    slopes = np.array([(2.0 ** (-8.0 / H)) * (2.0 ** (-8.0 / H)) ** k for k in range(H)], dtype=np.float32)
    block = np.kron(np.eye(HC, dtype=np.float32), np.ones((DH, DH), np.float32))
    mask = np.zeros((P, S), np.float32)
    mask[:, S - P:] = np.where(np.arange(P)[None, :] > np.arange(P)[:, None], np.float32(MASKED), np.float32(0))
    alibi_k = np.stack([np.stack([sl * pos, -sl * np.ones(S, np.float32)]) for sl in slopes])
    a = {
        "x": tiles(arr("x").reshape(B * S, D)),
        "ident": np.eye(P, dtype=np.float32),
        "blockmask": block,
        "headmask": keep(block[:, ::DH]),
        "causal": mask,
        "alibi_q": np.stack([np.ones(S, np.float32), pos]),
        "alibi_k": keep(np.tile(alibi_k.astype(np.float32), (B, 1, 1)).reshape(B * H * 2, S)),
        "ctxT": tiles(ctx.T),
        "ctxV": keep(ctx.reshape(B, CTB, P, H, DH).transpose(2, 0, 3, 1, 4).reshape(P, B * H * CTB * DH)),
        "scale1": col("L0_attn_scale1"), "scale2": col("L0_attn_scale2"), "conv1_b": col("L0_attn_conv1_b"),
        "aq_b": col("L1_attn_q_b"), "ak_b": col("L1_attn_k_b"), "lq_b": col("L1_xattn_bq"),
        "proj_b": row("L0_attn_proj_b"), "conv2_b": row("L0_attn_conv2_b"), "av_b": row("L1_attn_v_b"),
        "ao_b": row("L1_attn_o_b"), "lkv_b": row("L1_xattn_bk", "L1_xattn_bv"), "lo_b": row("L1_xattn_bo"),
        "base_b": row("L1_ffn_base_b"), "gamma": row("L0_attn_gamma"),
        "qkvT": wT("L0_attn_qkv_w"), "projT": wT("L0_attn_proj_w"), "conv1T": wT("L0_attn_conv1_w"),
        "conv2T": wT("L0_attn_conv2_w"), "xqT": wT("L0_xattn_Wq"), "xkT": wT("L0_xattn_Wk"),
        "gateT": wT("L0_ffn_w_gate").reshape(P, -1), "upT": wT("L0_ffn_w_up").reshape(P, -1),
        "downT": wT("L0_ffn_w_down").reshape(P, -1),
        "aqT": wT("L1_attn_q_w"), "akT": wT("L1_attn_k_w"), "avT": wT("L1_attn_v_w"), "aoT": wT("L1_attn_o_w"),
        "lqT": wT("L1_xattn_Wq"), "lkvT": wT("L1_xattn_Wk", "L1_xattn_Wv"), "loT": wT("L1_xattn_Wo"),
        "baseT": wT("L1_ffn_base_W"),
        "muT": tiles(arr("L1_ffn_disc_mu").T), "sigmaT": tiles(arr("L1_ffn_disc_sigma").T),
        "down": keep(arr("L1_ffn_down_W").reshape(E, C, P, R).transpose(0, 2, 1, 3)),
        "up": keep(arr("L1_ffn_up_W")),
        "convT": keep(arr("L1_ffn_conv_W").transpose(0, 2, 1).reshape(E, C, P, D).transpose(0, 2, 1, 3)),
        "down_b": keep(arr("L1_ffn_down_b").reshape(E, R, 1)),
        "up_b": keep(arr("L1_ffn_up_b").reshape(E, C, P).transpose(0, 2, 1)),
        "conv_b": keep(arr("L1_ffn_conv_b")),
    }
    nc = bacc.Bacc("TRN2", target_bir_lowering=False, num_devices=1)
    t = {n: nc.dram_tensor("in_" + n, v.shape, mybir.dt.from_np(v.dtype), kind="ExternalInput").ap()
         for n, v in a.items()}
    t["out"] = nc.dram_tensor("out", (P, T, D), F32, kind="ExternalOutput").ap()
    decoder(nc, t)
    r = run_bass_kernel_spmd(nc, [{"in_" + n: v for n, v in a.items()}], core_ids=[0])
    return r.results[0]["out"].transpose(1, 0, 2).reshape(B, S, D)
```

```python
from contextlib import ExitStack

import numpy as np

import concourse.bass as bass
from concourse import mybir

P = 128
B, S, D = 2, 512, 256
SC = 1024
H, DH = 16, 16
T = B * S // P
TB = S // P
CT = B * SC // P
CTB = SC // P
C = D // P
HC = P // DH
HID = 512
MC = HID // P
INNER = 1024
KC = INNER // P
E, R = 8, 64
K_TOP = 64
NTOP = K_TOP // 8
NBLK = 16
BLK = SC // NBLK
PAIRS = B * H * TB // 2
V1 = DH + 1
I32 = mybir.dt.int32
KV = P + HC
AUG = DH + 2

F32 = mybir.dt.float32
BF16 = mybir.dt.bfloat16
U32 = mybir.dt.uint32
ALU = mybir.AluOpType
ACT = mybir.ActivationFunctionType
AX = mybir.AxisListType

LN_EPS = 1e-5
RMS_GAIN = 16.0 + 1e-6
ROUND = 12582912.0
MARK = -3.0e38
MASKED = -1.0e30


def decoder(nc, t):
    with ExitStack() as ctx:
        def sb(name, shape, dt=F32):
            return ctx.enter_context(nc.sbuf_tensor(name, shape, dt))

        sems = {}

        def sem(name):
            if name not in sems:
                sems[name] = ctx.enter_context(nc.semaphore(name))
            return sems[name]

        bank = [ctx.enter_context(nc.psum_tensor(f"bank{i}", [P, 512], F32)) for i in range(2)]
        wide = [ctx.enter_context(nc.psum_tensor(f"wide{i}", [P, 1024], F32)) for i in range(3)]
        def half(i, j):
            return wide[i][:, 512 * j:512 * j + 512]

        ident = sb("ident", [P, P])
        negident = sb("negident", [P, P])
        ident_bf = sb("ident_bf", [P, P], BF16)
        ones = sb("ones", [P, P])
        blockmask = sb("blockmask", [P, P])
        headmask = sb("headmask", [P, HC])
        causal = sb("causal", [P, S])
        x = sb("x", [P, T, D])
        y = sb("y", [P, T, D])
        yT = sb("yT", [P, C, T * P])
        xin = sb("xin", [P, T, D])
        ctxT = sb("ctxT", [P, C, B * SC])
        bn = sb("bn", [P, T, 6])
        mv = sb("mv", [P, T, 2])
        var = sb("var", [P, T])
        sd = sb("sd", [P, T])
        rstd = sb("rstd", [P, T])
        sq = sb("sq", [P, 2, 512])
        names = {"qkvT": 3 * D, "projT": D, "conv1T": HID, "xqT": D, "xkT": D,
                 "aqT": D, "akT": D, "avT": D, "aoT": D, "lqT": D, "lkvT": 2 * D, "loT": D, "baseT": D}
        w = {n: sb("w_" + n, [P, C, k]) for n, k in names.items()}
        conv2T = sb("w_conv2T", [P, MC, D])
        wq_gate = sb("wq_gate", [P, C, INNER], BF16)
        wq_up = sb("wq_up", [P, C, INNER], BF16)
        wq_down = sb("wq_down", [P, KC, D], BF16)
        cols = {n: sb("c_" + n, [P, k]) for n, k in
                {"scale1": C, "scale2": C, "conv1_b": MC, "aq_b": C, "ak_b": C, "lq_b": C}.items()}
        rows = {n: sb("r_" + n, [1, k]) for n, k in
                {"proj_b": D, "conv2_b": D, "av_b": D, "ao_b": D, "lkv_b": 2 * D, "lo_b": D,
                 "base_b": D}.items()}
        gamma = sb("gamma", [P, D])
        vB = sb("vB", [P, B * H * CTB * V1])
        w_mean = sb("w_mean", [P, 3])
        w_scale = sb("w_scale", [P, 3])
        w_abs = sb("w_abs", [P, 3])
        gate_out = sb("gate_out", [P, TB])
        bq_dram = nc.dram_tensor("bq_dram", [B * H * DH, S], F32, kind="Internal").ap()
        bk_dram = nc.dram_tensor("bk_dram", [B * H * DH, SC], F32, kind="Internal").ap()
        dq_dram = nc.dram_tensor("dq_dram", [B * H * DH, S], F32, kind="Internal").ap()
        dk_dram = nc.dram_tensor("dk_dram", [B * H * DH, S], F32, kind="Internal").ap()

        WORK = 18560
        work = sb("work", [P, WORK])

        class Area:
            def __init__(self):
                self.at = 0

            def take(self, *shape, dt=F32):
                n = int(np.prod(shape))
                words = n if dt != BF16 else (n + 1) // 2
                ap = work[:, self.at:self.at + words]
                self.at += words
                assert self.at <= WORK, self.at
                if dt != F32:
                    ap = ap.bitcast(dt)
                if len(shape) > 1:
                    lab = "abcd"[:len(shape)]
                    ap = ap.rearrange(f"p ({' '.join(lab)}) -> p {' '.join(lab)}",
                                      **{k: v for k, v in zip(lab, shape)})
                return ap

        a = Area()
        a_qT = a.take(C, T * P)
        a_k = a.take(T, D)
        a_v = a.take(T, C, P + 1)
        a_kv = a.take(B, C, KV)
        a_den = a.take(2, C, HC)
        a_z = a.take(C, HC)
        a_x1 = a.take(T, D)
        a_tmp = a.take(2, D)
        a_hT = a.take(MC, T * P)
        w_raw = [vB[:, 0:C * INNER], vB[:, C * INNER:2 * C * INNER], a.take(C * INNER)]
        b = Area()
        b_q = b.take(2, S)
        b_k = b.take(2, SC)
        b_s = b.take(4, SC)
        b_e = b.take(4, SC)
        b_z = b.take(4, SC)
        b_m = b.take(2, SC, dt=BF16)
        b_junk = b.take(2, SC, dt=BF16)
        b_proj = b_z[:, 0, :].rearrange("p (a n) -> p a n", a=2)
        b_pT = yT
        b_o = y[:].rearrange("p t d -> p (t d)")
        b_cand = b.take(2, NBLK * 8)
        b_m8 = b.take(2, 8)
        b_f8 = b.take(2, 8)
        b_g8 = b.take(2, 8)
        b_neg = b.take(2)
        b_te = b.take(2)
        b_cnt = b.take(2)
        b_least = b.take(2)
        b_bad = b.take(2)
        b_flagf = b.take(1)
        b_flag = b.take(1, dt=I32)
        b_all = b.take(4, 2)
        b_den = b.take(2)
        b_r = b.take(2)
        g_max = b.take(2, NTOP, 8)
        g_neg = b.take(2, 1)
        g_all = b.take(2, 1)
        g_top = b.take(2, 1)
        g_den = b.take(2, 1)
        g_r = b.take(2, 1)
        c = Area()
        c_am = c.take(T)
        c_am1 = c.take(T)
        c_s = c.take(T)
        c_si = c.take(T)
        c_ag = c.take(T)
        c_au = c.take(T)
        c_q = c.take(2, D)
        c_qb = c.take(2, D, dt=BF16)
        c_qT = c.take(C, T * P, dt=BF16)
        c_g = c.take(2, INNER)
        c_h = c.take(2, INNER)
        c_hr = c.take(INNER)
        c_hb = c.take(2, INNER, dt=BF16)
        c_hT = c.take(2, KC, P, dt=BF16)
        c_hm = c.take(T)
        c_hm1 = c.take(T)
        c_hs = c.take(T)
        c_hi = c.take(T)
        c_ad = c.take(T)
        d = Area()
        d_q = d.take(2, S)
        d_k = d.take(2, S)
        d_s = d.take(2, TB, S)
        d_p = d.take(2, TB, S)
        d_pT = d.take(2, S)
        d_v = d.take(B * H * TB * V1)
        d_o = d.take(B * H * TB * DH)
        d_proj = d.take(2, 512)
        d_max = d.take(2, TB)
        d_neg = d.take(2, TB)
        d_r = d.take(2, TB)
        e = Area()
        e_k = e.take(CT, D)
        e_v = e.take(CT, D)
        e_t = e.take(2, 2 * D)
        e_kk = e.take(2, D)
        e_qT = e.take(C, T * P)
        e_qq = e.take(C, T * P)
        e_kv = e.take(B, C, P)
        e_kn = e.take(B * C)
        e_kr = e.take(B * C)
        e_qn = e.take(2, C, HC)
        e_qr = e.take(2, C, HC)
        f = Area()
        f_mu = f.take(C, E)
        f_sig = f.take(C, E)
        f_s2 = f.take(C, E)
        f_iv = f.take(C, E)
        f_mi = f.take(C, E)
        f_mm = f.take(C, E)
        f_m2i = f.take(C, E)
        f_bn = f.take(C, B, 6)
        f_mv = f.take(C, B, 2)
        f_m1s = f.take(C, B)
        f_m2 = f.take(C, B)
        f_sq = f.take(C, B)
        f_nl = f.take(E)
        f_best = f.take(8)
        f_idx = f.take(8, dt=U32)
        f_down = f.take(B, C, R)
        f_up = f.take(B, D)
        f_conv = f.take(B, C, D)
        f_db = f.take(B)
        f_ub = f.take(B, C)
        f_cb = f.take(B, D)
        f_hT = f.take(T * P)
        f_aT = f.take(C, T * P)

        below = sb("below", [P, 8])

        def wait(eng, name, value):
            if not (isinstance(value, int) and value <= 0):
                eng.wait_ge(sem(name), value)

        block = ctx.enter_context(nc.Block())

        LNS = ["A", "B", "C", "D", "E", "F"]

        @block.sync
        def _(sp):
            sp.dma_start(x[:], t["x"]).then_inc(sem("x_loaded"), 16)
            for n, ap in (("ident", ident), ("blockmask", blockmask), ("headmask", headmask),
                          ("causal", causal), ("below", below)):
                sp.dma_start(ap[:], t[n]).then_inc(sem("const_loaded"), 16)
            for n in ("scale1", "scale2", "conv1_b", "aq_b", "ak_b", "lq_b"):
                sp.dma_start(cols[n][:], t[n]).then_inc(sem("const_loaded"), 16)
            for n in ("proj_b", "conv2_b", "av_b", "ao_b", "lkv_b", "lo_b", "base_b"):
                sp.dma_start(rows[n][:], t[n]).then_inc(sem("const_loaded"), 16)
            sp.dma_start(gamma[:], t["gamma"].broadcast_to([P, D])).then_inc(sem("const_loaded"), 16)
            sp.dma_start(w["qkvT"][:], t["qkvT"]).then_inc(sem("w_A"), 16)
            sp.dma_start(w["projT"][:], t["projT"]).then_inc(sem("w_A"), 16)
            sp.dma_start(w["conv1T"][:], t["conv1T"]).then_inc(sem("w_A"), 16)
            sp.dma_start(conv2T[:], t["conv2T"]).then_inc(sem("w_A"), 16)
            for n, name in enumerate(("gateT", "upT", "downT")):
                sp.dma_start(w_raw[n], t[name]).then_inc(sem("w_raw_loaded"), 16)
            sp.dma_start(ctxT[:], t["ctxT"]).then_inc(sem("w_B"), 16)
            sp.dma_start(w["xkT"][:], t["xkT"]).then_inc(sem("w_B"), 16)
            sp.dma_start(w["xqT"][:], t["xqT"]).then_inc(sem("w_B"), 16)
            for n in ("aqT", "akT", "avT", "aoT", "lqT", "lkvT", "loT", "baseT"):
                sp.dma_start(w[n][:], t[n]).then_inc(sem("w_DEF"), 16)

            sp.wait_ge(sem("w_rounded"), 2)
            sp.dma_start(vB[:], t["ctxV"]).then_inc(sem("w_B"), 16)

            for g in range(C * B):
                cc, bb = g // B, g % B
                sp.wait_ge(sem("b_q_proj"), g + 1)
                sp.dma_start(bq_dram[(bb * C + cc) * P:(bb * C + cc + 1) * P, :],
                             b_proj[:, g % 2, :]).then_inc(sem(f"b_q_stored{g % 2}"), 16)
            for g in range(C * B * 2):
                cc, bb, hh = g // (2 * B), g // 2 % B, g % 2
                sp.wait_ge(sem("b_k_proj"), g + 1)
                sp.dma_start(bk_dram[(bb * C + cc) * P:(bb * C + cc + 1) * P, 512 * hh:512 * hh + 512],
                             b_proj[:, g % 2, :]).then_inc(sem(f"b_k_stored{g % 2}"), 16)
            for g in range(2):
                sp.wait_ge(sem(f"b_q_stored{g}"), 16 * C * B // 2)
                sp.wait_ge(sem(f"b_k_stored{g}"), 16 * C * B)
            def load_b(u, at, name):
                sp.dma_start(b_q[0:DH, u, :], bq_dram[bass.ds(at, DH), :]).then_inc(sem(f"{name}{u}_loaded"), 16)
                sp.dma_start(b_k[0:DH, u, :], bk_dram[bass.ds(at, DH), :]).then_inc(sem(f"{name}{u}_loaded"), 16)

            for name, scored in (("b_head", "b_scores"), ("g_head", "g_scores")):
                def stage_heads():
                    for u in range(2):
                        load_b(u, u * DH, name)
                    with sp.Fori(0, B * H // 2 - 1) as i:
                        for u in range(2):
                            sp.wait_ge(sem(scored), i * (2 * TB) + (u + 1) * TB)
                            load_b(u, (i * 2 + (2 + u)) * DH, name)

                if name == "b_head":
                    stage_heads()
                else:
                    sp.wait_ge(sem("b_flag"), 1)
                    with sp.If(sp.value_load(b_flag[0:1, 0:1], min_val=0, max_val=2 * P) > 0):
                        stage_heads()

            sp.wait_ge(sem("c_added"), T)
            for u in range(2):
                sp.dma_start(d_q[DH:AUG, u, :], t["alibi_q"]).then_inc(sem(f"d_head{u}_loaded"), 16)
            for g in range(C * B):
                cc, bb = g // B, g % B
                for n, dst, s_in, s_out in ((0, dq_dram, "d_q_proj", "d_q_stored"), (1, dk_dram, "d_k_proj", "d_k_stored")):
                    sp.wait_ge(sem(s_in), g + 1)
                    sp.dma_start(dst[(bb * C + cc) * P:(bb * C + cc + 1) * P, :],
                                 d_proj[:, n, :]).then_inc(sem(s_out), 16)
            sp.wait_ge(sem("d_q_stored"), 16 * C * B)
            sp.wait_ge(sem("d_k_stored"), 16 * C * B)

            def load_d(u, at, ah):
                sp.dma_start(d_q[0:DH, u, :], dq_dram[bass.ds(at, DH), :]).then_inc(sem(f"d_head{u}_loaded"), 16)
                sp.dma_start(d_k[0:DH, u, :], dk_dram[bass.ds(at, DH), :]).then_inc(sem(f"d_head{u}_loaded"), 16)
                sp.dma_start(d_k[DH:AUG, u, :], t["alibi_k"][bass.ds(ah, 2), :]).then_inc(sem(f"d_head{u}_loaded"), 16)

            for u in range(2):
                load_d(u, u * DH, u * 2)
            with sp.Fori(0, B * H // 2 - 1) as i:
                for u in range(2):
                    sp.wait_ge(sem("d_scores"), i * (2 * TB) + (u + 1) * TB)
                    load_d(u, (i * 2 + (2 + u)) * DH, (i * 2 + (2 + u)) * 2)

            sp.wait_ge(sem("e_added"), T)
            sp.dma_start(f_mu, t["muT"]).then_inc(sem("f_table_loaded"), 16)
            sp.dma_start(f_sig, t["sigmaT"]).then_inc(sem("f_table_loaded"), 16)
            sp.wait_ge(sem("f_chosen"), 1)
            for bb in range(B):
                k = sp.value_load(f_idx[bb:bb + 1, 0:1], min_val=0, max_val=E - 1)
                sp.dma_start(f_down[:, bb], t["down"][bass.ds(k, 1)].rearrange("a p c r -> p (a c) r")).then_inc(sem("f_expert_loaded"), 16)
                sp.dma_start(f_up[0:R, bb], t["up"][bass.ds(k, 1)].rearrange("a r d -> (a r) d")).then_inc(sem("f_expert_loaded"), 16)
                sp.dma_start(f_conv[:, bb], t["convT"][bass.ds(k, 1)].rearrange("a p c d -> p (a c) d")).then_inc(sem("f_expert_loaded"), 16)
                sp.dma_start(f_db[0:R, bb:bb + 1], t["down_b"][bass.ds(k, 1)].rearrange("a r o -> (a r) o")).then_inc(sem("f_expert_loaded"), 16)
                sp.dma_start(f_ub[:, bb], t["up_b"][bass.ds(k, 1)].rearrange("a p c -> p (a c)")).then_inc(sem("f_expert_loaded"), 16)
                sp.dma_start(f_cb[0:1, bb], t["conv_b"][bass.ds(k, 1)]).then_inc(sem("f_expert_loaded"), 16)
            for tt in range(T):
                sp.wait_ge(sem("f_added"), tt + 1)
                sp.dma_start(t["out"][:, tt, :], x[:, tt, :]).then_inc(sem("out_stored"), 16)
            sp.wait_ge(sem("out_stored"), 16 * T)

        @block.tensor
        def _(pe):
            def transposes(src, n, dst_banks=bank):
                for tt in range(T):
                    pe.wait_ge(sem("y_ready"), n * T + tt + 1)
                    if tt >= 2:
                        pe.wait_ge(sem("yT_ready"), n * T + tt - 1)
                    for cc in range(C):
                        last = nc.tensor.transpose(dst_banks[tt % 2][:, cc * P:(cc + 1) * P],
                                                   src(tt, cc), ident[:])
                    last.then_inc(sem("y_turned"), 1)

            def tile_of(buf):
                return lambda tt, cc: buf[:, tt, cc * P:(cc + 1) * P]

            def channels_out(dst, wT, col, srcT, tok, n, k=C):
                for ic in range(k):
                    last = nc.tensor.matmul(dst, wT[:, ic, col:col + P], srcT[:, ic, tok:tok + n],
                                            start=(ic == 0), stop=(ic == k - 1))
                return last

            def tokens_out(dst, srcT, tt, wT, lo, n, bias=None, k=C):
                for ic in range(k):
                    last = nc.tensor.matmul(dst, srcT[:, ic, tt * P:(tt + 1) * P], wT[:, ic, lo:lo + n],
                                            start=(ic == 0), stop=(ic == k - 1 and bias is None))
                if bias is not None:
                    last = nc.tensor.matmul(dst, ones[0:1, 0:P], bias, start=False, stop=True)
                return last

            pe.wait_ge(sem("const_loaded"), 16 * 19)
            pe.wait_ge(sem("ones_set"), 1)
            transposes(tile_of(y), 0)
            pe.wait_ge(sem("w_A"), 64)
            pe.wait_ge(sem("yT_ready"), T)
            for g in range(C * B):
                cc, bb = g // B, g % B
                if g >= 2:
                    pe.wait_ge(sem("a_qT"), g - 1)
                channels_out(half(0, g % 2), w["qkvT"], cc * P, yT, bb * S, S).then_inc(sem("a_q_ps"), 1)
            for tt in range(T):
                if tt >= 2:
                    pe.wait_ge(sem("a_kv"), tt - 1)
                tokens_out(half(1, tt % 2), yT, tt, w["qkvT"], D, 2 * D).then_inc(sem("a_kv_ps"), 1)
            pe.wait_ge(sem("a_vones"), 1)
            pe.wait_ge(sem("a_kv"), T)
            for bb in range(B):
                for cc in range(C):
                    for j in range(TB):
                        tt = bb * TB + j
                        last = nc.tensor.matmul(half(2, bb)[:, cc * KV:cc * KV + P + 1],
                                                a_k[:, tt, cc * P:(cc + 1) * P], a_v[:, tt, cc, :],
                                                start=(j == 0), stop=(j == TB - 1))
                last.then_inc(sem("a_kvsum_ps"), 1)
            pe.wait_ge(sem("w_abs"), 1)
            nc.tensor.matmul(half(0, 0)[:, 0:3], ones[:], w_abs[:], start=True, stop=True).then_inc(sem("w_abs_ps"), 1)
            for tt in range(T):
                pe.wait_ge(sem("a_kvsum"), tt // TB + 1)
                if tt >= 2:
                    pe.wait_ge(sem("y_ready"), 1 * T + tt - 1)
                for cc in range(C):
                    last = nc.tensor.matmul(bank[tt % 2][:, cc * KV:(cc + 1) * KV],
                                            a_qT[:, cc, tt * P:(tt + 1) * P], a_kv[:, tt // TB, cc, :],
                                            start=True, stop=True)
                last.then_inc(sem("a_at_ps"), 1)
            pe.wait_ge(sem("y_ready"), 2 * T)
            transposes(tile_of(y), 1)
            for tt in range(T):
                pe.wait_ge(sem("yT_ready"), 1 * T + tt + 1)
                if tt < 2:
                    pe.wait_ge(sem("w_mean"), 1)
                else:
                    pe.wait_ge(sem("a_x1"), tt - 1)
                tokens_out(half(0, tt % 2)[:, 0:D], yT, tt, w["projT"], 0, D, rows["proj_b"][:]).then_inc(sem("a_proj_ps"), 1)
            transposes(tile_of(y), 2)
            pe.wait_ge(sem("yT_ready"), 3 * T)
            for g in range(MC * B):
                m, bb = g // B, g % B
                if g >= 2:
                    pe.wait_ge(sem("a_hT"), g - 1)
                channels_out(half(1, g % 2), w["conv1T"], m * P, yT, bb * S, S).then_inc(sem("a_h_ps"), 1)
            pe.wait_ge(sem("a_hT"), MC * B)
            for tt in range(T):
                if tt >= 2:
                    pe.wait_ge(sem("a_added"), tt - 1)
                tokens_out(half(2, tt % 2)[:, 0:D], a_hT, tt, conv2T, 0, D, rows["conv2_b"][:], k=MC).then_inc(sem("a_mlp_ps"), 1)

            transposes(tile_of(y), 3)
            pe.wait_ge(sem("w_B"), 64)
            pe.wait_ge(sem("yT_ready"), 4 * T)
            for g in range(C * B):
                cc, bb = g // B, g % B
                if g >= 2:
                    pe.wait_ge(sem("b_q_proj"), g - 1)
                channels_out(half(0, g % 2), w["xqT"], cc * P, yT, bb * S, S).then_inc(sem("b_q_ps"), 1)
            for g in range(C * B * 2):
                cc, bb, hh = g // (2 * B), g // 2 % B, g % 2
                if g >= 2:
                    pe.wait_ge(sem("b_k_proj"), g - 1)
                channels_out(half(1, g % 2), w["xkT"], cc * P, ctxT, bb * SC + 512 * hh, 512).then_inc(sem("b_k_ps"), 1)
            pe.wait_ge(sem("b_k_proj"), C * B * 2)

            def b_scores(i, j):
                u, qt = j // 2 % 2, 2 * (j % 2)
                if qt == 0:
                    pe.wait_ge(sem(f"b_head{u}_loaded"), i * 32 + (32 + 32 * (j // 4)))
                for k in range(2):
                    wait(pe, "b_s_copied", i * 8 + (2 * j + k - 1))
                    for hh in range(2):
                        last = nc.tensor.matmul(wide[k][:, 512 * hh:512 * hh + 512],
                                                b_q[0:DH, u, (qt + k) * P:(qt + k + 1) * P],
                                                b_k[0:DH, u, 512 * hh:512 * hh + 512], start=True, stop=True)
                    last.then_inc(sem("b_scores"), 1)

            def b_attend(i, j):
                for k in range(2):
                    n = 2 * j + k
                    pe.wait_ge(sem("b_final"), i * 8 + (n + 1))
                    for hh in range(2):
                        wait(pe, "b_pT", i * 16 + (2 * n - 1 + hh))
                        for kt in range(CTB // 2 * hh, CTB // 2 * (hh + 1)):
                            dst = wide[2][:, kt * P:(kt + 1) * P]
                            nc.tensor.matmul(dst, b_e[:, n % 4, kt * P:(kt + 1) * P], ident[:], start=True, stop=False)
                            last = nc.tensor.matmul(dst, b_z[:, n % 4, kt * P:(kt + 1) * P], negident[:],
                                                    start=False, stop=True)
                        last.then_inc(sem("b_tr"), 1)
                wait(pe, "b_out", i * 4 + (j - 1))
                for k in range(2):
                    n = 2 * j + k
                    for kt in range(CTB):
                        if kt % (CTB // 2) == 0:
                            pe.wait_ge(sem("b_pT"), i * 16 + (2 * n + kt // (CTB // 2) + 1))
                        last = nc.tensor.matmul(bank[j % 2][:, k * V1:(k + 1) * V1], b_pT[:, k, kt * P:(kt + 1) * P],
                                                vB[:, bass.ds((i * 2 + j // 2) * (CTB * V1) + kt * V1, V1)],
                                                start=(kt == 0), stop=(kt == CTB - 1))
                last.then_inc(sem("b_o_ps"), 1)

            def b_slots(i, first=False, last=False):
                for j in range(4):
                    if not (last and j == 3):
                        b_scores(i, j + 1)
                    if not (first and j == 0):
                        if j == 0:
                            b_attend(i - 1, 3)
                        else:
                            b_attend(i, j - 1)

            b_scores(0, 0)
            b_slots(0, first=True)
            with pe.Fori(1, PAIRS // 4 - 1) as i:
                b_slots(i)
            b_slots(PAIRS // 4 - 1, last=True)
            b_attend(PAIRS // 4 - 1, 3)
            pe.wait_ge(sem("b_bad"), 1)
            pe.wait_ge(sem("b_out"), PAIRS)
            nc.tensor.matmul(bank[0][:, 0:2], ones[:], b_bad, start=True, stop=True).then_inc(sem("b_bad_ps"), 1)
            pe.wait_ge(sem("b_flag"), 1)
            with pe.If(pe.value_load(b_flag[0:1, 0:1], min_val=0, max_val=2 * P) > 0):
                with pe.Fori(0, B * H // 2) as i:
                    def scores(j):
                        u, qt = j // TB, j % TB
                        if qt == 0:
                            pe.wait_ge(sem(f"g_head{u}_loaded"), i * 32 + 32)
                        if j >= 2:
                            pe.wait_ge(sem("g_s_copied"), i * 8 + (j - 1))
                        for hh in range(2):
                            last = nc.tensor.matmul(wide[j % 2][:, 512 * hh:512 * hh + 512],
                                                    b_q[0:DH, u, qt * P:(qt + 1) * P],
                                                    b_k[0:DH, u, 512 * hh:512 * hh + 512], start=True, stop=True)
                        last.then_inc(sem("g_scores"), 1)

                    def weights_out(j):
                        u = j // TB
                        pe.wait_ge(sem("g_probs"), i * 8 + (j + 1))
                        if j >= 1:
                            pe.wait_ge(sem("g_pT"), i * 8 + j)
                        for kt in range(CTB):
                            last = nc.tensor.transpose(wide[2][:, kt * P:(kt + 1) * P],
                                                       b_s[:, 2:4][:, j % 2, kt * P:(kt + 1) * P], ident[:])
                        last.then_inc(sem("g_p_tr"), 1)
                        pe.wait_ge(sem("g_pT"), i * 8 + (j + 1))
                        if j >= 1:
                            pe.wait_ge(sem("g_o"), i * 8 + j)
                        for kt in range(CTB):
                            last = nc.tensor.matmul(bank[0][:, 0:DH], b_pT[:, j % 2, kt * P:(kt + 1) * P],
                                                    vB[:, bass.ds((i * 2 + u) * (CTB * V1) + kt * V1, DH)],
                                                    start=(kt == 0), stop=(kt == CTB - 1))
                        last.then_inc(sem("g_o_ps"), 1)

                    for j in range(2 * TB):
                        scores(j)
                        if j >= 1:
                            weights_out(j - 1)
                    weights_out(2 * TB - 1)
                    pe.wait_ge(sem("g_o"), i * 8 + 8)

            for tt in range(T):
                pe.wait_ge(sem("c_xq"), tt + 1)
                if tt >= 2:
                    pe.wait_ge(sem("c_xqT"), tt - 1)
                for cc in range(C):
                    last = nc.tensor.transpose(bank[tt % 2][:, 0:P].bitcast(BF16)[:, cc * P:(cc + 1) * P],
                                               c_qb[:, tt % 2, cc * P:(cc + 1) * P], ident_bf[:])
                last.then_inc(sem("c_xq_tr"), 1)
            pe.wait_ge(sem("w_rounded"), 3)
            pe.wait_ge(sem("c_xqT"), T)
            for tt in range(T):
                for n, (dst, wq) in enumerate(((wide[0], wq_gate), (wide[1], wq_up))):
                    if tt >= 1:
                        pe.wait_ge(sem(("c_g", "c_h")[n]), tt)
                    for hh in range(2):
                        for ic in range(C):
                            last = nc.tensor.matmul(dst[:, 512 * hh:512 * hh + 512], c_qT[:, ic, tt * P:(tt + 1) * P],
                                                    wq[:, ic, 512 * hh:512 * hh + 512],
                                                    start=(ic == 0), stop=(ic == C - 1))
                    last.then_inc(sem(("c_g_ps", "c_u_ps")[n]), 1)
                pe.wait_ge(sem("c_hq"), tt + 1)
                if tt >= 2:
                    pe.wait_ge(sem("c_hT"), tt - 1)
                for kt in range(KC):
                    last = nc.tensor.transpose(half(2, tt % 2).bitcast(BF16)[:, kt * P:(kt + 1) * P],
                                               c_hb[:, tt % 2, kt * P:(kt + 1) * P], ident_bf[:])
                last.then_inc(sem("c_h_tr"), 1)
                pe.wait_ge(sem("c_hT"), tt + 1)
                if tt >= 2:
                    pe.wait_ge(sem("c_added"), tt - 1)
                for kt in range(KC):
                    last = nc.tensor.matmul(bank[tt % 2][:, 0:D], c_hT[:, tt % 2, kt], wq_down[:, kt, :],
                                            start=(kt == 0), stop=(kt == KC - 1))
                last.then_inc(sem("c_d_ps"), 1)

            transposes(tile_of(y), 4)
            pe.wait_ge(sem("w_DEF"), 16 * 8)
            pe.wait_ge(sem("yT_ready"), 5 * T)
            for g in range(C * B):
                cc, bb = g // B, g % B
                for n, wn in enumerate(("aqT", "akT")):
                    if g >= 1:
                        pe.wait_ge(sem(("d_q_proj", "d_k_proj")[n]), g)
                    channels_out(half(0, n), w[wn], cc * P, yT, bb * S, S).then_inc(sem(("d_q_ps", "d_k_ps")[n]), 1)
            for tt in range(T):
                if tt >= 2:
                    pe.wait_ge(sem("d_v"), tt - 1)
                tokens_out(half(1, tt % 2)[:, 0:D], yT, tt, w["avT"], 0, D, rows["av_b"][:]).then_inc(sem("d_v_ps"), 1)
            pe.wait_ge(sem("d_v"), T)
            pe.wait_ge(sem("d_vones"), 1)
            def d_scores(i, j):
                u = j % 2
                pe.wait_ge(sem(f"d_head{u}_loaded"), i * 48 + (64 + 48 * (j // 2)))
                for qt in range(TB):
                    n = (qt + 1) * P
                    wait(pe, "d_s", i * 8 + (TB * (j - 1) + qt + 1))
                    nc.tensor.matmul(half(qt // 2, qt % 2)[:, 0:n], d_q[0:AUG, u, qt * P:(qt + 1) * P],
                                     d_k[0:AUG, u, 0:n], start=True, stop=True).then_inc(sem("d_scores"), 1)

            def d_attend(i, j):
                def times_values(qt):
                    pe.wait_ge(sem("d_pT"), i * 8 + (TB * j + qt + 1))
                    for kt in range(qt + 1):
                        last = nc.tensor.matmul(bank[j % 2][:, qt * V1:(qt + 1) * V1], d_pT[:, qt % 2, kt * P:(kt + 1) * P],
                                                d_v[:, bass.ds((i * 2 + j) * (TB * V1) + kt * V1, V1)],
                                                start=(kt == 0), stop=(kt == qt))
                    return last

                wait(pe, "d_o", i * 2 + (j - 1))
                for qt in range(TB):
                    pe.wait_ge(sem("d_p"), i * 8 + (TB * j + qt + 1))
                    wait(pe, "d_pT", i * 8 + (TB * j + qt - 1))
                    for kt in range(qt + 1):
                        last = nc.tensor.transpose(half(2, qt % 2)[:, kt * P:(kt + 1) * P],
                                                   d_p[:, j % 2, qt, kt * P:(kt + 1) * P], ident[:])
                    last.then_inc(sem("d_p_tr"), 1)
                    if qt >= 1:
                        times_values(qt - 1).then_inc(sem("d_pv"), 1)
                last = times_values(TB - 1)
                last.then_inc(sem("d_o_ps"), 1)

            def d_slots(i, last=False):
                for j in range(2):
                    if not (last and j == 1):
                        d_scores(i, j + 1)
                    d_attend(i, j)

            d_scores(0, 0)
            d_slots(0)
            with pe.Fori(1, B * H // 2 - 1) as i:
                d_slots(i)
            d_slots(B * H // 2 - 1, last=True)
            transposes(tile_of(y), 5)
            for tt in range(T):
                pe.wait_ge(sem("yT_ready"), 5 * T + tt + 1)
                if tt >= 2:
                    pe.wait_ge(sem("d_added"), tt - 1)
                tokens_out(half(2, tt % 2)[:, 0:D], yT, tt, w["aoT"], 0, D, rows["ao_b"][:]).then_inc(sem("d_out_ps"), 1)

            pe.wait_ge(sem("d_added"), T)
            for tt in range(CT):
                if tt >= 2:
                    pe.wait_ge(sem("e_kv"), tt - 1)
                tokens_out(half(0, tt % 2), ctxT, tt, w["lkvT"], 0, 2 * D, rows["lkv_b"][:]).then_inc(sem("e_kv_ps"), 1)
            pe.wait_ge(sem("e_kv"), CT)
            for bb in range(B):
                for cc in range(C):
                    for j in range(CTB):
                        tt = bb * CTB + j
                        last = nc.tensor.matmul(half(1, bb)[:, cc * P:(cc + 1) * P],
                                                e_k[:, tt, cc * P:(cc + 1) * P], e_v[:, tt, cc * P:(cc + 1) * P],
                                                start=(j == 0), stop=(j == CTB - 1))
                last.then_inc(sem("e_sum_ps"), 1)
            for tt in range(CT):
                pe.wait_ge(sem("e_kk"), tt + 1)
                for cc in range(C):
                    bb = tt // CTB
                    last = nc.tensor.matmul(half(2, cc)[:, bb:bb + 1],
                                            e_kk[:, tt % 2, cc * P:(cc + 1) * P], ones[:, 0:1],
                                            start=(tt % CTB == 0), stop=(tt % CTB == CTB - 1))
                last.then_inc(sem("e_kk_summed"), 1)
            transposes(tile_of(y), 6)
            pe.wait_ge(sem("yT_ready"), 7 * T)
            for g in range(C * B):
                cc, bb = g // B, g % B
                if g >= 2:
                    pe.wait_ge(sem("e_qelu"), g - 1)
                channels_out(half(0, g % 2), w["lqT"], cc * P, yT, bb * S, S).then_inc(sem("e_q_ps"), 1)
            pe.wait_ge(sem("e_qT"), C * B)
            pe.wait_ge(sem("e_sum"), B)
            for tt in range(T):
                if tt >= 2:
                    pe.wait_ge(sem("y_ready"), 7 * T + tt - 1)
                for cc in range(C):
                    nc.tensor.matmul(half(1, tt % 2)[:, cc * P:(cc + 1) * P], e_qT[:, cc, tt * P:(tt + 1) * P],
                                     e_kv[:, tt // TB, cc, :], start=True, stop=True)
                for cc in range(C):
                    last = nc.tensor.matmul(half(1, tt % 2)[:, D + cc * HC:D + (cc + 1) * HC],
                                            e_qq[:, cc, tt * P:(tt + 1) * P], headmask[:], start=True, stop=True)
                last.then_inc(sem("e_at_ps"), 1)
            transposes(tile_of(y), 7)
            for tt in range(T):
                pe.wait_ge(sem("yT_ready"), 7 * T + tt + 1)
                if tt >= 2:
                    pe.wait_ge(sem("e_added"), tt - 1)
                tokens_out(half(2, tt % 2)[:, 0:D], yT, tt, w["loT"], 0, D, rows["lo_b"][:]).then_inc(sem("e_out_ps"), 1)

            transposes(tile_of(y), 8)
            pe.wait_ge(sem("f_moments"), 1)
            n_terms = [(f_m2, f_iv), (f_m1s, f_mi)]
            for k_, (m, tab) in enumerate(n_terms):
                for cc in range(C):
                    nc.tensor.matmul(half(0, 0)[0:B, 0:E], m[:, cc, :], tab[:, cc, :],
                                     start=(k_ == 0 and cc == 0), stop=False)
            for cc in range(C):
                last = nc.tensor.matmul(half(0, 0)[0:B, 0:E], ones[:, 0:B], f_m2i[:, cc, :],
                                        start=False, stop=(cc == C - 1))
            last.then_inc(sem("f_loss_ps"), 1)
            pe.wait_ge(sem("f_expert_loaded"), 16 * 6 * B)
            for bb in range(B):
                for ic in range(C):
                    last = nc.tensor.matmul(half(1, bb)[0:R, :], f_down[:, bb, ic, :], yT[:, ic, bb * S:(bb + 1) * S],
                                            start=(ic == 0), stop=(ic == C - 1))
                last.then_inc(sem("f_h_ps"), 1)
            for bb in range(B):
                pe.wait_ge(sem("f_hT"), bb + 1)
                for cc in range(C):
                    g = bb * C + cc
                    if g >= 2:
                        pe.wait_ge(sem("f_aT"), g - 1)
                    nc.tensor.matmul(half(2, g % 2), f_up[0:R, bb, cc * P:(cc + 1) * P], f_hT[0:R, bb * S:(bb + 1) * S],
                                     start=True, stop=True).then_inc(sem("f_a_ps"), 1)
            for tt in range(T):
                bb = tt // TB
                pe.wait_ge(sem("f_aT"), C * (bb + 1))
                if tt >= 2:
                    pe.wait_ge(sem("f_added"), tt - 1)
                dst = bank[tt % 2][:, 0:D]
                for ic in range(C):
                    nc.tensor.matmul(dst, yT[:, ic, tt * P:(tt + 1) * P], w["baseT"][:, ic, :], start=(ic == 0), stop=False)
                for ic in range(C):
                    nc.tensor.matmul(dst, f_aT[:, ic, tt * P:(tt + 1) * P], f_conv[:, bb, ic, :], start=False, stop=False)
                nc.tensor.matmul(dst, ones[0:1, 0:P], rows["base_b"][:], start=False, stop=False)
                nc.tensor.matmul(dst, ones[0:1, 0:P], f_cb[0:1, bb, :], start=False, stop=True).then_inc(sem("f_out_ps"), 1)

        @block.scalar
        def _(act):
            def roots(n):
                act.wait_ge(sem("ln_var"), n)
                nc.scalar.activation(sd[:], var[:], ACT.Sqrt).then_inc(sem("ln_sd"), 1)

            def copy_T(n, scales=None):
                for tt in range(T):
                    act.wait_ge(sem("y_turned"), n * T + tt + 1)
                    if scales is None:
                        nc.scalar.activation(yT[:, :, tt * P:(tt + 1) * P],
                                             bank[tt % 2][:, 0:D].rearrange("p (c n) -> p c n", c=C),
                                             ACT.Copy).then_inc(sem("yT_ready"), 1)
                    else:
                        nc.scalar.activation(yT[:, 0, tt * P:(tt + 1) * P], bank[tt % 2][:, 0:P], ACT.Copy,
                                             scale=cols[scales][:, 0:1])
                        nc.scalar.activation(yT[:, 1, tt * P:(tt + 1) * P], bank[tt % 2][:, P:D], ACT.Copy,
                                             scale=cols[scales][:, 1:2]).then_inc(sem("yT_ready"), 1)

            act.wait_ge(sem("const_loaded"), 16 * 19)
            roots(1)
            for tt in range(T):
                act.wait_ge(sem("a_ln"), tt + 1)
                if tt >= 2:
                    act.wait_ge(sem("act_sq"), tt - 1)
                nc.scalar.activation(sq[:, tt % 2, 0:D], xin[:, tt, :], ACT.Square,
                                     accum_out=var[:, tt:tt + 1]).then_inc(sem("act_sq"), 1)
            act.wait_ge(sem("act_sq"), T)
            nc.scalar.activation(sd[:], var[:], ACT.Sqrt).then_inc(sem("a_norm"), 1)
            copy_T(0, "scale1")
            for g in range(C * B):
                cc, bb = g // B, g % B
                act.wait_ge(sem("a_q_ps"), g + 1)
                nc.scalar.activation(sq[:, g % 2, :], half(0, g % 2), ACT.Square).then_inc(sem("act_sq"), 1)
                act.wait_ge(sem("act_sq"), T + g + 1)
                nc.scalar.activation(a_qT[:, cc, bb * S:(bb + 1) * S], sq[:, g % 2, :], ACT.Exp,
                                     scale=-0.5).then_inc(sem("a_qT"), 1)
            for tt in range(T):
                act.wait_ge(sem("a_kv_ps"), tt + 1)
                if tt < 2:
                    act.wait_ge(sem("a_qT"), C * B)
                nc.scalar.activation(sq[:, tt % 2, 0:D], half(1, tt % 2)[:, 0:D], ACT.Square).then_inc(sem("act_sq"), 1)
                nc.scalar.activation(a_v[:, tt, :, 0:P], half(1, tt % 2)[:, D:2 * D].rearrange("p (c n) -> p c n", c=C),
                                     ACT.Copy)
                act.wait_ge(sem("act_sq"), T + C * B + tt + 1)
                nc.scalar.activation(a_k[:, tt, :], sq[:, tt % 2, 0:D], ACT.Exp, scale=-0.5).then_inc(sem("a_kv"), 1)
            copy_T(1)
            for tt in range(T):
                act.wait_ge(sem("a_x1"), tt + 1)
                act.wait_ge(sem("a_kv"), T)
                if tt >= 2:
                    act.wait_ge(sem("act_sq"), 2 * T + C * B + tt - 1)
                nc.scalar.activation(sq[:, tt % 2, 0:D], a_x1[:, tt, :], ACT.Square,
                                     accum_out=var[:, tt:tt + 1]).then_inc(sem("act_sq"), 1)
            act.wait_ge(sem("act_sq"), 3 * T + C * B)
            nc.scalar.activation(sd[:], var[:], ACT.Sqrt).then_inc(sem("a_norm"), 1)
            copy_T(2, "scale2")
            for g in range(MC * B):
                m, bb = g // B, g % B
                act.wait_ge(sem("a_h_ps"), g + 1)
                nc.scalar.activation(a_hT[:, m, bb * S:(bb + 1) * S], half(1, g % 2), ACT.Gelu,
                                     bias=cols["conv1_b"][:, m:m + 1]).then_inc(sem("a_hT"), 1)

            act.wait_ge(sem("w_rounded"), 3)
            roots(2)
            copy_T(3)
            for g in range(C * B):
                act.wait_ge(sem("b_q_ps"), g + 1)
                if g >= 2:
                    act.wait_ge(sem(f"b_q_stored{g % 2}"), 16 * (g // 2))
                nc.scalar.activation(b_proj[:, g % 2, :], half(0, g % 2), ACT.Copy, scale=DH ** -0.5).then_inc(sem("b_q_proj"), 1)
            for g in range(2):
                act.wait_ge(sem(f"b_q_stored{g}"), 16 * C * B // 2)
            for g in range(C * B * 2):
                act.wait_ge(sem("b_k_ps"), g + 1)
                if g >= 2:
                    act.wait_ge(sem(f"b_k_stored{g % 2}"), 16 * (g // 2))
                nc.scalar.activation(b_proj[:, g % 2, :], half(1, g % 2), ACT.Copy).then_inc(sem("b_k_proj"), 1)

            def b_copy(i, j):
                for k in range(2):
                    act.wait_ge(sem("b_scores"), i * 8 + (2 * j + k + 1))
                    nc.scalar.activation(b_s[:, (2 * j + k) % 4, :], wide[k][:], ACT.Copy).then_inc(sem("b_s_copied"), 1)

            def b_exp(i, j):
                act.wait_ge(sem("b_cand"), i * 4 + (j + 1))
                for k in range(2):
                    n = (2 * j + k) % 4
                    wait(act, "b_tr", i * 16 + 2 * (2 * j + k - 3))
                    nc.scalar.activation(b_e[:, n, :], b_s[:, n, :], ACT.Exp, bias=b_neg[:, k:k + 1],
                                         accum_out=b_all[:, j, k:k + 1]).then_inc(sem("b_exp"), 1)

            def b_threshold(i, j):
                act.wait_ge(sem("b_thr"), i * 8 + (2 * j + 2))
                for k in range(2):
                    ins = nc.scalar.activation(b_te[:, k:k + 1], b_m8[:, k, 7:8], ACT.Exp, bias=b_neg[:, k:k + 1])
                ins.then_inc(sem("b_te"), 1)

            def b_weights(i, j):
                for k in range(2):
                    n = 2 * j + k
                    for hh in range(2):
                        act.wait_ge(sem("b_tr"), i * 16 + (2 * n + hh + 1))
                        if k == 0 and hh == 0:
                            wait(act, "b_o_ps", i * 4 + j)
                        nc.scalar.activation(b_pT[:, k, 512 * hh:512 * hh + 512], half(2, hh), ACT.Copy).then_inc(sem("b_pT"), 1)

            def b_counts(i, j):
                for k in range(2):
                    act.wait_ge(sem("b_mask"), i * 8 + (2 * j + k + 1))
                    nc.scalar.activation(b_junk[:, k, :], b_m[:, k, :], ACT.Copy, accum_out=b_cnt[:, k:k + 1]).then_inc(sem("b_count"), 1)

            def b_slots(i, first=False, last=False):
                for j in range(4):
                    b_exp(i, j)
                    if not (last and j == 3):
                        b_copy(i, j + 1)
                    b_threshold(i, j)
                    if not (first and j == 0):
                        if j == 0:
                            b_weights(i - 1, 3)
                        else:
                            b_weights(i, j - 1)
                    b_counts(i, j)

            b_copy(0, 0)
            b_slots(0, first=True)
            with act.Fori(1, PAIRS // 4 - 1) as i:
                b_slots(i)
            b_slots(PAIRS // 4 - 1, last=True)
            b_weights(PAIRS // 4 - 1, 3)
            act.wait_ge(sem("b_flag"), 1)
            with act.If(act.value_load(b_flag[0:1, 0:1], min_val=0, max_val=2 * P) > 0):
                with act.Fori(0, B * H // 2) as i:
                    for j in range(2 * TB):
                        act.wait_ge(sem("g_scores"), i * 8 + (j + 1))
                        if j >= 2:
                            act.wait_ge(sem("g_exp"), i * 8 + (j - 1))
                            act.wait_ge(sem("g_probs"), i * 8 + (j - 1))
                        nc.scalar.activation(b_s[:, j % 2, :], wide[j % 2][:], ACT.Copy).then_inc(sem("g_s_copied"), 1)
                        act.wait_ge(sem("g_neg"), i * 8 + (j + 1))
                        nc.scalar.activation(b_e[:, j % 2, :], b_s[:, j % 2, :], ACT.Exp, bias=g_neg[:, j % 2, :],
                                             accum_out=g_all[:, j % 2, :]).then_inc(sem("g_exp"), 1)
                        if j >= 1:
                            act.wait_ge(sem("g_p_tr"), i * 8 + j)
                            if j >= 3:
                                act.wait_ge(sem("g_o_ps"), i * 8 + (j - 2))
                            nc.scalar.activation(b_pT[:, (j - 1) % 2, :], wide[2][:], ACT.Copy).then_inc(sem("g_pT"), 1)
                    act.wait_ge(sem("g_p_tr"), i * 8 + 8)
                    act.wait_ge(sem("g_o_ps"), i * 8 + 6)
                    nc.scalar.activation(b_pT[:, 1, :], wide[2][:], ACT.Copy).then_inc(sem("g_pT"), 1)
                    act.wait_ge(sem("g_o"), i * 8 + 8)

            roots(3)
            for tt in range(T):
                act.wait_ge(sem("c_g_ps"), tt + 1)
                if tt >= 2:
                    act.wait_ge(sem("c_h"), tt - 1)
                nc.scalar.activation(c_g[:, tt % 2, :], wide[0][:], ACT.Silu, scale=c_ag[:, tt:tt + 1]).then_inc(sem("c_g"), 1)

            roots(4)
            copy_T(4)
            for g in range(C * B):
                cc = g // B
                act.wait_ge(sem("d_k_ps"), g + 1)
                if g >= 1:
                    act.wait_ge(sem("d_k_stored"), 16 * g)
                nc.scalar.activation(d_proj[:, 1, :], half(0, 1), ACT.Identity, bias=cols["ak_b"][:, cc:cc + 1]).then_inc(sem("d_k_proj"), 1)
            def d_exp(i, j, qt):
                n = (qt + 1) * P
                if qt == 0:
                    act.wait_ge(sem("d_neg"), i * 2 + (j + 1))
                wait(act, "d_p_tr", i * 8 + (TB * (j - 2) + qt + 1))
                nc.scalar.activation(d_p[:, j % 2, qt, 0:n], d_s[:, j % 2, qt, 0:n], ACT.Exp,
                                     bias=d_neg[:, j % 2, qt:qt + 1]).then_inc(sem("d_p"), 1)

            def d_weights(i, j, qt):
                n = (qt + 1) * P
                act.wait_ge(sem("d_p_tr"), i * 8 + (TB * j + qt + 1))
                if qt < 2:
                    wait(act, "d_o_ps", i * 2 + j)
                else:
                    act.wait_ge(sem("d_pv"), i * 6 + (3 * j + qt - 1))
                nc.scalar.activation(d_pT[:, qt % 2, 0:n], half(2, qt % 2)[:, 0:n], ACT.Copy).then_inc(sem("d_pT"), 1)

            def d_slots(i, last=False):
                for j in range(2):
                    for qt in range(TB):
                        d_weights(i, j, qt)
                        if not (last and j == 1):
                            d_exp(i, j + 1, qt)

            for qt in range(TB):
                d_exp(0, 0, qt)
            d_slots(0)
            with act.Fori(1, B * H // 2 - 1) as i:
                d_slots(i)
            d_slots(B * H // 2 - 1, last=True)
            copy_T(5)

            for tt in range(CT):
                act.wait_ge(sem("e_kmin"), tt + 1)
                nc.scalar.activation(e_t[:, tt % 2, D:2 * D], e_t[:, tt % 2, 0:D], ACT.Exp).then_inc(sem("e_kexp"), 1)
            for tt in range(CT):
                act.wait_ge(sem("e_kv"), tt + 1)
                if tt >= 2:
                    act.wait_ge(sem("e_kk_summed"), tt - 1)
                nc.scalar.activation(e_kk[:, tt % 2, :], e_k[:, tt, :], ACT.Square).then_inc(sem("e_kk"), 1)
            act.wait_ge(sem("e_kk_summed"), CT)
            for cc in range(C):
                nc.scalar.activation(e_kn[:, cc * B:(cc + 1) * B], half(2, cc)[:, 0:B], ACT.Sqrt,
                                     scale=float(S)).then_inc(sem("e_kn"), 1)
            roots(5)
            copy_T(6)
            for g in range(C * B):
                cc, bb = g // B, g % B
                act.wait_ge(sem("e_qmin"), g + 1)
                nc.scalar.activation(e_qq[:, cc, bb * S:(bb + 1) * S], sq[:, g % 2, :], ACT.Exp).then_inc(sem("e_qexp"), 1)
            for g in range(C * B):
                cc, bb = g // B, g % B
                act.wait_ge(sem("e_qelu"), g + 1)
                nc.scalar.activation(e_qq[:, cc, bb * S:(bb + 1) * S], e_qT[:, cc, bb * S:(bb + 1) * S],
                                     ACT.Square).then_inc(sem("e_qT"), 1)
            for tt in range(T):
                act.wait_ge(sem("e_at_ps"), tt + 1)
                if tt >= 2:
                    act.wait_ge(sem("y_ready"), 7 * T + tt - 1)
                nc.scalar.activation(e_qn[:, tt % 2], half(1, tt % 2)[:, D:D + H].rearrange("p (c h) -> p c h", c=C),
                                     ACT.Sqrt, scale=float(DH)).then_inc(sem("e_qn"), 1)
            copy_T(7)

            roots(6)
            copy_T(8)
            for bb in range(B):
                act.wait_ge(sem("f_h_ps"), bb + 1)
                nc.scalar.activation(f_hT[0:R, bb * S:(bb + 1) * S], half(1, bb)[0:R, :], ACT.Relu,
                                     bias=f_db[0:R, bb:bb + 1]).then_inc(sem("f_hT"), 1)
            for g in range(C * B):
                bb, cc = g // C, g % C
                act.wait_ge(sem("f_a_ps"), g + 1)
                nc.scalar.activation(f_aT[:, cc, bb * S:(bb + 1) * S], half(2, g % 2), ACT.Identity,
                                     bias=f_ub[:, bb, cc:cc + 1]).then_inc(sem("f_aT"), 1)

        @block.gpsimd
        def _(pool):
            pool.wait_ge(sem("w_mean"), 1)
            for n in range(3):
                nc.gpsimd.tensor_scalar(w_raw[n], w_raw[n], w_scale[:, n:n + 1], 1.0, ALU.mult, ALU.mult).then_inc(sem("pool_step"), 1)
                pool.wait_ge(sem("pool_step"), 2 * n + 1)
                nc.gpsimd.tensor_scalar(w_raw[n], w_raw[n], ROUND, 1.0, ALU.add, ALU.mult).then_inc(sem("pool_step"), 1)
                pool.wait_ge(sem("pool_step"), 2 * n + 2)
                nc.gpsimd.tensor_scalar(w_raw[n], w_raw[n], -ROUND, 1.0, ALU.add, ALU.mult).then_inc(sem("w_whole"), 1)

            def b_rest(i, j):
                for k in range(2):
                    n = (2 * j + k) % 4
                    wait(pool, "b_tr", i * 16 + 2 * (2 * j + k - 3))
                    pool.wait_ge(sem("b_mask"), i * 8 + (2 * j + k + 1))
                    nc.gpsimd.tensor_tensor(b_z[:, n, :], b_e[:, n, :], b_m[:, k, :], ALU.mult).then_inc(sem("b_z"), 1)

            for j in range(4):
                b_rest(0, j)
            with pool.Fori(1, PAIRS // 4) as i:
                for j in range(4):
                    b_rest(i, j)

        @block.vector
        def _(dve):
            steps = [0]

            def link(ins):
                steps[0] += 1
                ins.then_inc(sem("dve_step"), 1)
                dve.wait_ge(sem("dve_step"), steps[0])

            def gate(k=0):
                nc.vector.tensor_copy(gate_out[:, k:k + 1], w_abs[:, 0:1])

            def layer_norm(n, dst, done):
                for tt in range(T):
                    ins = nc.vector.bn_stats(bn[:, tt, :], x[:, tt, :])
                link(ins)
                for tt in range(T):
                    ins = nc.vector.bn_aggr(mv[:, tt, :], bn[:, tt, :])
                link(ins)
                nc.vector.tensor_scalar(var[:], mv[:, :, 1], LN_EPS, None, ALU.add).then_inc(sem("ln_var"), 1)
                dve.wait_ge(sem("ln_sd"), n)
                link(nc.vector.reciprocal(rstd[:], sd[:]))
                for tt in range(T):
                    nc.vector.tensor_scalar(dst[:, tt, :], x[:, tt, :], mv[:, tt, 0:1], rstd[:, tt:tt + 1],
                                            ALU.subtract, ALU.mult).then_inc(sem(done), 1)

            def rms_scale(src, n):
                dve.wait_ge(sem("a_norm"), n)
                link(nc.vector.reciprocal(rstd[:], sd[:]))
                link(nc.vector.tensor_scalar(rstd[:], rstd[:], RMS_GAIN, None, ALU.mult))
                for tt in range(T):
                    nc.vector.tensor_scalar(y[:, tt, :], src[:, tt, :], rstd[:, tt:tt + 1], None,
                                            ALU.mult).then_inc(sem("y_ready"), 1)

            nc.vector.memset(ones[:], 1.0).then_inc(sem("ones_set"), 1)
            nc.vector.memset(a_v[:, :, :, P:P + 1], 1.0).then_inc(sem("a_vones"), 1)
            dve.wait_ge(sem("const_loaded"), 16 * 19)
            nc.vector.tensor_scalar(negident[:], ident[:], -1.0, None, ALU.mult)
            link(nc.vector.tensor_copy(ident_bf[:], ident[:]))
            dve.wait_ge(sem("x_loaded"), 16)

            layer_norm(1, xin, "a_ln")
            rms_scale(xin, 1)
            dve.wait_ge(sem("w_raw_loaded"), 48)
            for n in range(3):
                ins = nc.vector.tensor_reduce(w_abs[:, n:n + 1], w_raw[n], AX.X, ALU.add, apply_absolute_value=True)
            ins.then_inc(sem("w_abs"), 1)
            for bb in range(B):
                dve.wait_ge(sem("a_kvsum_ps"), bb + 1)
                for cc in range(C):
                    ps = half(2, bb)[:, cc * KV:(cc + 1) * KV]
                    nc.vector.tensor_tensor(a_kv[:, bb, cc, 0:P], ps[:, 0:P], blockmask[:], ALU.mult)
                    ins = nc.vector.tensor_scalar(a_kv[:, bb, cc, P:KV], headmask[:], ps[:, P:P + 1], None, ALU.mult)
                ins.then_inc(sem("a_kvsum"), 1)
            dve.wait_ge(sem("w_abs_ps"), 1)
            link(nc.vector.tensor_scalar(w_mean[:], half(0, 0)[:, 0:3], 1.0 / (D * INNER), 1e-5, ALU.mult, ALU.max))
            nc.vector.reciprocal(w_scale[:], w_mean[:]).then_inc(sem("w_mean"), 1)
            for tt in range(T):
                dve.wait_ge(sem("a_at_ps"), tt + 1)
                ps = bank[tt % 2][:, 0:C * KV].rearrange("p (c k) -> p c k", c=C)
                link(nc.vector.tensor_scalar(a_den[:, tt % 2], ps[:, :, P:KV], 1e-6, None, ALU.add))
                link(nc.vector.reciprocal(a_z, a_den[:, tt % 2]))
                for cc in range(C):
                    ins = nc.vector.tensor_tensor(y[:, tt, cc * P:(cc + 1) * P].rearrange("p (h e) -> p h e", h=HC),
                                            ps[:, cc, 0:P].rearrange("p (h e) -> p h e", h=HC),
                                            a_z[:, cc, :].unsqueeze(2).broadcast_to([P, HC, DH]),
                                            ALU.mult)
                ins.then_inc(sem("y_ready"), 1)
            for tt in range(T):
                dve.wait_ge(sem("a_proj_ps"), tt + 1)
                link(nc.vector.tensor_tensor(a_tmp[:, tt % 2, :], half(0, tt % 2)[:, 0:D], gamma[:], ALU.mult))
                nc.vector.tensor_tensor(a_x1[:, tt, :], a_tmp[:, tt % 2, :], xin[:, tt, :], ALU.add).then_inc(sem("a_x1"), 1)
            rms_scale(a_x1, 2)
            for n, wq in enumerate((wq_gate, wq_up, wq_down)):
                dve.wait_ge(sem("w_whole"), n + 1)
                nc.vector.tensor_scalar(wq[:].rearrange("p a b -> p (a b)"), w_raw[n], 1.0, -1.0,
                                        ALU.min, ALU.max).then_inc(sem("w_rounded"), 1)
            for tt in range(T):
                dve.wait_ge(sem("a_mlp_ps"), tt + 1)
                link(nc.vector.tensor_tensor(a_tmp[:, tt % 2, :], half(2, tt % 2)[:, 0:D], gamma[:], ALU.mult))
                link(nc.vector.tensor_tensor(a_tmp[:, tt % 2, :], a_tmp[:, tt % 2, :], a_x1[:, tt, :], ALU.add))
                ins = nc.vector.tensor_tensor(x[:, tt, :], x[:, tt, :], a_tmp[:, tt % 2, :], ALU.add)
                ins.then_inc(sem("a_added"), 1)
            dve.wait_ge(sem("a_added"), T)

            layer_norm(2, y, "y_ready")
            step = [0]

            def stepped(ins):
                step[0] += 1
                ins.then_inc(sem("b_step"), 1)
                return step[0]

            def after(value):
                dve.wait_ge(sem("b_step"), value)

            def b_candidates(i, j):
                if step[0]:
                    after(step[0])
                    dve.sem_clear(sem("b_step"))
                step[0] = 0
                for k in range(2):
                    dve.wait_ge(sem("b_s_copied"), i * 8 + (2 * j + k + 1))
                    gate(k)
                    for blk in range(NBLK):
                        ins = nc.vector.max(b_cand[:, k, 8 * blk:8 * blk + 8],
                                            b_s[:, (2 * j + k) % 4, BLK * blk:BLK * (blk + 1)])
                    there = stepped(ins)
                after(there)
                nc.vector.tensor_reduce(b_neg, b_cand[:, :, 0:NBLK * 8:8], AX.X, ALU.max, negate=True).then_inc(sem("b_cand"), 1)
                dve.wait_ge(sem("b_cand"), i * 4 + (j + 1))
                gate()
                cut = [there, there]
                for r in range(NTOP - 1):
                    found = [0, 0]
                    for k in range(2):
                        after(cut[k])
                        ins = nc.vector.max(b_m8[:, k, :], b_cand[:, k, :])
                        if r == NTOP - 2:
                            ins.then_inc(sem("b_thr"), 1)
                        else:
                            found[k] = stepped(ins)
                    if r < NTOP - 2:
                        for k in range(2):
                            after(found[k])
                            cut[k] = stepped(nc.vector.match_replace(b_cand[:, k, :], b_m8[:, k, :], b_cand[:, k, :], MARK))

            def b_finish(i, j):
                found = [0, 0]
                for k in range(2):
                    n = 2 * j + k
                    dve.wait_ge(sem("b_z"), i * 8 + (n + 1))
                    gate(k)
                    found[k] = stepped(nc.vector.max(b_f8[:, k, :], b_z[:, n % 4, :]))
                kept = [0, 0]
                for k in range(2):
                    dve.wait_ge(sem("b_count"), i * 8 + (2 * j + k + 1))
                    after(found[k])
                    kept[k] = stepped(nc.vector.scalar_tensor_tensor(out=b_g8[:, k, :], in0=below[:], scalar=b_cnt[:, k:k + 1],
                                                                     in1=b_f8[:, k, :], op0=ALU.is_lt, op1=ALU.mult))
                stepped(nc.vector.tensor_tensor(b_least, b_least, b_cnt, ALU.min))
                for k in range(2):
                    n = (2 * j + k) % 4
                    after(kept[k])
                    nc.vector.match_replace(b_z[:, n, :], b_g8[:, k, :], b_z[:, n, :], 0.0).then_inc(sem("b_final"), 1)

            def b_below(i, j):
                dve.wait_ge(sem("b_te"), i * 4 + (j + 1))
                for k in range(2):
                    dve.wait_ge(sem("b_exp"), i * 8 + (2 * j + k + 1))
                    nc.vector.tensor_scalar(b_m[:, k, :], b_e[:, (2 * j + k) % 4, :], b_te[:, k:k + 1], None,
                                            ALU.is_lt).then_inc(sem("b_mask"), 1)

            def b_output(i, j):
                dve.wait_ge(sem("b_o_ps"), i * 4 + (j + 1))
                ps = bank[j % 2][:, 0:2 * V1].rearrange("p (k v) -> p k v", k=2)
                after(stepped(nc.vector.scalar_tensor_tensor(out=b_den, in0=b_all[:, j, :], scalar=1e-9, in1=ps[:, :, DH],
                                                             op0=ALU.mult, op1=ALU.add)))
                after(stepped(nc.vector.reciprocal(b_r, b_den)))
                nc.vector.tensor_tensor(b_o[:, bass.ds((i * 4 + j) * (2 * DH), 2 * DH)].rearrange("p (k e) -> p k e", k=2),
                                        ps[:, :, 0:DH], b_r.unsqueeze(2).broadcast_to([P, 2, DH]),
                                        ALU.mult).then_inc(sem("b_out"), 1)

            def b_slots(i, first=False):
                for j in range(4):
                    b_candidates(i, j)
                    if not (first and j == 0):
                        if j == 0:
                            b_finish(i - 1, 3)
                        else:
                            b_finish(i, j - 1)
                    b_below(i, j)
                    if not (first and j < 2):
                        if j < 2:
                            b_output(i - 1, j + 2)
                        else:
                            b_output(i, j - 2)

            link(nc.vector.memset(b_least, float(SC)))
            b_slots(0, first=True)
            with dve.Fori(1, PAIRS // 4) as i:
                b_slots(i)
            b_finish(PAIRS // 4 - 1, 3)
            b_output(PAIRS // 4 - 1, 2)
            b_output(PAIRS // 4 - 1, 3)
            dve.wait_ge(sem("b_out"), PAIRS)
            nc.vector.tensor_scalar(b_bad, b_least, float(SC - K_TOP), None, ALU.is_lt).then_inc(sem("b_bad"), 1)
            dve.wait_ge(sem("b_bad_ps"), 1)
            link(nc.vector.tensor_reduce(b_flagf, bank[0][:, 0:2], AX.X, ALU.add))
            nc.vector.tensor_copy(b_flag, b_flagf).then_inc(sem("b_flag"), 1)
            dve.wait_ge(sem("b_flag"), 1)
            with dve.If(dve.value_load(b_flag[0:1, 0:1], min_val=0, max_val=2 * P) > 0):
                DS = 2 * NTOP + 2
                with dve.Fori(0, B * H // 2) as i:
                    def chain(ins, k):
                        ins.then_inc(sem("g_step"), 1)
                        dve.wait_ge(sem("g_step"), k)

                    def top(j):
                        s, z, m8 = b_s[:, j % 2, :], b_z[:, j % 2, :], g_max[:, j % 2]
                        dve.wait_ge(sem("g_s_copied"), i * 8 + (j + 1))
                        gate()
                        dve.sem_clear(sem("g_step"))
                        chain(nc.vector.max(m8[:, 0, :], s), 1)
                        nc.vector.tensor_scalar(g_neg[:, j % 2, :], m8[:, 0, 0:1], -1.0, None,
                                                ALU.mult).then_inc(sem("g_neg"), 1)
                        chain(nc.vector.match_replace(z, m8[:, 0, :], s, MARK), 2)
                        for r in range(1, NTOP):
                            chain(nc.vector.max(m8[:, r, :], z), 2 * r + 1)
                            ins = nc.vector.match_replace(z, m8[:, r, :], z, MARK)
                            chain(ins, 2 * r + 2)

                    def probs(j):
                        dve.wait_ge(sem("g_exp"), i * 8 + (j + 1))
                        if j >= 2:
                            dve.wait_ge(sem("g_p_tr"), i * 8 + (j - 1))
                        nc.vector.scalar_tensor_tensor(out=b_s[:, 2:4][:, j % 2, :], in0=b_z[:, j % 2, :], scalar=MARK,
                                                       in1=b_e[:, j % 2, :], op0=ALU.is_equal, op1=ALU.mult,
                                                       accum_out=g_top[:, j % 2, :]).then_inc(sem("g_probs"), 1)
                        dve.wait_ge(sem("g_probs"), i * 8 + (j + 1))
                        chain(nc.vector.scalar_tensor_tensor(out=g_den[:, j % 2, :], in0=g_all[:, j % 2, :], scalar=1e-9,
                                                             in1=g_top[:, j % 2, :], op0=ALU.mult, op1=ALU.add), DS - 1)
                        chain(nc.vector.reciprocal(g_r[:, j % 2, :], g_den[:, j % 2, :]), DS)

                    def out(j):
                        dve.wait_ge(sem("g_o_ps"), i * 8 + (j + 1))
                        nc.vector.tensor_scalar(b_o[:, bass.ds((i * 8 + j) * DH, DH)], bank[0][:, 0:DH],
                                                g_r[:, j % 2, :], None, ALU.mult).then_inc(sem("g_o"), 1)

                    for j in range(2 * TB):
                        top(j)
                        probs(j)
                        if j >= 1:
                            out(j - 1)
                    out(2 * TB - 1)
                dve.wait_ge(sem("g_o"), B * H * TB)
            o4 = b_o.rearrange("p (b h q e) -> p b h q e", b=B, h=H, q=TB)
            for tt in range(T):
                xv = x[:, tt, :].rearrange("p (h e) -> p h e", h=H)
                nc.vector.tensor_tensor(xv, xv, o4[:, tt // TB, :, tt % TB, :], ALU.add).then_inc(sem("b_added"), 1)
            dve.wait_ge(sem("b_added"), T)

            layer_norm(3, y, "c_y")
            dve.wait_ge(sem("c_y"), T)

            def absmax(dst, src):
                return nc.vector.tensor_reduce(dst, src, AX.X, ALU.max, apply_absolute_value=True)

            link(absmax(c_am, y[:]))
            link(nc.vector.tensor_scalar(c_am1, c_am, 1e-5, None, ALU.max))
            link(nc.vector.reciprocal(c_s, c_am1))
            link(nc.vector.tensor_scalar(c_s, c_s, 127.0, None, ALU.mult))
            link(nc.vector.tensor_scalar(c_si, c_am1, 1.0 / 127.0, None, ALU.mult))
            nc.vector.tensor_scalar(c_ag, c_si, w_mean[:, 0:1], None, ALU.mult)
            link(nc.vector.tensor_scalar(c_au, c_si, w_mean[:, 1:2], None, ALU.mult))

            def xq_T(tt):
                dve.wait_ge(sem("c_xq_tr"), tt + 1)
                nc.vector.tensor_scalar(c_qT[:, :, tt * P:(tt + 1) * P],
                                        bank[tt % 2][:, 0:P].bitcast(BF16).rearrange("p (c n) -> p c n", c=C),
                                        127.0, -128.0, ALU.min, ALU.max).then_inc(sem("c_xqT"), 1)

            for tt in range(T):
                link(nc.vector.tensor_scalar(c_q[:, tt % 2, :], y[:, tt, :], c_s[:, tt:tt + 1], ROUND, ALU.mult, ALU.add))
                if tt >= 2:
                    dve.wait_ge(sem("c_xq_tr"), tt - 1)
                nc.vector.tensor_scalar(c_qb[:, tt % 2, :], c_q[:, tt % 2, :], ROUND, None, ALU.subtract).then_inc(sem("c_xq"), 1)
                if tt >= 1:
                    xq_T(tt - 1)
            xq_T(T - 1)
            for tt in range(T):
                dve.wait_ge(sem("c_g"), tt + 1)
                dve.wait_ge(sem("c_u_ps"), tt + 1)
                nc.vector.scalar_tensor_tensor(out=c_h[:, tt % 2, :], in0=wide[1][:], scalar=c_au[:, tt:tt + 1],
                                               in1=c_g[:, tt % 2, :], op0=ALU.mult, op1=ALU.mult).then_inc(sem("c_h"), 1)
                dve.wait_ge(sem("c_h"), tt + 1)
                link(absmax(c_hm[:, tt:tt + 1], c_h[:, tt % 2, :]))
                link(nc.vector.tensor_scalar(c_hm1[:, tt:tt + 1], c_hm[:, tt:tt + 1], 1e-5, None, ALU.max))
                link(nc.vector.reciprocal(c_hs[:, tt:tt + 1], c_hm1[:, tt:tt + 1]))
                link(nc.vector.tensor_scalar(c_hi[:, tt:tt + 1], c_hs[:, tt:tt + 1], 127.0, None, ALU.mult))
                link(nc.vector.tensor_scalar(c_hr, c_h[:, tt % 2, :], c_hi[:, tt:tt + 1], ROUND, ALU.mult, ALU.add))
                if tt >= 2:
                    dve.wait_ge(sem("c_h_tr"), tt - 1)
                nc.vector.tensor_scalar(c_hb[:, tt % 2, :], c_hr, ROUND, None, ALU.subtract).then_inc(sem("c_hq"), 1)
                nc.vector.tensor_scalar(c_ad[:, tt:tt + 1], c_hm1[:, tt:tt + 1], w_mean[:, 2:3], 1.0 / 127.0, ALU.mult, ALU.mult).then_inc(sem("c_ad"), 1)
                dve.wait_ge(sem("c_h_tr"), tt + 1)
                nc.vector.tensor_scalar(c_hT[:, tt % 2], half(2, tt % 2).bitcast(BF16).rearrange("p (k n) -> p k n", k=KC),
                                        127.0, -128.0, ALU.min, ALU.max).then_inc(sem("c_hT"), 1)
                dve.wait_ge(sem("c_d_ps"), tt + 1)
                dve.wait_ge(sem("c_ad"), tt + 1)
                nc.vector.scalar_tensor_tensor(out=x[:, tt, :], in0=bank[tt % 2][:, 0:D], scalar=c_ad[:, tt:tt + 1],
                                               in1=x[:, tt, :], op0=ALU.mult, op1=ALU.add).then_inc(sem("c_added"), 1)
            dve.wait_ge(sem("c_added"), T)

            layer_norm(4, y, "y_ready")
            for g in range(C * B):
                cc = g // B
                dve.wait_ge(sem("d_q_ps"), g + 1)
                if g >= 1:
                    dve.wait_ge(sem("d_q_stored"), 16 * g)
                nc.vector.tensor_scalar(d_proj[:, 0, :], half(0, 0), cols["aq_b"][:, cc:cc + 1], DH ** -0.5,
                                        ALU.add, ALU.mult).then_inc(sem("d_q_proj"), 1)
            v4 = d_v.rearrange("p (b h q e) -> p b h q e", b=B, h=H, q=TB)
            nc.vector.memset(d_v.rearrange("p (n e) -> p n e", e=V1)[:, :, DH:V1], 1.0).then_inc(sem("d_vones"), 1)
            for tt in range(T):
                dve.wait_ge(sem("d_v_ps"), tt + 1)
                nc.vector.tensor_copy(v4[:, tt // TB, :, tt % TB, 0:DH],
                                      half(1, tt % 2)[:, 0:D].rearrange("p (h e) -> p h e", h=H)).then_inc(sem("d_v"), 1)
            def d_row_max(i, j):
                for qt in range(TB):
                    n = (qt + 1) * P
                    dve.wait_ge(sem("d_scores"), i * 8 + (TB * j + qt + 1))
                    wait(dve, "d_p", i * 8 + (TB * (j - 2) + qt + 1))
                    gate(qt)
                    nc.vector.tensor_tensor_reduce(out=d_s[:, j % 2, qt, 0:n], in0=half(qt // 2, qt % 2)[:, 0:n],
                                                   in1=causal[:, S - n:S], scale=1.0, scalar=MARK, op0=ALU.add,
                                                   op1=ALU.max, accum_out=d_max[:, j % 2, qt:qt + 1]).then_inc(sem("d_s"), 1)
                dve.wait_ge(sem("d_s"), i * 8 + (TB * j + TB))
                nc.vector.tensor_scalar(d_neg[:, j % 2, :], d_max[:, j % 2, :], -1.0, None, ALU.mult).then_inc(sem("d_neg"), 1)

            def d_output(i, j):
                dve.wait_ge(sem("d_o_ps"), i * 2 + (j + 1))
                ps = bank[j % 2][:, 0:TB * V1].rearrange("p (q v) -> p q v", q=TB)
                nc.vector.reciprocal(d_r[:, j % 2, :], ps[:, :, DH]).then_inc(sem("d_r"), 1)
                dve.wait_ge(sem("d_r"), i * 2 + (j + 1))
                nc.vector.tensor_tensor(d_o[:, bass.ds((i * 2 + j) * (TB * DH), TB * DH)].rearrange("p (q e) -> p q e", q=TB),
                                        ps[:, :, 0:DH], d_r[:, j % 2, :].unsqueeze(2).broadcast_to([P, TB, DH]),
                                        ALU.mult).then_inc(sem("d_o"), 1)

            def d_slots(i, first=False, last=False):
                for j in range(2):
                    if not (last and j == 1):
                        d_row_max(i, j + 1)
                    if not (first and j == 0):
                        if j == 0:
                            d_output(i - 1, 1)
                        else:
                            d_output(i, 0)

            d_row_max(0, 0)
            d_slots(0, first=True)
            with dve.Fori(1, B * H // 2 - 1) as i:
                d_slots(i)
            d_slots(B * H // 2 - 1, last=True)
            d_output(B * H // 2 - 1, 1)
            dve.wait_ge(sem("d_o"), B * H)
            o5 = d_o.rearrange("p (b h q e) -> p b h q e", b=B, h=H, q=TB)
            for tt in range(T):
                nc.vector.tensor_copy(y[:, tt, :].rearrange("p (h e) -> p h e", h=H),
                                      o5[:, tt // TB, :, tt % TB, :]).then_inc(sem("y_ready"), 1)

            def add_to_x(ready, banks, done):
                for tt in range(T):
                    dve.wait_ge(sem(ready), tt + 1)
                    nc.vector.tensor_tensor(x[:, tt, :], banks(tt % 2)[:, 0:D], x[:, tt, :], ALU.add).then_inc(sem(done), 1)
                dve.wait_ge(sem(done), T)

            add_to_x("d_out_ps", lambda k: half(2, k), "d_added")

            for tt in range(CT):
                k_ps = half(0, tt % 2)[:, 0:D]
                dve.wait_ge(sem("e_kv_ps"), tt + 1)
                nc.vector.tensor_scalar(e_t[:, tt % 2, 0:D], k_ps, 0.0, None, ALU.min).then_inc(sem("e_kmin"), 1)
                nc.vector.tensor_copy(e_v[:, tt, :], half(0, tt % 2)[:, D:2 * D])
                dve.wait_ge(sem("e_kexp"), tt + 1)
                link(nc.vector.tensor_scalar(e_t[:, tt % 2, 0:D], e_t[:, tt % 2, D:2 * D], -1.0, None, ALU.add))
                nc.vector.scalar_tensor_tensor(out=e_k[:, tt, :], in0=k_ps, scalar=0.0, in1=e_t[:, tt % 2, 0:D],
                                               op0=ALU.max, op1=ALU.add).then_inc(sem("e_kv"), 1)
            dve.wait_ge(sem("e_kn"), C)
            link(nc.vector.reciprocal(e_kr, e_kn))
            for bb in range(B):
                dve.wait_ge(sem("e_sum_ps"), bb + 1)
                for cc in range(C):
                    n = cc * B + bb
                    ins = nc.vector.scalar_tensor_tensor(out=e_kv[:, bb, cc, :], in0=half(1, bb)[:, cc * P:(cc + 1) * P],
                                                         scalar=e_kr[:, n:n + 1], in1=blockmask[:],
                                                         op0=ALU.mult, op1=ALU.mult)
                ins.then_inc(sem("e_sum"), 1)
            layer_norm(5, y, "y_ready")
            for g in range(C * B):
                cc, bb = g // B, g % B
                q_ps, bias, sl = half(0, g % 2), cols["lq_b"][:, cc:cc + 1], slice(bb * S, (bb + 1) * S)
                dve.wait_ge(sem("e_q_ps"), g + 1)
                nc.vector.tensor_scalar(sq[:, g % 2, :], q_ps, bias, 0.0, ALU.add, ALU.min).then_inc(sem("e_qmin"), 1)
                nc.vector.tensor_scalar(e_qT[:, cc, sl], q_ps, bias, 0.0, ALU.add, ALU.max)
                dve.wait_ge(sem("e_qexp"), g + 1)
                link(nc.vector.tensor_scalar(e_qq[:, cc, sl], e_qq[:, cc, sl], -1.0, None, ALU.add))
                nc.vector.tensor_tensor(e_qT[:, cc, sl], e_qT[:, cc, sl], e_qq[:, cc, sl], ALU.add).then_inc(sem("e_qelu"), 1)
            for tt in range(T):
                dve.wait_ge(sem("e_qn"), tt + 1)
                link(nc.vector.reciprocal(e_qr[:, tt % 2], e_qn[:, tt % 2]))
                for cc in range(C):
                    ins = nc.vector.tensor_tensor(y[:, tt, cc * P:(cc + 1) * P].rearrange("p (h e) -> p h e", h=HC),
                                                  half(1, tt % 2)[:, cc * P:(cc + 1) * P].rearrange("p (h e) -> p h e", h=HC),
                                                  e_qr[:, tt % 2, cc, :].unsqueeze(2).broadcast_to([P, HC, DH]), ALU.mult)
                ins.then_inc(sem("y_ready"), 1)
            add_to_x("e_out_ps", lambda k: half(2, k), "e_added")

            layer_norm(6, y, "y_ready")
            dve.wait_ge(sem("f_table_loaded"), 32)
            link(nc.vector.tensor_tensor(f_s2, f_sig, f_sig, ALU.mult))
            link(nc.vector.reciprocal(f_iv, f_s2))
            link(nc.vector.tensor_tensor(f_mi, f_mu, f_iv, ALU.mult))
            link(nc.vector.tensor_tensor(f_m2i, f_mu, f_mi, ALU.mult))
            dve.wait_ge(sem("yT_ready"), 9 * T)
            for cc in range(C):
                for bb in range(B):
                    ins = nc.vector.bn_stats(f_bn[:, cc, bb, :], yT[:, cc, bb * S:(bb + 1) * S])
            link(ins)
            for cc in range(C):
                for bb in range(B):
                    ins = nc.vector.bn_aggr(f_mv[:, cc, bb, :], f_bn[:, cc, bb, :])
            link(ins)
            nc.vector.tensor_scalar(f_m1s, f_mv[:, :, :, 0], -2.0, None, ALU.mult)
            link(nc.vector.tensor_tensor(f_sq, f_mv[:, :, :, 0], f_mv[:, :, :, 0], ALU.mult))
            nc.vector.tensor_tensor(f_m2, f_sq, f_mv[:, :, :, 1], ALU.add).then_inc(sem("f_moments"), 1)
            dve.wait_ge(sem("f_loss_ps"), 1)
            link(nc.vector.tensor_scalar(f_nl[0:B], half(0, 0)[0:B, 0:E], -1.0 / D, None, ALU.mult))
            link(nc.vector.max(f_best[0:B], f_nl[0:B]))
            nc.vector.max_index(f_idx[0:B], f_best[0:B], f_nl[0:B]).then_inc(sem("f_chosen"), 1)
            add_to_x("f_out_ps", lambda k: bank[k], "f_added")


def kernel(**inputs):
    import concourse.bacc as bacc
    from concourse.bass_utils import run_bass_kernel_spmd

    def arr(name):
        return np.asarray(inputs[name])

    def keep(a):
        return np.ascontiguousarray(a)

    def tiles(a):
        return keep(a.reshape(-1, P, a.shape[-1]).transpose(1, 0, 2))

    def wT(*names):
        return tiles(np.concatenate([arr(n) for n in names], 0).T)

    def col(name):
        return keep(arr(name).reshape(-1, P).T)

    def row(*names):
        return keep(np.concatenate([arr(n) for n in names]).reshape(1, -1))

    ctx = arr("ctx_1024").reshape(B * SC, D)
    pos = np.arange(S, dtype=np.float32)
    slopes = np.array([(2.0 ** (-8.0 / H)) * (2.0 ** (-8.0 / H)) ** k for k in range(H)], dtype=np.float32)
    block = np.kron(np.eye(HC, dtype=np.float32), np.ones((DH, DH), np.float32))
    mask = np.zeros((P, S), np.float32)
    mask[:, S - P:] = np.where(np.arange(P)[None, :] > np.arange(P)[:, None], np.float32(MASKED), np.float32(0))
    alibi_k = np.stack([np.stack([sl * pos, -sl * np.ones(S, np.float32)]) for sl in slopes])
    a = {
        "x": tiles(arr("x").reshape(B * S, D)),
        "ident": np.eye(P, dtype=np.float32),
        "blockmask": block,
        "headmask": keep(block[:, ::DH]),
        "causal": mask,
        "alibi_q": np.stack([np.ones(S, np.float32), pos]),
        "alibi_k": keep(np.tile(alibi_k.astype(np.float32), (B, 1, 1)).reshape(B * H * 2, S)),
        "ctxT": tiles(ctx.T),
        "ctxV": keep(np.concatenate([ctx.reshape(B, CTB, P, H, DH), np.ones((B, CTB, P, H, 1), np.float32)], -1)
                     .transpose(2, 0, 3, 1, 4).reshape(P, B * H * CTB * V1)),
        "below": np.broadcast_to(np.arange(SC - K_TOP, SC - K_TOP + 8, dtype=np.float32), (P, 8)).copy(),
        "scale1": col("L0_attn_scale1"), "scale2": col("L0_attn_scale2"), "conv1_b": col("L0_attn_conv1_b"),
        "aq_b": col("L1_attn_q_b"), "ak_b": col("L1_attn_k_b"), "lq_b": col("L1_xattn_bq"),
        "proj_b": row("L0_attn_proj_b"), "conv2_b": row("L0_attn_conv2_b"), "av_b": row("L1_attn_v_b"),
        "ao_b": row("L1_attn_o_b"), "lkv_b": row("L1_xattn_bk", "L1_xattn_bv"), "lo_b": row("L1_xattn_bo"),
        "base_b": row("L1_ffn_base_b"), "gamma": row("L0_attn_gamma"),
        "qkvT": wT("L0_attn_qkv_w"), "projT": wT("L0_attn_proj_w"), "conv1T": wT("L0_attn_conv1_w"),
        "conv2T": wT("L0_attn_conv2_w"), "xqT": wT("L0_xattn_Wq"), "xkT": wT("L0_xattn_Wk"),
        "gateT": wT("L0_ffn_w_gate").reshape(P, -1), "upT": wT("L0_ffn_w_up").reshape(P, -1),
        "downT": wT("L0_ffn_w_down").reshape(P, -1),
        "aqT": wT("L1_attn_q_w"), "akT": wT("L1_attn_k_w"), "avT": wT("L1_attn_v_w"), "aoT": wT("L1_attn_o_w"),
        "lqT": wT("L1_xattn_Wq"), "lkvT": wT("L1_xattn_Wk", "L1_xattn_Wv"), "loT": wT("L1_xattn_Wo"),
        "baseT": wT("L1_ffn_base_W"),
        "muT": tiles(arr("L1_ffn_disc_mu").T), "sigmaT": tiles(arr("L1_ffn_disc_sigma").T),
        "down": keep(arr("L1_ffn_down_W").reshape(E, C, P, R).transpose(0, 2, 1, 3)),
        "up": keep(arr("L1_ffn_up_W")),
        "convT": keep(arr("L1_ffn_conv_W").transpose(0, 2, 1).reshape(E, C, P, D).transpose(0, 2, 1, 3)),
        "down_b": keep(arr("L1_ffn_down_b").reshape(E, R, 1)),
        "up_b": keep(arr("L1_ffn_up_b").reshape(E, C, P).transpose(0, 2, 1)),
        "conv_b": keep(arr("L1_ffn_conv_b")),
    }
    nc = bacc.Bacc("TRN2", target_bir_lowering=False, num_devices=1)
    t = {n: nc.dram_tensor("in_" + n, v.shape, mybir.dt.from_np(v.dtype), kind="ExternalInput").ap()
         for n, v in a.items()}
    t["out"] = nc.dram_tensor("out", (P, T, D), F32, kind="ExternalOutput").ap()
    decoder(nc, t)
    r = run_bass_kernel_spmd(nc, [{"in_" + n: v for n, v in a.items()}], core_ids=[0])
    return r.results[0]["out"].transpose(1, 0, 2).reshape(B, S, D)
```

```python
from contextlib import ExitStack

import numpy as np

import concourse.bass as bass
from concourse import mybir

P = 128
B, S, D = 2, 512, 256
SC = 1024
H, DH = 16, 16
T = B * S // P
TB = S // P
CT = B * SC // P
CTB = SC // P
C = D // P
HC = P // DH
HID = 512
MC = HID // P
INNER = 1024
KC = INNER // P
E, R = 8, 64
K_TOP = 64
NTOP = K_TOP // 8
NBLK = 16
BLK = SC // NBLK
PAIRS = B * H * TB // 2
V1 = DH + 1
I32 = mybir.dt.int32
KV = P + HC
PARTS_Q = ((0, 0, 3), (3, 1, 3), (6, 2, 2))
PARTS_K = ((0, 3), (3, 3), (6, 2))
BIAS_AT = 7 * DH
D_DMAS = 16 * (len(PARTS_Q) + len(PARTS_K) + 1)
HEAD_DMAS = 16 * (len(PARTS_Q) + len(PARTS_K))
ALIBI = 9

F32 = mybir.dt.float32
BF16 = mybir.dt.bfloat16
U32 = mybir.dt.uint32
ALU = mybir.AluOpType
ACT = mybir.ActivationFunctionType
AX = mybir.AxisListType

LN_EPS = 1e-5
RMS_GAIN = 16.0 + 1e-6
ROUND = 12582912.0
MARK = -3.0e38
MASKED = -1.0e30


def decoder(nc, t):
    with ExitStack() as ctx:
        def sb(name, shape, dt=F32):
            return ctx.enter_context(nc.sbuf_tensor(name, shape, dt))

        sems = {}

        def sem(name):
            if name not in sems:
                sems[name] = ctx.enter_context(nc.semaphore(name))
            return sems[name]

        bank = [ctx.enter_context(nc.psum_tensor(f"bank{i}", [P, 512], F32)) for i in range(2)]
        wide = [ctx.enter_context(nc.psum_tensor(f"wide{i}", [P, 1024], F32)) for i in range(3)]
        def half(i, j):
            return wide[i][:, 512 * j:512 * j + 512]

        ident = sb("ident", [P, P])
        negident = sb("negident", [P, P])
        ident_bf = sb("ident_bf", [P, P], BF16)
        ones = sb("ones", [P, P])
        blockmask = sb("blockmask", [P, P])
        headmask = sb("headmask", [P, HC])
        causal = sb("causal", [P, S])
        x = sb("x", [P, T, D])
        y = sb("y", [P, T, D])
        yT = sb("yT", [P, C, T * P])
        xin = sb("xin", [P, T, D])
        ctxT = sb("ctxT", [P, C, B * SC])
        bn = sb("bn", [P, T, 6])
        mv = sb("mv", [P, T, 2])
        var = sb("var", [P, T])
        sd = sb("sd", [P, T])
        rstd = sb("rstd", [P, T])
        sq = sb("sq", [P, 2, 512])
        names = {"qkvT": 3 * D, "projT": D, "conv1T": HID, "xqT": D, "xkT": D,
                 "aqT": D, "akT": D, "avT": D, "aoT": D, "lqT": D, "lkvT": 2 * D, "loT": D, "baseT": D}
        w = {n: sb("w_" + n, [P, C, k]) for n, k in names.items()}
        conv2T = sb("w_conv2T", [P, MC, D])
        wq_gate = sb("wq_gate", [P, C, INNER], BF16)
        wq_up = sb("wq_up", [P, C, INNER], BF16)
        wq_down = sb("wq_down", [P, KC, D], BF16)
        cols = {n: sb("c_" + n, [P, k]) for n, k in
                {"scale1": C, "scale2": C, "conv1_b": MC, "aq_b": C, "ak_b": C, "lq_b": C}.items()}
        rows = {n: sb("r_" + n, [1, k]) for n, k in
                {"proj_b": D, "conv2_b": D}.items()}
        gamma = sb("gamma", [P, D])
        vB = sb("vB", [P, B * H * CTB * V1])
        w_mean = sb("w_mean", [P, 3])
        w_scale = sb("w_scale", [P, 3])
        w_abs = sb("w_abs", [P, 3])
        gate_out = sb("gate_out", [P, TB])
        bq_dram = nc.dram_tensor("bq_dram", [3, B * H * DH, S], BF16, kind="Internal").ap()
        bk_dram = nc.dram_tensor("bk_dram", [3, B * H * DH, SC], BF16, kind="Internal").ap()
        dq_dram = nc.dram_tensor("dq_dram", [3, B * H * DH, S], BF16, kind="Internal").ap()
        dk_dram = nc.dram_tensor("dk_dram", [3, B * H * DH, S], BF16, kind="Internal").ap()

        WORK = 18560
        work = sb("work", [P, WORK])

        class Area:
            def __init__(self):
                self.at = 0

            def take(self, *shape, dt=F32):
                n = int(np.prod(shape))
                words = n if dt != BF16 else (n + 1) // 2
                ap = work[:, self.at:self.at + words]
                self.at += words
                assert self.at <= WORK, self.at
                if dt != F32:
                    ap = ap.bitcast(dt)
                if len(shape) > 1:
                    lab = "abcd"[:len(shape)]
                    ap = ap.rearrange(f"p ({' '.join(lab)}) -> p {' '.join(lab)}",
                                      **{k: v for k, v in zip(lab, shape)})
                return ap

        a = Area()
        a_qT = a.take(C, T * P)
        a_k = a.take(T, D)
        a_v = a.take(T, C, P + 1)
        a_kv = a.take(B, C, KV)
        a_den = a.take(2, C, HC)
        a_z = a.take(C, HC)
        a_x1 = a.take(T, D)
        a_tmp = a.take(2, D)
        a_hT = a.take(MC, T * P)
        w_raw = [vB[:, 0:C * INNER], vB[:, C * INNER:2 * C * INNER], a.take(C * INNER)]
        spread, at = {}, 0
        for n, k in (("lkv_b", 2 * D), ("av_b", D), ("ao_b", D), ("lo_b", D), ("base_b", D)):
            spread[n] = xin[:].rearrange("p t d -> p (t d)")[:, at:at + k]
            at += k
        b = Area()
        b_q = b.take(2, S, dt=BF16)
        b_k = b.take(2, SC, dt=BF16)
        b_x = b.take(8, SC)
        b_z = b.take(4, SC)
        b_sgn = b.take(2, SC, dt=BF16)
        b_m = b.take(2, SC, dt=BF16)
        b_part = (b_z.rearrange("p a n -> p (a n)")[:, 0:6 * 512].bitcast(BF16)
                  .rearrange("p (g a n) -> p g a n", g=4, a=3))
        b_rest = b_z[:, 3, :].rearrange("p (g n) -> p g n", g=2)
        b_pT = yT
        b_o = y[:].rearrange("p t d -> p (t d)")
        b_cand = b.take(2, NBLK * 8)
        b_top8 = b.take(2, 8)
        b_m8 = b.take(2, 8)
        b_f8 = b.take(2, 8)
        b_g8 = b.take(2, 8)
        b_neg = b.take(2)
        b_te = b.take(2)
        b_cnt = b.take(2, 2)
        b_least = b.take(2)
        b_bad = b.take(2)
        b_all = b.take(4, 2)
        b_den = b.take(2)
        b_r = b.take(2)
        g_s, g_w, g_e = b_x[:, 0:2], b_x[:, 2:4], b_x[:, 4:6]
        g_max = b.take(2, NTOP, 8)
        g_neg = b.take(2, 1)
        g_all = b.take(2, 1)
        g_top = b.take(2, 1)
        g_den = b.take(2, 1)
        g_r = b.take(2, 1)
        c = Area()
        c_am = c.take(T)
        c_am1 = c.take(T)
        c_s = c.take(T)
        c_si = c.take(T)
        c_ag = c.take(T)
        c_au = c.take(T)
        c_q = c.take(2, D)
        c_qb = c.take(2, D, dt=BF16)
        c_qT = c.take(C, T * P, dt=BF16)
        c_g = c.take(2, INNER)
        c_h = c.take(2, INNER)
        c_hr = c.take(INNER)
        c_hb = c.take(2, INNER, dt=BF16)
        c_hT = c.take(2, KC, P, dt=BF16)
        c_hm = c.take(T)
        c_hm1 = c.take(T)
        c_hs = c.take(T)
        c_hi = c.take(T)
        c_ad = c.take(T)
        d = Area()
        d_q = d.take(2, S, dt=BF16)
        d_k = d.take(2, S, dt=BF16)
        d_s = d.take(2, TB, S)
        d_p = d.take(2, TB, S)
        d_pT = d.take(TB, S)
        d_vh = d.take(2, TB * V1)
        d_oT = d.take(2, S)
        d_v = d.take(B * H * TB * V1)
        d_o = d.take(B * H * TB * DH)
        d_val, d_rest = d_s[:, 0, 0:2], d_s[:, 1, 0:2]
        d_part = (d_p.rearrange("p a q n -> p (a q n)")[:, 0:6 * 512].bitcast(BF16)
                  .rearrange("p (g a n) -> p g a n", g=4, a=3))
        d_max = d.take(2, TB)
        d_neg = d.take(2, TB)
        d_r = d.take(2, TB)
        e = Area()
        e_kv2 = e.take(CT, 2 * D)
        e_t = e.take(2, 2 * D)
        e_kk = e.take(2, D)
        e_qT = e.take(C, T * P)
        e_qq = e.take(C, T * P)
        e_kv = e.take(B, C, P)
        e_kn = e.take(B * C)
        e_kr = e.take(B * C)
        e_qn = e.take(2, C, HC)
        e_qr = e.take(2, C, HC)
        f = Area()
        f_mu = f.take(C, E)
        f_sig = f.take(C, E)
        f_s2 = f.take(C, E)
        f_iv = f.take(C, E)
        f_mi = f.take(C, E)
        f_mm = f.take(C, E)
        f_m2i = f.take(C, E)
        f_bn = f.take(C, B, 6)
        f_mv = f.take(C, B, 2)
        f_m1s = f.take(C, B)
        f_m2 = f.take(C, B)
        f_sq = f.take(C, B)
        f_nl = f.take(E)
        f_best = f.take(8)
        f_idx = f.take(8, dt=U32)
        f_down = f.take(B, C, R)
        f_up = f.take(B, D)
        f_conv = f.take(B, C, D)
        f_db = f.take(B)
        f_ub = f.take(B, C)
        f_cb = f.take(B, D)
        f_hT = f.take(T * P)
        f_aT = f.take(C, T * P)

        b_flagf = sb("b_flagf", [P, 1])
        b_flag = sb("b_flag", [P, 1], I32)
        below = sb("below", [P, 8])

        def wait(eng, name, value):
            if not (isinstance(value, int) and value <= 0):
                eng.wait_ge(sem(name), value)

        def back(i, j, n):
            if n <= j:
                return i, j - n
            if isinstance(i, int) and i == 0:
                return None
            return i - 1, j - n + 4

        block = ctx.enter_context(nc.Block())

        LNS = ["A", "B", "C", "D", "E", "F"]

        @block.sync
        def _(sp):
            sp.dma_start(x[:], t["x"]).then_inc(sem("x_loaded"), 16)
            for n, ap in (("ident", ident), ("blockmask", blockmask), ("headmask", headmask),
                          ("causal", causal), ("below", below)):
                sp.dma_start(ap[:], t[n]).then_inc(sem("const_loaded"), 16)
            for n in ("scale1", "scale2", "conv1_b", "aq_b", "ak_b", "lq_b"):
                sp.dma_start(cols[n][:], t[n]).then_inc(sem("const_loaded"), 16)
            for n in ("proj_b", "conv2_b"):
                sp.dma_start(rows[n][:], t[n]).then_inc(sem("const_loaded"), 16)
            sp.dma_start(gamma[:], t["gamma"].broadcast_to([P, D])).then_inc(sem("const_loaded"), 16)
            sp.dma_start(w["qkvT"][:], t["qkvT"]).then_inc(sem("w_A"), 16)
            sp.dma_start(w["projT"][:], t["projT"]).then_inc(sem("w_A"), 16)
            sp.dma_start(w["conv1T"][:], t["conv1T"]).then_inc(sem("w_A"), 16)
            sp.dma_start(conv2T[:], t["conv2T"]).then_inc(sem("w_A"), 16)
            for n, name in enumerate(("gateT", "upT", "downT")):
                sp.dma_start(w_raw[n], t[name]).then_inc(sem("w_raw_loaded"), 16)
            sp.dma_start(ctxT[:], t["ctxT"]).then_inc(sem("w_B"), 16)
            sp.dma_start(w["xkT"][:], t["xkT"]).then_inc(sem("w_B"), 16)
            sp.dma_start(w["xqT"][:], t["xqT"]).then_inc(sem("w_B"), 16)
            for n in ("aqT", "akT", "avT", "aoT", "lqT", "lkvT", "loT", "baseT"):
                sp.dma_start(w[n][:], t[n]).then_inc(sem("w_DEF"), 16)

            sp.wait_ge(sem("w_rounded"), 2)
            sp.dma_start(vB[:], t["ctxV"]).then_inc(sem("w_B"), 16)

            sp.wait_ge(sem("a_added"), T)
            for n, ap in spread.items():
                sp.dma_start(ap, t[n].broadcast_to(list(ap.shape))).then_inc(sem("spread_loaded"), 16)

            for g in range(C * B * 3):
                gk = g - C * B
                if gk < 0:
                    chunk = g % B * C + g // B
                    dst = bq_dram[:, chunk * P:(chunk + 1) * P, :]
                else:
                    chunk, hh = gk // 2 % B * C + gk // (2 * B), gk % 2
                    dst = bk_dram[:, chunk * P:(chunk + 1) * P, 512 * hh:512 * hh + 512]
                sp.wait_ge(sem("b_part3"), g + 1)
                sp.dma_start(dst.rearrange("a r s -> r a s"), b_part[:, g % 4]).then_inc(sem(f"b_stored{g % 4}"), 16)
            for g in range(4):
                sp.wait_ge(sem(f"b_stored{g}"), 16 * C * B * 3 // 4)

            def load_b(u, at, name):
                for lo, a, n in PARTS_Q:
                    sp.dma_start(b_q[lo * DH:(lo + n) * DH, u, :],
                                 bq_dram[a:a + 1, bass.ds(at, DH), :].broadcast_to([n, DH, S])).then_inc(sem(f"{name}{u}_loaded"), 16)
                for lo, n in PARTS_K:
                    sp.dma_start(b_k[lo * DH:(lo + n) * DH, u, :],
                                 bk_dram[0:n, bass.ds(at, DH), :]).then_inc(sem(f"{name}{u}_loaded"), 16)

            for name, scored in (("b_head", "b_scores"), ("g_head", "g_scores")):
                def stage_heads():
                    for u in range(2):
                        load_b(u, u * DH, name)
                    with sp.Fori(0, B * H // 2 - 1) as i:
                        for u in range(2):
                            sp.wait_ge(sem(scored), i * (2 * TB) + (u + 1) * TB)
                            load_b(u, (i * 2 + (2 + u)) * DH, name)

                if name == "b_head":
                    stage_heads()
                else:
                    sp.wait_ge(sem("b_flag"), 1)
                    with sp.If(sp.value_load(b_flag[0:1, 0:1], min_val=0, max_val=2 * P) > 0):
                        stage_heads()

            sp.wait_ge(sem("c_added"), T)
            for u in range(2):
                sp.dma_start(d_q[BIAS_AT:BIAS_AT + ALIBI, u, :], t["alibi_q"].bitcast(BF16)).then_inc(sem("d_alibi_loaded"), 16)
            for m in range(C * B * 2):
                chunk = m // 2 % B * C + m // (2 * B)
                dst = (dq_dram, dk_dram)[m % 2][:, chunk * P:(chunk + 1) * P, :]
                sp.wait_ge(sem("d_part3"), m + 1)
                sp.dma_start(dst.rearrange("a r s -> r a s"), d_part[:, m % 4]).then_inc(sem(f"d_stored{m % 4}"), 16)
            for m in range(4):
                sp.wait_ge(sem(f"d_stored{m}"), 16 * C * B * 2 // 4)

            def load_d(u, head):
                at = head * DH
                for lo, a, n in PARTS_Q:
                    n = min(n, BIAS_AT // DH - lo)
                    sp.dma_start(d_q[lo * DH:(lo + n) * DH, u, :],
                                 dq_dram[a:a + 1, bass.ds(at, DH), :].broadcast_to([n, DH, S])).then_inc(sem(f"d_head{u}_loaded"), 16)
                for lo, n in PARTS_K:
                    n = min(n, BIAS_AT // DH - lo)
                    sp.dma_start(d_k[lo * DH:(lo + n) * DH, u, :],
                                 dk_dram[0:n, bass.ds(at, DH), :]).then_inc(sem(f"d_head{u}_loaded"), 16)
                sp.dma_start(d_k[BIAS_AT:BIAS_AT + ALIBI, u, :],
                             t["alibi_k"][bass.ds(head, 1)].bitcast(BF16)).then_inc(sem(f"d_head{u}_loaded"), 16)

            for u in range(2):
                load_d(u, u)
            with sp.Fori(0, B * H // 2 - 1) as i:
                for u in range(2):
                    sp.wait_ge(sem("d_scores"), i * (2 * TB) + (u + 1) * TB)
                    load_d(u, i * 2 + (2 + u))

            sp.wait_ge(sem("e_added"), T)
            sp.dma_start(f_mu, t["muT"]).then_inc(sem("f_table_loaded"), 16)
            sp.dma_start(f_sig, t["sigmaT"]).then_inc(sem("f_table_loaded"), 16)
            sp.wait_ge(sem("f_chosen"), 1)
            for bb in range(B):
                k = sp.value_load(f_idx[bb:bb + 1, 0:1], min_val=0, max_val=E - 1)
                sp.dma_start(f_down[:, bb], t["down"][bass.ds(k, 1)].rearrange("a p c r -> p (a c) r")).then_inc(sem("f_expert_loaded"), 16)
                sp.dma_start(f_up[0:R, bb], t["up"][bass.ds(k, 1)].rearrange("a r d -> (a r) d")).then_inc(sem("f_expert_loaded"), 16)
                sp.dma_start(f_conv[:, bb], t["convT"][bass.ds(k, 1)].rearrange("a p c d -> p (a c) d")).then_inc(sem("f_expert_loaded"), 16)
                sp.dma_start(f_db[0:R, bb:bb + 1], t["down_b"][bass.ds(k, 1)].rearrange("a r o -> (a r) o")).then_inc(sem("f_expert_loaded"), 16)
                sp.dma_start(f_ub[:, bb], t["up_b"][bass.ds(k, 1)].rearrange("a p c -> p (a c)")).then_inc(sem("f_expert_loaded"), 16)
                sp.dma_start(f_cb[:, bb], t["conv_b"][bass.ds(k, 1)].broadcast_to([P, D])).then_inc(sem("f_expert_loaded"), 16)
            for tt in range(T):
                sp.wait_ge(sem("f_added"), T + tt + 1)
                sp.dma_start(t["out"][:, tt, :], x[:, tt, :]).then_inc(sem("out_stored"), 16)
            sp.wait_ge(sem("out_stored"), 16 * T)

        @block.tensor
        def _(pe):
            def transposes(src, n, dst_banks=bank):
                for tt in range(T):
                    pe.wait_ge(sem("y_ready"), n * T + tt + 1)
                    if tt >= 2:
                        pe.wait_ge(sem("yT_ready"), n * T + tt - 1)
                    for cc in range(C):
                        last = nc.tensor.transpose(dst_banks[tt % 2][:, cc * P:(cc + 1) * P],
                                                   src(tt, cc), ident[:])
                    last.then_inc(sem("y_turned"), 1)

            def tile_of(buf):
                return lambda tt, cc: buf[:, tt, cc * P:(cc + 1) * P]

            def channels_out(dst, wT, col, srcT, tok, n, k=C):
                for ic in range(k):
                    last = nc.tensor.matmul(dst, wT[:, ic, col:col + P], srcT[:, ic, tok:tok + n],
                                            start=(ic == 0), stop=(ic == k - 1))
                return last

            def tokens_out(dst, srcT, tt, wT, lo, n, bias=None, k=C):
                for ic in range(k):
                    last = nc.tensor.matmul(dst, srcT[:, ic, tt * P:(tt + 1) * P], wT[:, ic, lo:lo + n],
                                            start=(ic == 0), stop=(ic == k - 1 and bias is None))
                if bias is not None:
                    last = nc.tensor.matmul(dst, ones[0:1, 0:P], bias, start=False, stop=True)
                return last

            pe.wait_ge(sem("const_loaded"), 16 * 14)
            pe.wait_ge(sem("ones_set"), 1)
            transposes(tile_of(y), 0)
            pe.wait_ge(sem("w_A"), 64)
            pe.wait_ge(sem("yT_ready"), T)
            for g in range(C * B):
                cc, bb = g // B, g % B
                if g >= 2:
                    pe.wait_ge(sem("a_qT"), g - 1)
                channels_out(half(0, g % 2), w["qkvT"], cc * P, yT, bb * S, S).then_inc(sem("a_q_ps"), 1)
            for tt in range(T):
                if tt >= 2:
                    pe.wait_ge(sem("a_kv"), tt - 1)
                tokens_out(half(1, tt % 2), yT, tt, w["qkvT"], D, 2 * D).then_inc(sem("a_kv_ps"), 1)
            pe.wait_ge(sem("a_vones"), 1)
            pe.wait_ge(sem("a_kv"), T)
            for bb in range(B):
                for cc in range(C):
                    for j in range(TB):
                        tt = bb * TB + j
                        last = nc.tensor.matmul(half(2, bb)[:, cc * KV:cc * KV + P + 1],
                                                a_k[:, tt, cc * P:(cc + 1) * P], a_v[:, tt, cc, :],
                                                start=(j == 0), stop=(j == TB - 1))
                last.then_inc(sem("a_kvsum_ps"), 1)
            pe.wait_ge(sem("w_abs"), 1)
            nc.tensor.matmul(half(0, 0)[:, 0:3], ones[:], w_abs[:], start=True, stop=True).then_inc(sem("w_abs_ps"), 1)
            for tt in range(T):
                pe.wait_ge(sem("a_kvsum"), tt // TB + 1)
                if tt >= 2:
                    pe.wait_ge(sem("y_ready"), 1 * T + tt - 1)
                for cc in range(C):
                    last = nc.tensor.matmul(bank[tt % 2][:, cc * KV:(cc + 1) * KV],
                                            a_qT[:, cc, tt * P:(tt + 1) * P], a_kv[:, tt // TB, cc, :],
                                            start=True, stop=True)
                last.then_inc(sem("a_at_ps"), 1)
            pe.wait_ge(sem("y_ready"), 2 * T)
            transposes(tile_of(y), 1)
            for tt in range(T):
                pe.wait_ge(sem("yT_ready"), 1 * T + tt + 1)
                if tt < 2:
                    pe.wait_ge(sem("w_mean"), 1)
                else:
                    pe.wait_ge(sem("a_x1"), tt - 1)
                tokens_out(half(0, tt % 2)[:, 0:D], yT, tt, w["projT"], 0, D, rows["proj_b"][:]).then_inc(sem("a_proj_ps"), 1)
            transposes(tile_of(y), 2)
            pe.wait_ge(sem("yT_ready"), 3 * T)
            for g in range(MC * B):
                m, bb = g // B, g % B
                if g >= 2:
                    pe.wait_ge(sem("a_hT"), g - 1)
                channels_out(half(1, g % 2), w["conv1T"], m * P, yT, bb * S, S).then_inc(sem("a_h_ps"), 1)
            pe.wait_ge(sem("a_hT"), MC * B)
            for tt in range(T):
                if tt >= 2:
                    pe.wait_ge(sem("a_added"), tt - 1)
                tokens_out(half(2, tt % 2)[:, 0:D], a_hT, tt, conv2T, 0, D, rows["conv2_b"][:], k=MC).then_inc(sem("a_mlp_ps"), 1)

            transposes(tile_of(y), 3)
            pe.wait_ge(sem("w_B"), 64)
            pe.wait_ge(sem("yT_ready"), 4 * T)
            for g in range(C * B):
                cc, bb = g // B, g % B
                if g >= 2:
                    pe.wait_ge(sem("b_rest"), g - 1)
                channels_out(half(0, g % 2), w["xqT"], cc * P, yT, bb * S, S).then_inc(sem("b_q_ps"), 1)
            for g in range(C * B * 2):
                cc, bb, hh = g // (2 * B), g // 2 % B, g % 2
                if g >= 2:
                    pe.wait_ge(sem("b_rest"), C * B + g - 1)
                channels_out(half(1, g % 2), w["xkT"], cc * P, ctxT, bb * SC + 512 * hh, 512).then_inc(sem("b_k_ps"), 1)
            pe.wait_ge(sem("b_rest"), C * B * 3)

            def b_scores(i, j, k):
                u, qt = j // 2 % 2, 2 * (j % 2)
                if qt == 0 and k == 0:
                    pe.wait_ge(sem(f"b_head{u}_loaded"), i * HEAD_DMAS + HEAD_DMAS * (1 + j // 4))
                wait(pe, "b_s_copied", i * 8 + (2 * j + k - 1))
                for hh in range(2):
                    last = nc.tensor.matmul(wide[k][:, 512 * hh:512 * hh + 512],
                                            b_q[:, u, (qt + k) * P:(qt + k + 1) * P],
                                            b_k[:, u, 512 * hh:512 * hh + 512], start=True, stop=True)
                last.then_inc(sem("b_scores"), 1)

            def b_turn(i, j, k):
                n = 2 * j + k
                pe.wait_ge(sem("b_weights"), i * 8 + (n + 1))
                for hh in range(2):
                    wait(pe, "b_pT", i * 16 + (2 * n - 1 + hh))
                    for kt in range(CTB // 2 * hh, CTB // 2 * (hh + 1)):
                        last = nc.tensor.transpose(wide[2][:, kt * P:(kt + 1) * P],
                                                   b_z[:, n % 4, kt * P:(kt + 1) * P], ident[:])
                    last.then_inc(sem("b_tr"), 1)

            def b_attend(i, j):
                wait(pe, "b_out", i * 4 + (j - 1))
                for k in range(2):
                    n = 2 * j + k
                    for kt in range(CTB):
                        if kt % (CTB // 2) == 0:
                            pe.wait_ge(sem("b_pT"), i * 16 + (2 * n + kt // (CTB // 2) + 1))
                        last = nc.tensor.matmul(bank[j % 2][:, k * V1:(k + 1) * V1], b_pT[:, k, kt * P:(kt + 1) * P],
                                                vB[:, bass.ds((i * 2 + j // 2) * (CTB * V1) + kt * V1, V1)],
                                                start=(kt == 0), stop=(kt == CTB - 1))
                last.then_inc(sem("b_o_ps"), 1)

            def b_slot(i, j, more=True):
                if more:
                    for k in range(2):
                        b_scores(i, j + 1, k)
                two, three = back(i, j, 2), back(i, j, 3)
                if three:
                    b_attend(*three)
                if two and not (isinstance(i, int) and i * 4 + j - 2 >= PAIRS):
                    for k in range(2):
                        b_turn(*two, k)

            for k in range(2):
                b_scores(0, 0, k)
            for j in range(4):
                b_slot(0, j)
            with pe.Fori(1, PAIRS // 4 - 1) as i:
                for j in range(4):
                    b_slot(i, j)
            for j in range(4):
                b_slot(PAIRS // 4 - 1, j, more=j < 3)
            for j in range(3):
                b_slot(PAIRS // 4, j, more=False)
            pe.wait_ge(sem("b_bad"), 1)
            pe.wait_ge(sem("b_out"), PAIRS)
            nc.tensor.matmul(bank[0][:, 0:2], ones[:], b_bad, start=True, stop=True).then_inc(sem("b_bad_ps"), 1)
            pe.wait_ge(sem("b_flag"), 1)
            with pe.If(pe.value_load(b_flag[0:1, 0:1], min_val=0, max_val=2 * P) > 0):
                with pe.Fori(0, B * H // 2) as i:
                    def scores(j):
                        u, qt = j // TB, j % TB
                        if qt == 0:
                            pe.wait_ge(sem(f"g_head{u}_loaded"), i * HEAD_DMAS + HEAD_DMAS)
                        if j >= 2:
                            pe.wait_ge(sem("g_s_copied"), i * 8 + (j - 1))
                        for hh in range(2):
                            last = nc.tensor.matmul(wide[j % 2][:, 512 * hh:512 * hh + 512],
                                                    b_q[:, u, qt * P:(qt + 1) * P],
                                                    b_k[:, u, 512 * hh:512 * hh + 512], start=True, stop=True)
                        last.then_inc(sem("g_scores"), 1)

                    def weights_out(j):
                        u = j // TB
                        pe.wait_ge(sem("g_probs"), i * 8 + (j + 1))
                        if j >= 1:
                            pe.wait_ge(sem("g_pT"), i * 8 + j)
                        for kt in range(CTB):
                            last = nc.tensor.transpose(wide[2][:, kt * P:(kt + 1) * P],
                                                       g_w[:, j % 2, kt * P:(kt + 1) * P], ident[:])
                        last.then_inc(sem("g_p_tr"), 1)
                        pe.wait_ge(sem("g_pT"), i * 8 + (j + 1))
                        if j >= 1:
                            pe.wait_ge(sem("g_o"), i * 8 + j)
                        for kt in range(CTB):
                            last = nc.tensor.matmul(bank[0][:, 0:DH], b_pT[:, j % 2, kt * P:(kt + 1) * P],
                                                    vB[:, bass.ds((i * 2 + u) * (CTB * V1) + kt * V1, DH)],
                                                    start=(kt == 0), stop=(kt == CTB - 1))
                        last.then_inc(sem("g_o_ps"), 1)

                    for j in range(2 * TB):
                        scores(j)
                        if j >= 1:
                            weights_out(j - 1)
                    weights_out(2 * TB - 1)
                    pe.wait_ge(sem("g_o"), i * 8 + 8)

            for tt in range(T):
                pe.wait_ge(sem("c_xq"), tt + 1)
                if tt >= 2:
                    pe.wait_ge(sem("c_xqT"), tt - 1)
                for cc in range(C):
                    last = nc.tensor.transpose(bank[tt % 2][:, 0:P].bitcast(BF16)[:, cc * P:(cc + 1) * P],
                                               c_qb[:, tt % 2, cc * P:(cc + 1) * P], ident_bf[:])
                last.then_inc(sem("c_xq_tr"), 1)
            pe.wait_ge(sem("w_rounded"), 3)
            pe.wait_ge(sem("c_xqT"), T)

            def gate_up(tt):
                for n, (dst, wq) in enumerate(((wide[0], wq_gate), (wide[1], wq_up))):
                    if tt >= 1:
                        pe.wait_ge(sem(("c_g", "c_h")[n]), tt)
                    for hh in range(2):
                        for ic in range(C):
                            last = nc.tensor.matmul(dst[:, 512 * hh:512 * hh + 512], c_qT[:, ic, tt * P:(tt + 1) * P],
                                                    wq[:, ic, 512 * hh:512 * hh + 512],
                                                    start=(ic == 0), stop=(ic == C - 1))
                    last.then_inc(sem(("c_g_ps", "c_u_ps")[n]), 1)

            gate_up(0)
            for tt in range(T):
                if tt + 1 < T:
                    gate_up(tt + 1)
                pe.wait_ge(sem("c_hq"), tt + 1)
                if tt >= 2:
                    pe.wait_ge(sem("c_hT"), tt - 1)
                for kt in range(KC):
                    last = nc.tensor.transpose(half(2, tt % 2).bitcast(BF16)[:, kt * P:(kt + 1) * P],
                                               c_hb[:, tt % 2, kt * P:(kt + 1) * P], ident_bf[:])
                last.then_inc(sem("c_h_tr"), 1)
                pe.wait_ge(sem("c_hT"), tt + 1)
                if tt >= 2:
                    pe.wait_ge(sem("c_added"), tt - 1)
                for kt in range(KC):
                    last = nc.tensor.matmul(bank[tt % 2][:, 0:D], c_hT[:, tt % 2, kt], wq_down[:, kt, :],
                                            start=(kt == 0), stop=(kt == KC - 1))
                last.then_inc(sem("c_d_ps"), 1)

            transposes(tile_of(y), 4)
            pe.wait_ge(sem("w_DEF"), 16 * 8)
            pe.wait_ge(sem("yT_ready"), 5 * T)
            for g in range(C * B):
                cc, bb = g // B, g % B
                for n, wn in enumerate(("aqT", "akT")):
                    if g >= 1:
                        pe.wait_ge(sem("d_val"), 2 * g + n - 1)
                    channels_out(half(0, n), w[wn], cc * P, yT, bb * S, S).then_inc(sem("d_qk_ps"), 1)
            for tt in range(T):
                if tt >= 2:
                    pe.wait_ge(sem("d_v"), tt - 1)
                tokens_out(half(1, tt % 2)[:, 0:D], yT, tt, w["avT"], 0, D).then_inc(sem("d_v_ps"), 1)
            pe.wait_ge(sem("d_v"), T)
            pe.wait_ge(sem("d_vones"), 1)
            pe.wait_ge(sem("d_val"), C * B * 2)
            pe.wait_ge(sem("d_alibi_loaded"), 32)
            def d_scores(i, j):
                u = j % 2
                pe.wait_ge(sem(f"d_head{u}_loaded"), i * D_DMAS + D_DMAS * (1 + j // 2))
                for qt in range(TB):
                    n = (qt + 1) * P
                    wait(pe, "d_s", i * 8 + (TB * (j - 1) + qt + 1))
                    nc.tensor.matmul(half(qt // 2, qt % 2)[:, 0:n], d_q[0:BIAS_AT + ALIBI, u, qt * P:(qt + 1) * P],
                                     d_k[0:BIAS_AT + ALIBI, u, 0:n], start=True, stop=True).then_inc(sem("d_scores"), 1)

            def d_turn(i, j):
                for qt in range(TB):
                    pe.wait_ge(sem("d_p"), i * 8 + (TB * j + qt + 1))
                    wait(pe, "d_pT", i * 8 + (TB * j + qt - 1))
                    for kt in range(qt + 1):
                        last = nc.tensor.transpose(half(2, qt % 2)[:, kt * P:(kt + 1) * P],
                                                   d_p[:, j % 2, qt, kt * P:(kt + 1) * P], ident[:])
                    last.then_inc(sem("d_p_tr"), 1)

            def d_attend(i, j):
                wait(pe, "d_oT", i * 2 + j)
                pe.wait_ge(sem("d_vh"), i * 2 + (j + 1))
                pe.wait_ge(sem("d_pT"), i * 8 + (TB * j + TB))
                for kt in range(TB):
                    last = nc.tensor.matmul(bank[0][0:V1, kt * P:S], d_vh[:, j % 2, kt * V1:(kt + 1) * V1],
                                            d_pT[:, kt, kt * P:S], start=(kt == 0), stop=(kt == TB - 1))
                last.then_inc(sem("d_oT_ps"), 1)

            def d_back(i, j):
                pe.wait_ge(sem("d_oT"), i * 2 + (j + 1))
                wait(pe, "d_o", i * 2 + j)
                for qt in range(TB):
                    last = nc.tensor.matmul(bank[1][:, qt * V1:(qt + 1) * V1], d_oT[0:V1, j % 2, qt * P:(qt + 1) * P],
                                            ident[0:V1, 0:V1], start=True, stop=True)
                last.then_inc(sem("d_o_ps"), 1)

            def d_slots(i, first=False, last=False):
                for j in range(2):
                    if not (last and j == 1):
                        d_scores(i, j + 1)
                    d_turn(i, j)
                    if j == 1:
                        d_back(i, 0)
                    elif not first:
                        d_back(i - 1, 1)
                    d_attend(i, j)

            d_scores(0, 0)
            d_slots(0, first=True)
            with pe.Fori(1, B * H // 2 - 1) as i:
                d_slots(i)
            d_slots(B * H // 2 - 1, last=True)
            d_back(B * H // 2 - 1, 1)
            transposes(tile_of(y), 5)
            for tt in range(T):
                pe.wait_ge(sem("yT_ready"), 5 * T + tt + 1)
                if tt >= 2:
                    pe.wait_ge(sem("d_added"), tt - 1)
                tokens_out(half(2, tt % 2)[:, 0:D], yT, tt, w["aoT"], 0, D).then_inc(sem("d_out_ps"), 1)

            def e_kv_bank(bb, cc):
                return (half(1, bb), bank[bb])[cc][:, 0:P]

            for tt in range(CT + 2):
                if tt < CT:
                    if tt >= 2:
                        pe.wait_ge(sem("e_biased"), tt - 1)
                    tokens_out(half(0, tt % 2), ctxT, tt, w["lkvT"], 0, 2 * D).then_inc(sem("e_kv_ps"), 1)
                u = tt - 2
                if u == 0:
                    pe.wait_ge(sem("d_added"), T)
                if u >= 0:
                    bb, first, last_one = u // CTB, u % CTB == 0, u % CTB == CTB - 1
                    pe.wait_ge(sem("e_kv"), u + 1)
                    for cc in range(C):
                        last = nc.tensor.matmul(e_kv_bank(bb, cc), e_kv2[:, u, cc * P:(cc + 1) * P],
                                                e_kv2[:, u, D + cc * P:D + (cc + 1) * P], start=first, stop=last_one)
                    if last_one:
                        last.then_inc(sem("e_sum_ps"), 1)
                    pe.wait_ge(sem("e_kk"), u + 1)
                    for cc in range(C):
                        last = nc.tensor.matmul(half(2, cc)[:, bb:bb + 1], e_kk[:, u % 2, cc * P:(cc + 1) * P],
                                                ones[:, 0:1], start=first, stop=last_one)
                    last.then_inc(sem("e_kk_summed"), 1)
            pe.wait_ge(sem("e_sum"), B)
            transposes(tile_of(y), 6)
            pe.wait_ge(sem("yT_ready"), 7 * T)
            for g in range(C * B):
                cc, bb = g // B, g % B
                if g >= 2:
                    pe.wait_ge(sem("e_qelu"), g - 1)
                channels_out(half(0, g % 2), w["lqT"], cc * P, yT, bb * S, S).then_inc(sem("e_q_ps"), 1)
            pe.wait_ge(sem("e_qT"), C * B)
            pe.wait_ge(sem("e_sum"), B)
            for tt in range(T):
                if tt >= 2:
                    pe.wait_ge(sem("y_ready"), 7 * T + tt - 1)
                for cc in range(C):
                    nc.tensor.matmul(half(1, tt % 2)[:, cc * P:(cc + 1) * P], e_qT[:, cc, tt * P:(tt + 1) * P],
                                     e_kv[:, tt // TB, cc, :], start=True, stop=True)
                for cc in range(C):
                    last = nc.tensor.matmul(half(1, tt % 2)[:, D + cc * HC:D + (cc + 1) * HC],
                                            e_qq[:, cc, tt * P:(tt + 1) * P], headmask[:], start=True, stop=True)
                last.then_inc(sem("e_at_ps"), 1)
            transposes(tile_of(y), 7)
            for tt in range(T):
                pe.wait_ge(sem("yT_ready"), 7 * T + tt + 1)
                if tt >= 2:
                    pe.wait_ge(sem("e_added"), tt - 1)
                tokens_out(half(2, tt % 2)[:, 0:D], yT, tt, w["loT"], 0, D).then_inc(sem("e_out_ps"), 1)

            transposes(tile_of(y), 8)
            pe.wait_ge(sem("f_moments"), 1)
            n_terms = [(f_m2, f_iv), (f_m1s, f_mi)]
            for k_, (m, tab) in enumerate(n_terms):
                for cc in range(C):
                    nc.tensor.matmul(half(0, 0)[0:B, 0:E], m[:, cc, :], tab[:, cc, :],
                                     start=(k_ == 0 and cc == 0), stop=False)
            for cc in range(C):
                last = nc.tensor.matmul(half(0, 0)[0:B, 0:E], ones[:, 0:B], f_m2i[:, cc, :],
                                        start=False, stop=(cc == C - 1))
            last.then_inc(sem("f_loss_ps"), 1)
            for tt in range(T):
                if tt >= 2:
                    pe.wait_ge(sem("f_added"), tt - 1)
                tokens_out(bank[tt % 2][:, 0:D], yT, tt, w["baseT"], 0, D).then_inc(sem("f_out_ps"), 1)
            pe.wait_ge(sem("f_expert_loaded"), 16 * 6 * B)
            for bb in range(B):
                for ic in range(C):
                    last = nc.tensor.matmul(half(1, bb)[0:R, :], f_down[:, bb, ic, :], yT[:, ic, bb * S:(bb + 1) * S],
                                            start=(ic == 0), stop=(ic == C - 1))
                last.then_inc(sem("f_h_ps"), 1)
            for bb in range(B):
                pe.wait_ge(sem("f_hT"), bb + 1)
                for cc in range(C):
                    g = bb * C + cc
                    if g >= 2:
                        pe.wait_ge(sem("f_aT"), g - 1)
                    nc.tensor.matmul(half(2, g % 2), f_up[0:R, bb, cc * P:(cc + 1) * P], f_hT[0:R, bb * S:(bb + 1) * S],
                                     start=True, stop=True).then_inc(sem("f_a_ps"), 1)
            for tt in range(T):
                bb = tt // TB
                pe.wait_ge(sem("f_aT"), C * (bb + 1))
                pe.wait_ge(sem("f_added"), T + tt - 1 if tt >= 2 else T)
                dst = bank[tt % 2][:, 0:D]
                for ic in range(C):
                    last = nc.tensor.matmul(dst, f_aT[:, ic, tt * P:(tt + 1) * P], f_conv[:, bb, ic, :],
                                            start=(ic == 0), stop=(ic == C - 1))
                last.then_inc(sem("f_out_ps"), 1)

        @block.scalar
        def _(act):
            def roots(n):
                act.wait_ge(sem("ln_var"), n)
                nc.scalar.activation(sd[:], var[:], ACT.Sqrt).then_inc(sem("ln_sd"), 1)

            def copy_T(n, scales=None):
                for tt in range(T):
                    act.wait_ge(sem("y_turned"), n * T + tt + 1)
                    if scales is None:
                        nc.scalar.activation(yT[:, :, tt * P:(tt + 1) * P],
                                             bank[tt % 2][:, 0:D].rearrange("p (c n) -> p c n", c=C),
                                             ACT.Copy).then_inc(sem("yT_ready"), 1)
                    else:
                        nc.scalar.activation(yT[:, 0, tt * P:(tt + 1) * P], bank[tt % 2][:, 0:P], ACT.Copy,
                                             scale=cols[scales][:, 0:1])
                        nc.scalar.activation(yT[:, 1, tt * P:(tt + 1) * P], bank[tt % 2][:, P:D], ACT.Copy,
                                             scale=cols[scales][:, 1:2]).then_inc(sem("yT_ready"), 1)

            act.wait_ge(sem("const_loaded"), 16 * 14)
            roots(1)
            for tt in range(T):
                act.wait_ge(sem("a_ln"), tt + 1)
                if tt >= 2:
                    act.wait_ge(sem("act_sq"), tt - 1)
                nc.scalar.activation(sq[:, tt % 2, 0:D], xin[:, tt, :], ACT.Square,
                                     accum_out=var[:, tt:tt + 1]).then_inc(sem("act_sq"), 1)
            act.wait_ge(sem("act_sq"), T)
            nc.scalar.activation(sd[:], var[:], ACT.Sqrt).then_inc(sem("a_norm"), 1)
            copy_T(0, "scale1")
            for g in range(C * B):
                cc, bb = g // B, g % B
                act.wait_ge(sem("a_q_ps"), g + 1)
                nc.scalar.activation(sq[:, g % 2, :], half(0, g % 2), ACT.Square).then_inc(sem("act_sq"), 1)
                act.wait_ge(sem("act_sq"), T + g + 1)
                nc.scalar.activation(a_qT[:, cc, bb * S:(bb + 1) * S], sq[:, g % 2, :], ACT.Exp,
                                     scale=-0.5).then_inc(sem("a_qT"), 1)
            for tt in range(T):
                act.wait_ge(sem("a_kv_ps"), tt + 1)
                if tt < 2:
                    act.wait_ge(sem("a_qT"), C * B)
                nc.scalar.activation(sq[:, tt % 2, 0:D], half(1, tt % 2)[:, 0:D], ACT.Square).then_inc(sem("act_sq"), 1)
                nc.scalar.activation(a_v[:, tt, :, 0:P], half(1, tt % 2)[:, D:2 * D].rearrange("p (c n) -> p c n", c=C),
                                     ACT.Copy)
                act.wait_ge(sem("act_sq"), T + C * B + tt + 1)
                nc.scalar.activation(a_k[:, tt, :], sq[:, tt % 2, 0:D], ACT.Exp, scale=-0.5).then_inc(sem("a_kv"), 1)
            copy_T(1)
            for tt in range(T):
                act.wait_ge(sem("a_x1"), tt + 1)
                act.wait_ge(sem("a_kv"), T)
                if tt >= 2:
                    act.wait_ge(sem("act_sq"), 2 * T + C * B + tt - 1)
                nc.scalar.activation(sq[:, tt % 2, 0:D], a_x1[:, tt, :], ACT.Square,
                                     accum_out=var[:, tt:tt + 1]).then_inc(sem("act_sq"), 1)
            act.wait_ge(sem("act_sq"), 3 * T + C * B)
            nc.scalar.activation(sd[:], var[:], ACT.Sqrt).then_inc(sem("a_norm"), 1)
            copy_T(2, "scale2")
            for g in range(MC * B):
                m, bb = g // B, g % B
                act.wait_ge(sem("a_h_ps"), g + 1)
                nc.scalar.activation(a_hT[:, m, bb * S:(bb + 1) * S], half(1, g % 2), ACT.Gelu,
                                     bias=cols["conv1_b"][:, m:m + 1]).then_inc(sem("a_hT"), 1)

            act.wait_ge(sem("w_rounded"), 3)
            roots(2)
            copy_T(3)
            def b_split1(g):
                act.wait_ge(sem("b_q_ps" if g < C * B else "b_k_ps"), g + 1 if g < C * B else g - C * B + 1)
                if g >= 4:
                    act.wait_ge(sem(f"b_stored{g % 4}"), 16 * (g // 4))
                nc.scalar.activation(b_part[:, g % 4, 0, :], half(0 if g < C * B else 1, g % 2), ACT.Copy,
                                     scale=DH ** -0.5 if g < C * B else 1.0).then_inc(sem("b_part1"), 1)

            b_split1(0)
            for g in range(C * B * 3):
                if g + 1 < C * B * 3:
                    b_split1(g + 1)
                act.wait_ge(sem("b_rest"), g + 1)
                nc.scalar.activation(b_part[:, g % 4, 1, :], b_rest[:, g % 2, :], ACT.Copy).then_inc(sem("b_part2"), 1)

            def b_copy(i, j, k):
                act.wait_ge(sem("b_scores"), i * 8 + (2 * j + k + 1))
                wait(act, "b_weights", i * 8 + (2 * j + k - 7))
                nc.scalar.activation(b_x[:, (2 * j + k) % 8, :], wide[k][:], ACT.Copy).then_inc(sem("b_s_copied"), 1)

            def b_exp(i, j):
                act.wait_ge(sem("b_cand"), i * 4 + (j + 1))
                for k in range(2):
                    n = 2 * j + k
                    nc.scalar.activation(b_x[:, n, :], b_x[:, n, :], ACT.Exp, bias=b_neg[:, k:k + 1],
                                         accum_out=b_all[:, j, k:k + 1]).then_inc(sem("b_exp"), 1)

            def b_signs(i, j):
                act.wait_ge(sem("b_top56"), i * 8 + (2 * j + 2))
                for k in range(2):
                    ins = nc.scalar.activation(b_te[:, k:k + 1], b_m8[:, k, 7:8], ACT.Exp, bias=b_neg[:, k:k + 1])
                ins.then_inc(sem("b_te"), 1)
                act.wait_ge(sem("b_te"), i * 4 + (j + 1))
                for k in range(2):
                    nc.scalar.activation(b_sgn[:, k, :], b_x[:, 2 * j + k, :], ACT.Sign, scale=-1.0,
                                         bias=b_te[:, k:k + 1]).then_inc(sem("b_signs"), 1)
                    act.wait_ge(sem("b_signs"), i * 8 + (2 * j + k + 1))
                    wait(act, "b_z", i * 8 + (2 * j + k - 1))
                    nc.scalar.activation(b_m[:, k, :], b_sgn[:, k, :], ACT.Relu,
                                         accum_out=b_cnt[:, j % 2, k:k + 1]).then_inc(sem("b_mask"), 1)

            def b_weights(i, j, k):
                n = 2 * j + k
                for hh in range(2):
                    act.wait_ge(sem("b_tr"), i * 16 + (2 * n + hh + 1))
                    if k == 0 and hh == 0:
                        wait(act, "b_o_ps", i * 4 + j)
                    nc.scalar.activation(b_pT[:, k, 512 * hh:512 * hh + 512], half(2, hh), ACT.Copy).then_inc(sem("b_pT"), 1)

            def b_slot(i, j, now=True, more=True):
                old = back(i, j, 2)
                if more:
                    for k in range(2):
                        b_copy(i, j + 1, k)
                if now:
                    b_exp(i, j)
                    b_signs(i, j)
                if old:
                    for k in range(2):
                        b_weights(*old, k)

            for k in range(2):
                b_copy(0, 0, k)
            for j in range(4):
                b_slot(0, j)
            with act.Fori(1, PAIRS // 4 - 1) as i:
                for j in range(4):
                    b_slot(i, j)
            for j in range(4):
                b_slot(PAIRS // 4 - 1, j, more=j < 3)
            for j in range(2):
                b_slot(PAIRS // 4, j, now=False, more=False)
            act.wait_ge(sem("b_flag"), 1)
            with act.If(act.value_load(b_flag[0:1, 0:1], min_val=0, max_val=2 * P) > 0):
                with act.Fori(0, B * H // 2) as i:
                    for j in range(2 * TB):
                        act.wait_ge(sem("g_scores"), i * 8 + (j + 1))
                        if j >= 2:
                            act.wait_ge(sem("g_exp"), i * 8 + (j - 1))
                            act.wait_ge(sem("g_probs"), i * 8 + (j - 1))
                        nc.scalar.activation(g_s[:, j % 2, :], wide[j % 2][:], ACT.Copy).then_inc(sem("g_s_copied"), 1)
                        act.wait_ge(sem("g_neg"), i * 8 + (j + 1))
                        nc.scalar.activation(g_e[:, j % 2, :], g_s[:, j % 2, :], ACT.Exp, bias=g_neg[:, j % 2, :],
                                             accum_out=g_all[:, j % 2, :]).then_inc(sem("g_exp"), 1)
                        if j >= 1:
                            act.wait_ge(sem("g_p_tr"), i * 8 + j)
                            if j >= 3:
                                act.wait_ge(sem("g_o_ps"), i * 8 + (j - 2))
                            nc.scalar.activation(b_pT[:, (j - 1) % 2, :], wide[2][:], ACT.Copy).then_inc(sem("g_pT"), 1)
                    act.wait_ge(sem("g_p_tr"), i * 8 + 8)
                    act.wait_ge(sem("g_o_ps"), i * 8 + 6)
                    nc.scalar.activation(b_pT[:, 1, :], wide[2][:], ACT.Copy).then_inc(sem("g_pT"), 1)
                    act.wait_ge(sem("g_o"), i * 8 + 8)

            roots(3)
            for tt in range(T):
                act.wait_ge(sem("c_g_ps"), tt + 1)
                if tt >= 2:
                    act.wait_ge(sem("c_h"), tt - 1)
                nc.scalar.activation(c_g[:, tt % 2, :], wide[0][:], ACT.Silu, scale=c_ag[:, tt:tt + 1]).then_inc(sem("c_g"), 1)

            roots(4)
            copy_T(4)
            for m in range(C * B * 2 + 1):
                if m < C * B * 2:
                    act.wait_ge(sem("d_val"), m + 1)
                    if m >= 4:
                        act.wait_ge(sem(f"d_stored{m % 4}"), 16 * (m // 4))
                    nc.scalar.activation(d_part[:, m % 4, 0, :], d_val[:, m % 2, :], ACT.Copy).then_inc(sem("d_part1"), 1)
                if m >= 1:
                    act.wait_ge(sem("d_rest"), m)
                    nc.scalar.activation(d_part[:, (m - 1) % 4, 1, :], d_rest[:, (m - 1) % 2, :], ACT.Copy).then_inc(sem("d_part2"), 1)

            def d_exp(i, j, qt):
                n = (qt + 1) * P
                if qt == 0:
                    act.wait_ge(sem("d_neg"), i * 2 + (j + 1))
                wait(act, "d_p_tr", i * 8 + (TB * (j - 2) + qt + 1))
                nc.scalar.activation(d_p[:, j % 2, qt, 0:n], d_s[:, j % 2, qt, 0:n], ACT.Exp,
                                     bias=d_neg[:, j % 2, qt:qt + 1]).then_inc(sem("d_p"), 1)

            def d_weights(i, j, qt):
                n = (qt + 1) * P
                act.wait_ge(sem("d_p_tr"), i * 8 + (TB * j + qt + 1))
                if qt == 0:
                    wait(act, "d_oT_ps", i * 2 + j)
                nc.scalar.activation(d_pT[:, 0:qt + 1, qt * P:n], half(2, qt % 2)[:, 0:n].rearrange("p (k q) -> p k q", q=P),
                                     ACT.Copy).then_inc(sem("d_pT"), 1)

            def d_outputs(i, j):
                act.wait_ge(sem("d_oT_ps"), i * 2 + (j + 1))
                wait(act, "d_o_ps", i * 2 + (j - 1))
                nc.scalar.activation(d_oT[0:V1, j % 2, :], bank[0][0:V1, :], ACT.Copy).then_inc(sem("d_oT"), 1)

            def d_slots(i, last=False):
                for j in range(2):
                    for qt in range(TB):
                        d_weights(i, j, qt)
                    if not (last and j == 1):
                        for qt in range(TB):
                            d_exp(i, j + 1, qt)
                    d_outputs(i, j)

            for qt in range(TB):
                d_exp(0, 0, qt)
            d_slots(0)
            with act.Fori(1, B * H // 2 - 1) as i:
                d_slots(i)
            d_slots(B * H // 2 - 1, last=True)
            copy_T(5)

            for tt in range(CT + 1):
                if tt < CT:
                    act.wait_ge(sem("e_kmin"), tt + 1)
                    if tt >= 2:
                        act.wait_ge(sem("e_kv"), tt - 1)
                    nc.scalar.activation(e_t[:, tt % 2, D:2 * D], e_t[:, tt % 2, 0:D], ACT.Exp).then_inc(sem("e_kexp"), 1)
                u = tt - 1
                if u >= 0:
                    act.wait_ge(sem("e_kv"), u + 1)
                    if u >= 2:
                        act.wait_ge(sem("e_kk_summed"), u - 1)
                    nc.scalar.activation(e_kk[:, u % 2, :], e_kv2[:, u, 0:D], ACT.Square).then_inc(sem("e_kk"), 1)
            act.wait_ge(sem("e_kk_summed"), CT)
            for cc in range(C):
                nc.scalar.activation(e_kn[:, cc * B:(cc + 1) * B], half(2, cc)[:, 0:B], ACT.Sqrt,
                                     scale=float(S)).then_inc(sem("e_kn"), 1)
            roots(5)
            copy_T(6)
            for g in range(C * B):
                cc, bb = g // B, g % B
                act.wait_ge(sem("e_qmin"), g + 1)
                nc.scalar.activation(e_qq[:, cc, bb * S:(bb + 1) * S], sq[:, g % 2, :], ACT.Exp).then_inc(sem("e_qexp"), 1)
            for g in range(C * B):
                cc, bb = g // B, g % B
                act.wait_ge(sem("e_qelu"), g + 1)
                nc.scalar.activation(e_qq[:, cc, bb * S:(bb + 1) * S], e_qT[:, cc, bb * S:(bb + 1) * S],
                                     ACT.Square).then_inc(sem("e_qT"), 1)
            for tt in range(T):
                act.wait_ge(sem("e_at_ps"), tt + 1)
                if tt >= 2:
                    act.wait_ge(sem("y_ready"), 7 * T + tt - 1)
                nc.scalar.activation(e_qn[:, tt % 2], half(1, tt % 2)[:, D:D + H].rearrange("p (c h) -> p c h", c=C),
                                     ACT.Sqrt, scale=float(DH)).then_inc(sem("e_qn"), 1)
            copy_T(7)

            roots(6)
            copy_T(8)
            for bb in range(B):
                act.wait_ge(sem("f_h_ps"), bb + 1)
                nc.scalar.activation(f_hT[0:R, bb * S:(bb + 1) * S], half(1, bb)[0:R, :], ACT.Relu,
                                     bias=f_db[0:R, bb:bb + 1]).then_inc(sem("f_hT"), 1)
            for g in range(C * B):
                bb, cc = g // C, g % C
                act.wait_ge(sem("f_a_ps"), g + 1)
                nc.scalar.activation(f_aT[:, cc, bb * S:(bb + 1) * S], half(2, g % 2), ACT.Identity,
                                     bias=f_ub[:, bb, cc:cc + 1]).then_inc(sem("f_aT"), 1)

        @block.gpsimd
        def _(pool):
            pool.wait_ge(sem("w_mean"), 1)
            for n in range(3):
                nc.gpsimd.tensor_scalar(w_raw[n], w_raw[n], w_scale[:, n:n + 1], 1.0, ALU.mult, ALU.mult).then_inc(sem("pool_step"), 1)
                pool.wait_ge(sem("pool_step"), 2 * n + 1)
                nc.gpsimd.tensor_scalar(w_raw[n], w_raw[n], ROUND, 1.0, ALU.add, ALU.mult).then_inc(sem("pool_step"), 1)
                pool.wait_ge(sem("pool_step"), 2 * n + 2)
                nc.gpsimd.tensor_scalar(w_raw[n], w_raw[n], -ROUND, 1.0, ALU.add, ALU.mult).then_inc(sem("w_whole"), 1)

            def b_below(i, j):
                for k in range(2):
                    n = (2 * j + k) % 4
                    wait(pool, "b_tr", i * 16 + 2 * (2 * j + k - 3))
                    pool.wait_ge(sem("b_mask"), i * 8 + (2 * j + k + 1))
                    nc.gpsimd.tensor_tensor(b_z[:, n, :], b_x[:, 2 * j + k, :], b_m[:, k, :], ALU.mult).then_inc(sem("b_z"), 1)

            def b_chosen(i, j):
                for k in range(2):
                    n = (2 * j + k) % 4
                    pool.wait_ge(sem("b_final"), i * 8 + (2 * j + k + 1))
                    nc.gpsimd.tensor_tensor(b_z[:, n, :], b_x[:, 2 * j + k, :], b_z[:, n, :], ALU.subtract).then_inc(sem("b_weights"), 1)

            def b_slot(i, j, now=True):
                old = back(i, j, 2)
                if old:
                    b_chosen(*old)
                if now:
                    b_below(i, j)

            for j in range(4):
                b_slot(0, j)
            with pool.Fori(1, PAIRS // 4) as i:
                for j in range(4):
                    b_slot(i, j)
            for j in range(2):
                b_slot(PAIRS // 4, j, now=False)

        @block.vector
        def _(dve):
            steps = [0]

            def link(ins):
                steps[0] += 1
                ins.then_inc(sem("dve_step"), 1)
                dve.wait_ge(sem("dve_step"), steps[0])

            def gate(k=0):
                nc.vector.tensor_copy(gate_out[:, k:k + 1], w_abs[:, 0:1])

            def layer_norm(n, dst, done):
                for tt in range(T):
                    ins = nc.vector.bn_stats(bn[:, tt, :], x[:, tt, :])
                link(ins)
                for tt in range(T):
                    ins = nc.vector.bn_aggr(mv[:, tt, :], bn[:, tt, :])
                link(ins)
                nc.vector.tensor_scalar(var[:], mv[:, :, 1], LN_EPS, None, ALU.add).then_inc(sem("ln_var"), 1)
                dve.wait_ge(sem("ln_sd"), n)
                link(nc.vector.reciprocal(rstd[:], sd[:]))
                for tt in range(T):
                    nc.vector.tensor_scalar(dst[:, tt, :], x[:, tt, :], mv[:, tt, 0:1], rstd[:, tt:tt + 1],
                                            ALU.subtract, ALU.mult).then_inc(sem(done), 1)

            def rms_scale(src, n):
                dve.wait_ge(sem("a_norm"), n)
                link(nc.vector.reciprocal(rstd[:], sd[:]))
                link(nc.vector.tensor_scalar(rstd[:], rstd[:], RMS_GAIN, None, ALU.mult))
                for tt in range(T):
                    nc.vector.tensor_scalar(y[:, tt, :], src[:, tt, :], rstd[:, tt:tt + 1], None,
                                            ALU.mult).then_inc(sem("y_ready"), 1)

            nc.vector.memset(ones[:], 1.0).then_inc(sem("ones_set"), 1)
            nc.vector.memset(a_v[:, :, :, P:P + 1], 1.0).then_inc(sem("a_vones"), 1)
            dve.wait_ge(sem("const_loaded"), 16 * 14)
            nc.vector.tensor_scalar(negident[:], ident[:], -1.0, None, ALU.mult)
            link(nc.vector.tensor_copy(ident_bf[:], ident[:]))
            dve.wait_ge(sem("x_loaded"), 16)

            layer_norm(1, xin, "a_ln")
            rms_scale(xin, 1)
            dve.wait_ge(sem("w_raw_loaded"), 48)
            for n in range(3):
                ins = nc.vector.tensor_reduce(w_abs[:, n:n + 1], w_raw[n], AX.X, ALU.add, apply_absolute_value=True)
            ins.then_inc(sem("w_abs"), 1)
            for bb in range(B):
                dve.wait_ge(sem("a_kvsum_ps"), bb + 1)
                for cc in range(C):
                    ps = half(2, bb)[:, cc * KV:(cc + 1) * KV]
                    nc.vector.tensor_tensor(a_kv[:, bb, cc, 0:P], ps[:, 0:P], blockmask[:], ALU.mult)
                    ins = nc.vector.tensor_scalar(a_kv[:, bb, cc, P:KV], headmask[:], ps[:, P:P + 1], None, ALU.mult)
                ins.then_inc(sem("a_kvsum"), 1)
            dve.wait_ge(sem("w_abs_ps"), 1)
            link(nc.vector.tensor_scalar(w_mean[:], half(0, 0)[:, 0:3], 1.0 / (D * INNER), 1e-5, ALU.mult, ALU.max))
            nc.vector.reciprocal(w_scale[:], w_mean[:]).then_inc(sem("w_mean"), 1)
            for tt in range(T):
                dve.wait_ge(sem("a_at_ps"), tt + 1)
                ps = bank[tt % 2][:, 0:C * KV].rearrange("p (c k) -> p c k", c=C)
                link(nc.vector.tensor_scalar(a_den[:, tt % 2], ps[:, :, P:KV], 1e-6, None, ALU.add))
                link(nc.vector.reciprocal(a_z, a_den[:, tt % 2]))
                for cc in range(C):
                    ins = nc.vector.tensor_tensor(y[:, tt, cc * P:(cc + 1) * P].rearrange("p (h e) -> p h e", h=HC),
                                            ps[:, cc, 0:P].rearrange("p (h e) -> p h e", h=HC),
                                            a_z[:, cc, :].unsqueeze(2).broadcast_to([P, HC, DH]),
                                            ALU.mult)
                ins.then_inc(sem("y_ready"), 1)
            for tt in range(T):
                dve.wait_ge(sem("a_proj_ps"), tt + 1)
                link(nc.vector.tensor_tensor(a_tmp[:, tt % 2, :], half(0, tt % 2)[:, 0:D], gamma[:], ALU.mult))
                nc.vector.tensor_tensor(a_x1[:, tt, :], a_tmp[:, tt % 2, :], xin[:, tt, :], ALU.add).then_inc(sem("a_x1"), 1)
            rms_scale(a_x1, 2)
            for n, wq in enumerate((wq_gate, wq_up, wq_down)):
                dve.wait_ge(sem("w_whole"), n + 1)
                nc.vector.tensor_scalar(wq[:].rearrange("p a b -> p (a b)"), w_raw[n], 1.0, -1.0,
                                        ALU.min, ALU.max).then_inc(sem("w_rounded"), 1)
            for tt in range(T):
                dve.wait_ge(sem("a_mlp_ps"), tt + 1)
                link(nc.vector.tensor_tensor(a_tmp[:, tt % 2, :], half(2, tt % 2)[:, 0:D], gamma[:], ALU.mult))
                link(nc.vector.tensor_tensor(a_tmp[:, tt % 2, :], a_tmp[:, tt % 2, :], a_x1[:, tt, :], ALU.add))
                ins = nc.vector.tensor_tensor(x[:, tt, :], x[:, tt, :], a_tmp[:, tt % 2, :], ALU.add)
                ins.then_inc(sem("a_added"), 1)
            dve.wait_ge(sem("a_added"), T)

            layer_norm(2, y, "y_ready")

            def b_split3(g):
                dve.wait_ge(sem("b_part2"), g + 1)
                nc.vector.tensor_tensor(b_part[:, g % 4, 2, :], b_rest[:, g % 2, :], b_part[:, g % 4, 1, :],
                                        ALU.subtract).then_inc(sem("b_part3"), 1)

            for g in range(C * B * 3):
                if g >= 2:
                    b_split3(g - 2)
                    dve.wait_ge(sem("b_part3"), g - 1)
                dve.wait_ge(sem("b_part1"), g + 1)
                nc.vector.scalar_tensor_tensor(out=b_rest[:, g % 2, :], in0=half(0 if g < C * B else 1, g % 2),
                                               scalar=DH ** -0.5 if g < C * B else 1.0, in1=b_part[:, g % 4, 0, :],
                                               op0=ALU.mult, op1=ALU.subtract).then_inc(sem("b_rest"), 1)
            for g in range(C * B * 3 - 2, C * B * 3):
                b_split3(g)
            step = [0]

            def stepped(ins):
                step[0] += 1
                ins.then_inc(sem("b_step"), 1)
                return step[0]

            def after(value):
                dve.wait_ge(sem("b_step"), value)

            def b_candidates(i, j):
                there = [0, 0]
                for k in range(2):
                    for blk in range(NBLK):
                        ins = nc.vector.max(b_cand[:, k, 8 * blk:8 * blk + 8],
                                            b_x[:, 2 * j + k, BLK * blk:BLK * (blk + 1)])
                    there[k] = stepped(ins)
                return there

            def b_rounds(cut):
                for r in range(NTOP - 1):
                    m8 = b_m8 if r else b_top8
                    found = [0, 0]
                    for k in range(2):
                        after(cut[k])
                        ins = nc.vector.max(m8[:, k, :], b_cand[:, k, :])
                        if r == NTOP - 2:
                            ins.then_inc(sem("b_top56"), 1)
                        else:
                            found[k] = stepped(ins)
                    if r < NTOP - 2:
                        for k in range(2):
                            after(found[k])
                            if r == 0 and k == 1:
                                nc.vector.tensor_scalar(b_neg, b_top8[:, :, 0], -1.0, None, ALU.mult).then_inc(sem("b_cand"), 1)
                            cut[k] = stepped(nc.vector.match_replace(b_cand[:, k, :], m8[:, k, :], b_cand[:, k, :], MARK))

            def b_slot(i, j, now=True):
                if step[0]:
                    after(step[0])
                    dve.sem_clear(sem("b_step"))
                step[0] = 0
                one, four = back(i, j, 1), back(i, j, 4)
                if not now and j > 0:
                    one = None
                if now:
                    wait(dve, "b_te", i * 4 + j)
                if four:
                    i4, j4 = four
                    dve.wait_ge(sem("b_o_ps"), i4 * 4 + (j4 + 1))
                if now:
                    dve.wait_ge(sem("b_s_copied"), i * 8 + (2 * j + 2))
                if four:
                    ps = bank[j4 % 2][:, 0:2 * V1].rearrange("p (k v) -> p k v", k=2)
                    den = stepped(nc.vector.scalar_tensor_tensor(out=b_den, in0=b_all[:, j4, :], scalar=1e-9, in1=ps[:, :, DH],
                                                                 op0=ALU.mult, op1=ALU.add))
                else:
                    gate()
                if now:
                    there = b_candidates(i, j)
                if four:
                    after(den)
                    inv = stepped(nc.vector.reciprocal(b_r, b_den))
                if now:
                    b_rounds(there)
                if four:
                    after(inv)
                    nc.vector.tensor_tensor(b_o[:, bass.ds((i4 * 4 + j4) * (2 * DH), 2 * DH)].rearrange("p (k e) -> p k e", k=2),
                                            ps[:, :, 0:DH], b_r.unsqueeze(2).broadcast_to([P, 2, DH]),
                                            ALU.mult).then_inc(sem("b_out"), 1)
                if one:
                    i1, j1 = one
                    dve.wait_ge(sem("b_z"), i1 * 8 + (2 * j1 + 2))
                    stepped(nc.vector.tensor_tensor(b_least, b_least, b_cnt[:, j1 % 2, :], ALU.min))
                    next8, kept = [0, 0], [0, 0]
                    for k in range(2):
                        next8[k] = stepped(nc.vector.max(b_f8[:, k, :], b_z[:, (2 * j1 + k) % 4, :]))
                    for k in range(2):
                        after(next8[k])
                        kept[k] = stepped(nc.vector.scalar_tensor_tensor(
                            out=b_g8[:, k, :], in0=below[:], scalar=b_cnt[:, j1 % 2, k:k + 1], in1=b_f8[:, k, :],
                            op0=ALU.is_lt, op1=ALU.mult))
                    for k in range(2):
                        n = (2 * j1 + k) % 4
                        after(kept[k])
                        nc.vector.match_replace(b_z[:, n, :], b_g8[:, k, :], b_z[:, n, :], 0.0).then_inc(sem("b_final"), 1)

            link(nc.vector.memset(b_least, float(SC)))
            for j in range(4):
                b_slot(0, j)
            with dve.Fori(1, PAIRS // 4) as i:
                for j in range(4):
                    b_slot(i, j)
            for j in range(4):
                b_slot(PAIRS // 4, j, now=False)
            dve.wait_ge(sem("b_out"), PAIRS)
            nc.vector.tensor_scalar(b_bad, b_least, float(SC - K_TOP), None, ALU.is_lt).then_inc(sem("b_bad"), 1)
            dve.wait_ge(sem("b_bad_ps"), 1)
            link(nc.vector.tensor_reduce(b_flagf[:], bank[0][:, 0:2], AX.X, ALU.add))
            nc.vector.tensor_copy(b_flag[:], b_flagf[:]).then_inc(sem("b_flag"), 1)
            dve.wait_ge(sem("b_flag"), 1)
            with dve.If(dve.value_load(b_flag[0:1, 0:1], min_val=0, max_val=2 * P) > 0):
                DS = 2 * NTOP + 2
                with dve.Fori(0, B * H // 2) as i:
                    def chain(ins, k):
                        ins.then_inc(sem("g_step"), 1)
                        dve.wait_ge(sem("g_step"), k)

                    def top(j):
                        s, z, m8 = g_s[:, j % 2, :], b_z[:, j % 2, :], g_max[:, j % 2]
                        dve.wait_ge(sem("g_s_copied"), i * 8 + (j + 1))
                        gate()
                        dve.sem_clear(sem("g_step"))
                        chain(nc.vector.max(m8[:, 0, :], s), 1)
                        nc.vector.tensor_scalar(g_neg[:, j % 2, :], m8[:, 0, 0:1], -1.0, None,
                                                ALU.mult).then_inc(sem("g_neg"), 1)
                        chain(nc.vector.match_replace(z, m8[:, 0, :], s, MARK), 2)
                        for r in range(1, NTOP):
                            chain(nc.vector.max(m8[:, r, :], z), 2 * r + 1)
                            ins = nc.vector.match_replace(z, m8[:, r, :], z, MARK)
                            chain(ins, 2 * r + 2)

                    def probs(j):
                        dve.wait_ge(sem("g_exp"), i * 8 + (j + 1))
                        if j >= 2:
                            dve.wait_ge(sem("g_p_tr"), i * 8 + (j - 1))
                        nc.vector.scalar_tensor_tensor(out=g_w[:, j % 2, :], in0=b_z[:, j % 2, :], scalar=MARK,
                                                       in1=g_e[:, j % 2, :], op0=ALU.is_equal, op1=ALU.mult,
                                                       accum_out=g_top[:, j % 2, :]).then_inc(sem("g_probs"), 1)
                        dve.wait_ge(sem("g_probs"), i * 8 + (j + 1))
                        chain(nc.vector.scalar_tensor_tensor(out=g_den[:, j % 2, :], in0=g_all[:, j % 2, :], scalar=1e-9,
                                                             in1=g_top[:, j % 2, :], op0=ALU.mult, op1=ALU.add), DS - 1)
                        chain(nc.vector.reciprocal(g_r[:, j % 2, :], g_den[:, j % 2, :]), DS)

                    def out(j):
                        dve.wait_ge(sem("g_o_ps"), i * 8 + (j + 1))
                        nc.vector.tensor_scalar(b_o[:, bass.ds((i * 8 + j) * DH, DH)], bank[0][:, 0:DH],
                                                g_r[:, j % 2, :], None, ALU.mult).then_inc(sem("g_o"), 1)

                    for j in range(2 * TB):
                        top(j)
                        probs(j)
                        if j >= 1:
                            out(j - 1)
                    out(2 * TB - 1)
                dve.wait_ge(sem("g_o"), B * H * TB)
            o4 = b_o.rearrange("p (b h q e) -> p b h q e", b=B, h=H, q=TB)
            for tt in range(T):
                xv = x[:, tt, :].rearrange("p (h e) -> p h e", h=H)
                nc.vector.tensor_tensor(xv, xv, o4[:, tt // TB, :, tt % TB, :], ALU.add).then_inc(sem("b_added"), 1)
            dve.wait_ge(sem("b_added"), T)

            layer_norm(3, y, "c_y")
            dve.wait_ge(sem("c_y"), T)

            def absmax(dst, src):
                return nc.vector.tensor_reduce(dst, src, AX.X, ALU.max, apply_absolute_value=True)

            link(absmax(c_am, y[:]))
            link(nc.vector.tensor_scalar(c_am1, c_am, 1e-5, None, ALU.max))
            link(nc.vector.reciprocal(c_s, c_am1))
            link(nc.vector.tensor_scalar(c_s, c_s, 127.0, None, ALU.mult))
            link(nc.vector.tensor_scalar(c_si, c_am1, 1.0 / 127.0, None, ALU.mult))
            nc.vector.tensor_scalar(c_ag, c_si, w_mean[:, 0:1], None, ALU.mult)
            link(nc.vector.tensor_scalar(c_au, c_si, w_mean[:, 1:2], None, ALU.mult))

            def xq_T(tt):
                dve.wait_ge(sem("c_xq_tr"), tt + 1)
                nc.vector.tensor_scalar(c_qT[:, :, tt * P:(tt + 1) * P],
                                        bank[tt % 2][:, 0:P].bitcast(BF16).rearrange("p (c n) -> p c n", c=C),
                                        127.0, -128.0, ALU.min, ALU.max).then_inc(sem("c_xqT"), 1)

            for tt in range(T):
                link(nc.vector.tensor_scalar(c_q[:, tt % 2, :], y[:, tt, :], c_s[:, tt:tt + 1], ROUND, ALU.mult, ALU.add))
                if tt >= 2:
                    dve.wait_ge(sem("c_xq_tr"), tt - 1)
                nc.vector.tensor_scalar(c_qb[:, tt % 2, :], c_q[:, tt % 2, :], ROUND, None, ALU.subtract).then_inc(sem("c_xq"), 1)
                if tt >= 1:
                    xq_T(tt - 1)
            xq_T(T - 1)

            def c_turned(tt):
                dve.wait_ge(sem("c_h_tr"), tt + 1)
                nc.vector.tensor_scalar(c_hT[:, tt % 2], half(2, tt % 2).bitcast(BF16).rearrange("p (k n) -> p k n", k=KC),
                                        127.0, -128.0, ALU.min, ALU.max).then_inc(sem("c_hT"), 1)

            def c_add(tt):
                dve.wait_ge(sem("c_d_ps"), tt + 1)
                dve.wait_ge(sem("c_ad"), tt + 1)
                nc.vector.scalar_tensor_tensor(out=x[:, tt, :], in0=bank[tt % 2][:, 0:D], scalar=c_ad[:, tt:tt + 1],
                                               in1=x[:, tt, :], op0=ALU.mult, op1=ALU.add).then_inc(sem("c_added"), 1)

            for tt in range(T):
                dve.wait_ge(sem("c_g"), tt + 1)
                dve.wait_ge(sem("c_u_ps"), tt + 1)
                nc.vector.scalar_tensor_tensor(out=c_h[:, tt % 2, :], in0=wide[1][:], scalar=c_au[:, tt:tt + 1],
                                               in1=c_g[:, tt % 2, :], op0=ALU.mult, op1=ALU.mult).then_inc(sem("c_h"), 1)
                if tt >= 1:
                    c_turned(tt - 1)
                dve.wait_ge(sem("c_h"), tt + 1)
                link(absmax(c_hm[:, tt:tt + 1], c_h[:, tt % 2, :]))
                link(nc.vector.tensor_scalar(c_hm1[:, tt:tt + 1], c_hm[:, tt:tt + 1], 1e-5, None, ALU.max))
                link(nc.vector.reciprocal(c_hs[:, tt:tt + 1], c_hm1[:, tt:tt + 1]))
                link(nc.vector.tensor_scalar(c_hi[:, tt:tt + 1], c_hs[:, tt:tt + 1], 127.0, None, ALU.mult))
                nc.vector.tensor_scalar(c_ad[:, tt:tt + 1], c_hm1[:, tt:tt + 1], w_mean[:, 2:3], 1.0 / 127.0, ALU.mult, ALU.mult).then_inc(sem("c_ad"), 1)
                link(nc.vector.tensor_scalar(c_hr, c_h[:, tt % 2, :], c_hi[:, tt:tt + 1], ROUND, ALU.mult, ALU.add))
                if tt >= 2:
                    dve.wait_ge(sem("c_h_tr"), tt - 1)
                nc.vector.tensor_scalar(c_hb[:, tt % 2, :], c_hr, ROUND, None, ALU.subtract).then_inc(sem("c_hq"), 1)
                if tt >= 1:
                    c_add(tt - 1)
            c_turned(T - 1)
            c_add(T - 1)
            dve.wait_ge(sem("c_added"), T)

            def bias_to_x(name, normed):
                dve.wait_ge(sem("y_ready"), normed)
                for tt in range(T):
                    ins = nc.vector.tensor_tensor(x[:, tt, :], x[:, tt, :], spread[name], ALU.add)
                link(ins)

            layer_norm(4, y, "y_ready")
            dve.wait_ge(sem("spread_loaded"), 16 * len(spread))
            bias_to_x("ao_b", 5 * T)
            for m in range(C * B * 2 + 2):
                if m < C * B * 2:
                    dve.wait_ge(sem("d_qk_ps"), m + 1)
                    bias = cols[("aq_b", "ak_b")[m % 2]][:, m // (2 * B):m // (2 * B) + 1]
                    if m >= 2:
                        dve.wait_ge(sem("d_rest"), m - 1)
                    nc.vector.tensor_scalar(d_val[:, m % 2, :], half(0, m % 2), bias, (DH ** -0.5, 1.0)[m % 2],
                                            ALU.add, ALU.mult).then_inc(sem("d_val"), 1)
                if 1 <= m <= C * B * 2:
                    dve.wait_ge(sem("d_part1"), m)
                    if m >= 3:
                        dve.wait_ge(sem("d_part3"), m - 2)
                    nc.vector.tensor_tensor(d_rest[:, (m - 1) % 2, :], d_val[:, (m - 1) % 2, :], d_part[:, (m - 1) % 4, 0, :],
                                            ALU.subtract).then_inc(sem("d_rest"), 1)
                if m >= 2:
                    dve.wait_ge(sem("d_part2"), m - 1)
                    nc.vector.tensor_tensor(d_part[:, (m - 2) % 4, 2, :], d_rest[:, m % 2, :], d_part[:, (m - 2) % 4, 1, :],
                                            ALU.subtract).then_inc(sem("d_part3"), 1)
            v4 = d_v.rearrange("p (b h q e) -> p b h q e", b=B, h=H, q=TB)
            nc.vector.memset(d_v.rearrange("p (n e) -> p n e", e=V1)[:, :, DH:V1], 1.0).then_inc(sem("d_vones"), 1)
            for tt in range(T):
                dve.wait_ge(sem("d_v_ps"), tt + 1)
                nc.vector.tensor_tensor(v4[:, tt // TB, :, tt % TB, 0:DH],
                                        half(1, tt % 2)[:, 0:D].rearrange("p (h e) -> p h e", h=H),
                                        spread["av_b"].rearrange("p (h e) -> p h e", h=H), ALU.add).then_inc(sem("d_v"), 1)
            def d_row_max(i, j):
                for qt in range(TB):
                    n = (qt + 1) * P
                    dve.wait_ge(sem("d_scores"), i * 8 + (TB * j + qt + 1))
                    wait(dve, "d_p", i * 8 + (TB * (j - 2) + qt + 1))
                    gate(qt)
                    nc.vector.tensor_tensor_reduce(out=d_s[:, j % 2, qt, 0:n], in0=half(qt // 2, qt % 2)[:, 0:n],
                                                   in1=causal[:, S - n:S], scale=1.0, scalar=MARK, op0=ALU.add,
                                                   op1=ALU.max, accum_out=d_max[:, j % 2, qt:qt + 1]).then_inc(sem("d_s"), 1)
                dve.wait_ge(sem("d_s"), i * 8 + (TB * j + TB))
                nc.vector.tensor_scalar(d_neg[:, j % 2, :], d_max[:, j % 2, :], -1.0, None, ALU.mult).then_inc(sem("d_neg"), 1)
                wait(dve, "d_oT_ps", i * 2 + (j - 1))
                nc.vector.tensor_copy(d_vh[:, j % 2, :], d_v[:, bass.ds((i * 2 + j) * (TB * V1), TB * V1)]).then_inc(sem("d_vh"), 1)

            def d_output(i, j):
                dve.wait_ge(sem("d_o_ps"), i * 2 + (j + 1))
                ps = bank[1][:, 0:TB * V1].rearrange("p (q v) -> p q v", q=TB)
                nc.vector.reciprocal(d_r[:, j % 2, :], ps[:, :, DH]).then_inc(sem("d_r"), 1)
                dve.wait_ge(sem("d_r"), i * 2 + (j + 1))
                nc.vector.tensor_tensor(d_o[:, bass.ds((i * 2 + j) * (TB * DH), TB * DH)].rearrange("p (q e) -> p q e", q=TB),
                                        ps[:, :, 0:DH], d_r[:, j % 2, :].unsqueeze(2).broadcast_to([P, TB, DH]),
                                        ALU.mult).then_inc(sem("d_o"), 1)

            def d_slots(i, first=False, last=False):
                for j in range(2):
                    if not (last and j == 1):
                        d_row_max(i, j + 1)
                    if not (first and j == 0):
                        if j == 0:
                            d_output(i - 1, 1)
                        else:
                            d_output(i, 0)

            d_row_max(0, 0)
            d_slots(0, first=True)
            with dve.Fori(1, B * H // 2 - 1) as i:
                d_slots(i)
            d_slots(B * H // 2 - 1, last=True)
            d_output(B * H // 2 - 1, 1)
            dve.wait_ge(sem("d_o"), B * H)
            o5 = d_o.rearrange("p (b h q e) -> p b h q e", b=B, h=H, q=TB)
            for tt in range(T):
                nc.vector.tensor_copy(y[:, tt, :].rearrange("p (h e) -> p h e", h=H),
                                      o5[:, tt // TB, :, tt % TB, :]).then_inc(sem("y_ready"), 1)

            def add_to_x(ready, banks, done, so_far=0):
                for tt in range(T):
                    dve.wait_ge(sem(ready), so_far + tt + 1)
                    nc.vector.tensor_tensor(x[:, tt, :], banks(tt % 2)[:, 0:D], x[:, tt, :], ALU.add).then_inc(sem(done), 1)
                dve.wait_ge(sem(done), so_far + T)

            add_to_x("d_out_ps", lambda k: half(2, k), "d_added")

            for tt in range(CT + 1):
                if tt < CT:
                    dve.wait_ge(sem("e_kv_ps"), tt + 1)
                    nc.vector.tensor_tensor(e_kv2[:, tt, :], half(0, tt % 2), spread["lkv_b"], ALU.add).then_inc(sem("e_biased"), 1)
                    dve.wait_ge(sem("e_biased"), tt + 1)
                    if tt >= 2:
                        dve.wait_ge(sem("e_kexp"), tt - 1)
                    nc.vector.tensor_scalar(e_t[:, tt % 2, 0:D], e_kv2[:, tt, 0:D], 0.0, None, ALU.min).then_inc(sem("e_kmin"), 1)
                u = tt - 1
                if u >= 0:
                    dve.wait_ge(sem("e_kexp"), u + 1)
                    nc.vector.scalar_tensor_tensor(out=e_kv2[:, u, 0:D], in0=e_t[:, u % 2, D:2 * D], scalar=-1.0,
                                                   in1=e_kv2[:, u, 0:D], op0=ALU.add, op1=ALU.max).then_inc(sem("e_kv"), 1)
            dve.wait_ge(sem("e_kn"), C)
            link(nc.vector.reciprocal(e_kr, e_kn))
            for bb in range(B):
                dve.wait_ge(sem("e_sum_ps"), bb + 1)
                for cc in range(C):
                    n = cc * B + bb
                    ins = nc.vector.scalar_tensor_tensor(out=e_kv[:, bb, cc, :], in0=(half(1, bb), bank[bb])[cc][:, 0:P],
                                                         scalar=e_kr[:, n:n + 1], in1=blockmask[:],
                                                         op0=ALU.mult, op1=ALU.mult)
                ins.then_inc(sem("e_sum"), 1)
            layer_norm(5, y, "y_ready")
            bias_to_x("lo_b", 7 * T)
            for g in range(C * B):
                cc, bb = g // B, g % B
                q_ps, bias, sl = half(0, g % 2), cols["lq_b"][:, cc:cc + 1], slice(bb * S, (bb + 1) * S)
                dve.wait_ge(sem("e_q_ps"), g + 1)
                nc.vector.tensor_scalar(sq[:, g % 2, :], q_ps, bias, 0.0, ALU.add, ALU.min).then_inc(sem("e_qmin"), 1)
                nc.vector.tensor_scalar(e_qT[:, cc, sl], q_ps, bias, 0.0, ALU.add, ALU.max)
                dve.wait_ge(sem("e_qexp"), g + 1)
                link(nc.vector.tensor_scalar(e_qq[:, cc, sl], e_qq[:, cc, sl], -1.0, None, ALU.add))
                nc.vector.tensor_tensor(e_qT[:, cc, sl], e_qT[:, cc, sl], e_qq[:, cc, sl], ALU.add).then_inc(sem("e_qelu"), 1)
            for tt in range(T):
                dve.wait_ge(sem("e_qn"), tt + 1)
                link(nc.vector.reciprocal(e_qr[:, tt % 2], e_qn[:, tt % 2]))
                for cc in range(C):
                    ins = nc.vector.tensor_tensor(y[:, tt, cc * P:(cc + 1) * P].rearrange("p (h e) -> p h e", h=HC),
                                                  half(1, tt % 2)[:, cc * P:(cc + 1) * P].rearrange("p (h e) -> p h e", h=HC),
                                                  e_qr[:, tt % 2, cc, :].unsqueeze(2).broadcast_to([P, HC, DH]), ALU.mult)
                ins.then_inc(sem("y_ready"), 1)
            add_to_x("e_out_ps", lambda k: half(2, k), "e_added")

            layer_norm(6, y, "y_ready")
            dve.wait_ge(sem("f_table_loaded"), 32)
            link(nc.vector.tensor_tensor(f_s2, f_sig, f_sig, ALU.mult))
            link(nc.vector.reciprocal(f_iv, f_s2))
            link(nc.vector.tensor_tensor(f_mi, f_mu, f_iv, ALU.mult))
            link(nc.vector.tensor_tensor(f_m2i, f_mu, f_mi, ALU.mult))
            bias_to_x("base_b", 9 * T)
            dve.wait_ge(sem("yT_ready"), 9 * T)
            for cc in range(C):
                for bb in range(B):
                    ins = nc.vector.bn_stats(f_bn[:, cc, bb, :], yT[:, cc, bb * S:(bb + 1) * S])
            link(ins)
            for cc in range(C):
                for bb in range(B):
                    ins = nc.vector.bn_aggr(f_mv[:, cc, bb, :], f_bn[:, cc, bb, :])
            link(ins)
            nc.vector.tensor_scalar(f_m1s, f_mv[:, :, :, 0], -2.0, None, ALU.mult)
            link(nc.vector.tensor_tensor(f_sq, f_mv[:, :, :, 0], f_mv[:, :, :, 0], ALU.mult))
            nc.vector.tensor_tensor(f_m2, f_sq, f_mv[:, :, :, 1], ALU.add).then_inc(sem("f_moments"), 1)
            dve.wait_ge(sem("f_loss_ps"), 1)
            link(nc.vector.tensor_scalar(f_nl[0:B], half(0, 0)[0:B, 0:E], -1.0 / D, None, ALU.mult))
            link(nc.vector.max(f_best[0:B], f_nl[0:B]))
            nc.vector.max_index(f_idx[0:B], f_best[0:B], f_nl[0:B]).then_inc(sem("f_chosen"), 1)
            add_to_x("f_out_ps", lambda k: bank[k], "f_added")
            dve.wait_ge(sem("f_expert_loaded"), 16 * 6 * B)
            for tt in range(T):
                ins = nc.vector.tensor_tensor(x[:, tt, :], x[:, tt, :], f_cb[:, tt // TB, :], ALU.add)
            link(ins)
            add_to_x("f_out_ps", lambda k: bank[k], "f_added", T)


def kernel(**inputs):
    import concourse.bacc as bacc
    from concourse.bass_utils import run_bass_kernel_spmd

    def arr(name):
        return np.asarray(inputs[name])

    def keep(a):
        return np.ascontiguousarray(a)

    def tiles(a):
        return keep(a.reshape(-1, P, a.shape[-1]).transpose(1, 0, 2))

    def wT(*names):
        return tiles(np.concatenate([arr(n) for n in names], 0).T)

    def col(name):
        return keep(arr(name).reshape(-1, P).T)

    def row(*names):
        return keep(np.concatenate([arr(n) for n in names]).reshape(1, -1))

    ctx = arr("ctx_1024").reshape(B * SC, D)
    pos = np.arange(S, dtype=np.float32)
    slopes = np.array([(2.0 ** (-8.0 / H)) * (2.0 ** (-8.0 / H)) ** k for k in range(H)], dtype=np.float32)
    block = np.kron(np.eye(HC, dtype=np.float32), np.ones((DH, DH), np.float32))
    mask = np.zeros((P, S), np.float32)
    mask[:, S - P:] = np.where(np.arange(P)[None, :] > np.arange(P)[:, None], np.float32(MASKED), np.float32(0))

    def parts(v, n):
        out = []
        for _ in range(n):
            top = (np.ascontiguousarray(v, np.float32).view(np.uint32) & np.uint32(0xFFFF0000)).view(np.float32)
            out.append((top.view(np.uint32) >> 16).astype(np.uint16))
            v = (v - top).astype(np.float32)
        return out

    one, (high, low) = parts(np.ones(S, np.float32), 1), parts(pos, 2)
    alibi_q = np.stack(one * 3 + [high] * 3 + [low] * 3)
    alibi_k = np.stack([np.stack(parts(sl * pos, 3) + parts(-sl * np.ones(S, np.float32), 3) * 2) for sl in slopes])
    a = {
        "x": tiles(arr("x").reshape(B * S, D)),
        "ident": np.eye(P, dtype=np.float32),
        "blockmask": block,
        "headmask": keep(block[:, ::DH]),
        "causal": mask,
        "alibi_q": alibi_q,
        "alibi_k": keep(np.tile(alibi_k, (B, 1, 1))),
        "ctxT": tiles(ctx.T),
        "ctxV": keep(np.concatenate([ctx.reshape(B, CTB, P, H, DH), np.ones((B, CTB, P, H, 1), np.float32)], -1)
                     .transpose(2, 0, 3, 1, 4).reshape(P, B * H * CTB * V1)),
        "below": np.broadcast_to(np.arange(SC - K_TOP, SC - K_TOP + 8, dtype=np.float32), (P, 8)).copy(),
        "scale1": col("L0_attn_scale1"), "scale2": col("L0_attn_scale2"), "conv1_b": col("L0_attn_conv1_b"),
        "aq_b": col("L1_attn_q_b"), "ak_b": col("L1_attn_k_b"), "lq_b": col("L1_xattn_bq"),
        "proj_b": row("L0_attn_proj_b"), "conv2_b": row("L0_attn_conv2_b"), "av_b": row("L1_attn_v_b"),
        "ao_b": row("L1_attn_o_b"), "lkv_b": row("L1_xattn_bk", "L1_xattn_bv"), "lo_b": row("L1_xattn_bo"),
        "base_b": row("L1_ffn_base_b"), "gamma": row("L0_attn_gamma"),
        "qkvT": wT("L0_attn_qkv_w"), "projT": wT("L0_attn_proj_w"), "conv1T": wT("L0_attn_conv1_w"),
        "conv2T": wT("L0_attn_conv2_w"), "xqT": wT("L0_xattn_Wq"), "xkT": wT("L0_xattn_Wk"),
        "gateT": wT("L0_ffn_w_gate").reshape(P, -1), "upT": wT("L0_ffn_w_up").reshape(P, -1),
        "downT": wT("L0_ffn_w_down").reshape(P, -1),
        "aqT": wT("L1_attn_q_w"), "akT": wT("L1_attn_k_w"), "avT": wT("L1_attn_v_w"), "aoT": wT("L1_attn_o_w"),
        "lqT": wT("L1_xattn_Wq"), "lkvT": wT("L1_xattn_Wk", "L1_xattn_Wv"), "loT": wT("L1_xattn_Wo"),
        "baseT": wT("L1_ffn_base_W"),
        "muT": tiles(arr("L1_ffn_disc_mu").T), "sigmaT": tiles(arr("L1_ffn_disc_sigma").T),
        "down": keep(arr("L1_ffn_down_W").reshape(E, C, P, R).transpose(0, 2, 1, 3)),
        "up": keep(arr("L1_ffn_up_W")),
        "convT": keep(arr("L1_ffn_conv_W").transpose(0, 2, 1).reshape(E, C, P, D).transpose(0, 2, 1, 3)),
        "down_b": keep(arr("L1_ffn_down_b").reshape(E, R, 1)),
        "up_b": keep(arr("L1_ffn_up_b").reshape(E, C, P).transpose(0, 2, 1)),
        "conv_b": keep(arr("L1_ffn_conv_b")),
    }
    nc = bacc.Bacc("TRN2", target_bir_lowering=False, num_devices=1)
    t = {n: nc.dram_tensor("in_" + n, v.shape, mybir.dt.from_np(v.dtype), kind="ExternalInput").ap()
         for n, v in a.items()}
    t["out"] = nc.dram_tensor("out", (P, T, D), F32, kind="ExternalOutput").ap()
    decoder(nc, t)
    r = run_bass_kernel_spmd(nc, [{"in_" + n: v for n, v in a.items()}], core_ids=[0])
    return r.results[0]["out"].transpose(1, 0, 2).reshape(B, S, D)
```
